# Optimizing a Trainium2 kernel written in Bass

```python
import numpy as np
import jax
import jax.numpy as jnp

def _softmax(x, axis=-1):
    return jax.nn.softmax(x, axis=axis)

def _gelu(x):
    return jax.nn.gelu(x, approximate=True)

def _silu(x):
    return jax.nn.silu(x)

def _sigmoid(x):
    return jax.nn.sigmoid(x)

def _layernorm(x, axis=-1, eps=1e-05):
    m = jnp.mean(x, axis=axis, keepdims=True)
    v = jnp.var(x, axis=axis, keepdims=True)
    return (x - m) / jnp.sqrt(v + eps)

def _scatter_add(tgt, idx, src, axis=0):
    return tgt.at[idx].add(src)

def _segment_sum(src, seg, n):
    return jax.ops.segment_sum(src, seg, n)
kernel_name = 'mk_hybrid_d2_jaxref_r8_adffda'

def setup_inputs(seed: int=0):
    np.random.seed(seed)
    _w = jnp.asarray

    def _L0_attn_a_setup():
        import jax, jax.numpy as jnp
        import numpy as np
        D_MODEL = 128
        N_HEADS = 16
        KEY_DIM = D_MODEL // 2
        VAL_DIM = D_MODEL
        HEAD_QK = KEY_DIM // N_HEADS
        HEAD_V = VAL_DIM // N_HEADS
        PROJ_LR = 32
        GATE_LR = 64
        EPS = 1e-05
        key = jax.random.key(seed)
        ks = jax.random.split(key, 16)
        s = 0.02
        B, T = (4, 128)
        return {'x': jax.random.normal(ks[0], (B, T, D_MODEL), jnp.float32), 'mu_x': jax.random.normal(ks[1], (D_MODEL,), jnp.float32) * s, 'W_x1': jax.random.normal(ks[2], (D_MODEL, 5 * PROJ_LR), jnp.float32) * s, 'W_x2': jax.random.normal(ks[3], (D_MODEL, 5, PROJ_LR), jnp.float32) * s, 'x_bias': jax.random.normal(ks[4], (5, D_MODEL), jnp.float32) * s, 'W_r': jax.random.normal(ks[5], (D_MODEL, KEY_DIM), jnp.float32) * s, 'W_w1': jax.random.normal(ks[6], (D_MODEL, GATE_LR), jnp.float32) * s, 'W_w2': jax.random.normal(ks[7], (GATE_LR, KEY_DIM), jnp.float32) * s, 'b_w2': jax.random.normal(ks[8], (KEY_DIM,), jnp.float32) * s, 'W_k': jax.random.normal(ks[9], (D_MODEL, KEY_DIM), jnp.float32) * s, 'W_v': jax.random.normal(ks[10], (D_MODEL, VAL_DIM), jnp.float32) * s, 'W_g': jax.random.normal(ks[11], (D_MODEL, VAL_DIM), jnp.float32) * s, 'u': jax.random.normal(ks[12], (N_HEADS, HEAD_QK), jnp.float32) * s, 'gn_w': jnp.ones((VAL_DIM,), jnp.float32), 'gn_b': jnp.zeros((VAL_DIM,), jnp.float32), 'W_o': jax.random.normal(ks[13], (VAL_DIM, D_MODEL), jnp.float32) * s}
    _L0_attn_a_in = _L0_attn_a_setup()

    def _L0_attn_b_setup():
        import jax, jax.numpy as jnp
        import numpy as np
        B, T, E, H = (1, 256, 128, 16)
        HD = E // H
        key = jax.random.key(seed)
        ks = jax.random.split(key, 8)
        s = 0.02
        mk = lambda k, sh: jax.random.normal(k, sh, jnp.float32) * s
        return {'x': jax.random.normal(ks[0], (B, T, E), jnp.float32), 'wq': mk(ks[1], (E, E)), 'bq': jnp.zeros((E,), jnp.float32), 'wk': mk(ks[2], (E, E)), 'bk': jnp.zeros((E,), jnp.float32), 'wv': mk(ks[3], (E, E)), 'bv': jnp.zeros((E,), jnp.float32), 'wg': mk(ks[4], (E, E)), 'bg': jnp.zeros((E,), jnp.float32), 'wo': mk(ks[5], (E, E)), 'bo': jnp.zeros((E,), jnp.float32), 'wd': mk(ks[6], (H, E)), 'bd': jnp.zeros((H,), jnp.float32), 'gamma': jnp.ones((E,), jnp.float32), 'beta': jnp.zeros((E,), jnp.float32)}
    _L0_attn_b_in = _L0_attn_b_setup()

    def _L0_ffn_setup():
        import jax, jax.numpy as jnp
        import numpy as np
        DIM = 128
        NUM_EXPERTS = 8
        HIDDEN = 512
        CAP_FACTOR = 2.0
        B, S = (4, 256)
        key = jax.random.key(seed)
        ks = jax.random.split(key, 6)
        scale_r = 1.0 / np.sqrt(DIM)
        scale_1 = 1.0 / np.sqrt(DIM)
        scale_2 = 1.0 / np.sqrt(HIDDEN)
        return {'x': jax.random.normal(ks[0], (B, S, DIM), dtype=jnp.float32), 'router_w': jax.random.uniform(ks[1], (NUM_EXPERTS, DIM), jnp.float32, -scale_r, scale_r), 'w1': jax.random.uniform(ks[2], (NUM_EXPERTS, DIM, HIDDEN), jnp.float32, -scale_1, scale_1), 'b1': jax.random.uniform(ks[3], (NUM_EXPERTS, HIDDEN), jnp.float32, -scale_1, scale_1), 'w2': jax.random.uniform(ks[4], (NUM_EXPERTS, HIDDEN, DIM), jnp.float32, -scale_2, scale_2), 'b2': jax.random.uniform(ks[5], (NUM_EXPERTS, DIM), jnp.float32, -scale_2, scale_2)}
    _L0_ffn_in = _L0_ffn_setup()

    def _L1_attn_a_setup():
        import jax, jax.numpy as jnp
        import numpy as np
        DIM = 128
        key = jax.random.key(seed)
        k1, k2, k3, k4 = jax.random.split(key, 4)
        x = jax.random.normal(k1, (4, 512, DIM), dtype=jnp.float32)
        A = jax.random.normal(k2, (DIM, DIM), dtype=jnp.float32) * 0.01
        B_w = jax.random.normal(k3, (DIM, DIM), dtype=jnp.float32) * (1.0 / np.sqrt(DIM))
        C_w = jax.random.normal(k4, (DIM, DIM), dtype=jnp.float32) * (1.0 / np.sqrt(DIM))
        D = jnp.ones((DIM,), dtype=jnp.float32)
        return {'x': x, 'A': A, 'B_w': B_w, 'C_w': C_w, 'D': D}
    _L1_attn_a_in = _L1_attn_a_setup()

    def _L1_attn_b_setup():
        import math
        import jax, jax.numpy as jnp
        import numpy as np
        N, T, C = (4, 256, 128)
        H, HS = (16, 64)
        LAYER_ID, N_LAYERS = (1, 12)
        _EPS = math.exp(-LAYER_ID / N_LAYERS)
        EPS_R = _EPS / 2.0
        EPS_K = _EPS + 0.3 * LAYER_ID / (N_LAYERS - 1)
        EPS_V = _EPS

        def _time_interp(x, eps):
            Tn = x.shape[1]
            curr = jnp.pad(x, ((0, 0), (1, 0), (0, 0)))[:, :Tn]
            prev = jnp.pad(x, ((0, 0), (0, 1), (0, 0)))[:, 1:]
            return eps * curr + (1.0 - eps) * prev
        key = jax.random.key(seed)
        ks = jax.random.split(key, 9)
        s = 1.0 / math.sqrt(C)
        return {'x': jax.random.normal(ks[0], (N, T, C), dtype=jnp.float32), 'Wr': jax.random.normal(ks[1], (H * HS, C), dtype=jnp.float32) * s, 'br': jax.random.normal(ks[2], (H * HS,), dtype=jnp.float32) * 0.01, 'Wk': jax.random.normal(ks[3], (H * HS, C), dtype=jnp.float32) * s, 'bk': jax.random.normal(ks[4], (H * HS,), dtype=jnp.float32) * 0.01, 'Wv': jax.random.normal(ks[5], (H * HS, C), dtype=jnp.float32) * s, 'bv': jax.random.normal(ks[6], (H * HS,), dtype=jnp.float32) * 0.01, 'Wo': jax.random.normal(ks[7], (C, H * HS), dtype=jnp.float32) * s, 'bo': jax.random.normal(ks[8], (C,), dtype=jnp.float32) * 0.01, 'time_decay': jnp.full((H * HS,), 0.1, dtype=jnp.float32), 'U': jnp.full((H * HS,), 0.1, dtype=jnp.float32)}
    _L1_attn_b_in = _L1_attn_b_setup()

    def _L1_ffn_setup():
        import jax, jax.numpy as jnp
        import numpy as np
        N_EMBD = 128
        N_STATE = 512
        key = jax.random.key(seed)
        k_x, k_w1, k_b1, k_w2, k_b2 = jax.random.split(key, 5)
        x = jax.random.normal(k_x, (4, 256, N_EMBD), dtype=jnp.float32)
        w1 = jax.random.normal(k_w1, (N_EMBD, N_STATE), dtype=jnp.float32) * (1.0 / np.sqrt(N_EMBD))
        b1 = jax.random.normal(k_b1, (N_STATE,), dtype=jnp.float32) * 0.02
        w2 = jax.random.normal(k_w2, (N_STATE, N_EMBD), dtype=jnp.float32) * (1.0 / np.sqrt(N_STATE))
        b2 = jax.random.normal(k_b2, (N_EMBD,), dtype=jnp.float32) * 0.02
        return {'x': x, 'w1': w1, 'b1': b1, 'w2': w2, 'b2': b2}
    _L1_ffn_in = _L1_ffn_setup()
    _d = {'L0_attn_a_x': _L0_attn_a_in['x'], 'L0_attn_a_mu_x': _L0_attn_a_in['mu_x'], 'L0_attn_a_W_x1': _L0_attn_a_in['W_x1'], 'L0_attn_a_W_x2': _L0_attn_a_in['W_x2'], 'L0_attn_a_x_bias': _L0_attn_a_in['x_bias'], 'L0_attn_a_W_r': _L0_attn_a_in['W_r'], 'L0_attn_a_W_w1': _L0_attn_a_in['W_w1'], 'L0_attn_a_W_w2': _L0_attn_a_in['W_w2'], 'L0_attn_a_b_w2': _L0_attn_a_in['b_w2'], 'L0_attn_a_W_k': _L0_attn_a_in['W_k'], 'L0_attn_a_W_v': _L0_attn_a_in['W_v'], 'L0_attn_a_W_g': _L0_attn_a_in['W_g'], 'L0_attn_a_u': _L0_attn_a_in['u'], 'L0_attn_a_gn_w': _L0_attn_a_in['gn_w'], 'L0_attn_a_gn_b': _L0_attn_a_in['gn_b'], 'L0_attn_a_W_o': _L0_attn_a_in['W_o'], 'L0_attn_b_wq': _L0_attn_b_in['wq'], 'L0_attn_b_bq': _L0_attn_b_in['bq'], 'L0_attn_b_wk': _L0_attn_b_in['wk'], 'L0_attn_b_bk': _L0_attn_b_in['bk'], 'L0_attn_b_wv': _L0_attn_b_in['wv'], 'L0_attn_b_bv': _L0_attn_b_in['bv'], 'L0_attn_b_wg': _L0_attn_b_in['wg'], 'L0_attn_b_bg': _L0_attn_b_in['bg'], 'L0_attn_b_wo': _L0_attn_b_in['wo'], 'L0_attn_b_bo': _L0_attn_b_in['bo'], 'L0_attn_b_wd': _L0_attn_b_in['wd'], 'L0_attn_b_bd': _L0_attn_b_in['bd'], 'L0_attn_b_gamma': _L0_attn_b_in['gamma'], 'L0_attn_b_beta': _L0_attn_b_in['beta'], 'L0_ffn_router_w': _L0_ffn_in['router_w'], 'L0_ffn_w1': _L0_ffn_in['w1'], 'L0_ffn_b1': _L0_ffn_in['b1'], 'L0_ffn_w2': _L0_ffn_in['w2'], 'L0_ffn_b2': _L0_ffn_in['b2'], 'L1_attn_a_A': _L1_attn_a_in['A'], 'L1_attn_a_B_w': _L1_attn_a_in['B_w'], 'L1_attn_a_C_w': _L1_attn_a_in['C_w'], 'L1_attn_a_D': _L1_attn_a_in['D'], 'L1_attn_b_Wr': _L1_attn_b_in['Wr'], 'L1_attn_b_br': _L1_attn_b_in['br'], 'L1_attn_b_Wk': _L1_attn_b_in['Wk'], 'L1_attn_b_bk': _L1_attn_b_in['bk'], 'L1_attn_b_Wv': _L1_attn_b_in['Wv'], 'L1_attn_b_bv': _L1_attn_b_in['bv'], 'L1_attn_b_Wo': _L1_attn_b_in['Wo'], 'L1_attn_b_bo': _L1_attn_b_in['bo'], 'L1_attn_b_time_decay': _L1_attn_b_in['time_decay'], 'L1_attn_b_U': _L1_attn_b_in['U'], 'L1_ffn_w1': _L1_ffn_in['w1'], 'L1_ffn_b1': _L1_ffn_in['b1'], 'L1_ffn_w2': _L1_ffn_in['w2'], 'L1_ffn_b2': _L1_ffn_in['b2']}
    _x0 = _d['L0_attn_a_x']
    _d['L0_attn_a_x'] = jax.random.normal(jax.random.fold_in(jax.random.key(seed), 1), (32, 256, 128), dtype=_x0.dtype)
    del _x0
    return _d

def reference(L0_attn_a_x, L0_attn_a_mu_x, L0_attn_a_W_x1, L0_attn_a_W_x2, L0_attn_a_x_bias, L0_attn_a_W_r, L0_attn_a_W_w1, L0_attn_a_W_w2, L0_attn_a_b_w2, L0_attn_a_W_k, L0_attn_a_W_v, L0_attn_a_W_g, L0_attn_a_u, L0_attn_a_gn_w, L0_attn_a_gn_b, L0_attn_a_W_o, L0_attn_b_wq, L0_attn_b_bq, L0_attn_b_wk, L0_attn_b_bk, L0_attn_b_wv, L0_attn_b_bv, L0_attn_b_wg, L0_attn_b_bg, L0_attn_b_wo, L0_attn_b_bo, L0_attn_b_wd, L0_attn_b_bd, L0_attn_b_gamma, L0_attn_b_beta, L0_ffn_router_w, L0_ffn_w1, L0_ffn_b1, L0_ffn_w2, L0_ffn_b2, L1_attn_a_A, L1_attn_a_B_w, L1_attn_a_C_w, L1_attn_a_D, L1_attn_b_Wr, L1_attn_b_br, L1_attn_b_Wk, L1_attn_b_bk, L1_attn_b_Wv, L1_attn_b_bv, L1_attn_b_Wo, L1_attn_b_bo, L1_attn_b_time_decay, L1_attn_b_U, L1_ffn_w1, L1_ffn_b1, L1_ffn_w2, L1_ffn_b2):

    def _L0_attn_a_ref(x, mu_x, W_x1, W_x2, x_bias, W_r, W_w1, W_w2, b_w2, W_k, W_v, W_g, u, gn_w, gn_b, W_o):
        import jax, jax.numpy as jnp
        import numpy as np
        D_MODEL = 128
        N_HEADS = 16
        KEY_DIM = D_MODEL // 2
        VAL_DIM = D_MODEL
        HEAD_QK = KEY_DIM // N_HEADS
        HEAD_V = VAL_DIM // N_HEADS
        PROJ_LR = 32
        GATE_LR = 64
        EPS = 1e-05
        B, T, D = x.shape
        shifted = jnp.pad(x, ((0, 0), (1, 0), (0, 0)))[:, :T]
        delta = shifted - x
        low = jnp.tanh((x + delta * mu_x) @ W_x1).reshape(B, T, 5, PROJ_LR)
        mus = jnp.einsum('blnr,dnr->blnd', low, W_x2) + x_bias
        xr, xw, xk, xv, xg = [x + delta * mus[:, :, i] for i in range(5)]
        r = (xr @ W_r).reshape(B, T, N_HEADS, HEAD_QK)
        w = (jnp.tanh(xw @ W_w1) @ W_w2 + b_w2).reshape(B, T, N_HEADS, HEAD_QK)
        k = (xk @ W_k).reshape(B, T, N_HEADS, HEAD_QK)
        v = (xv @ W_v).reshape(B, T, N_HEADS, HEAD_V)
        g = xg @ W_g
        w = -jnp.exp(w)

        def step(S, inp):
            r_t, k_t, v_t, w_t = inp
            o_t = jnp.einsum('bhk,bhkv->bhv', r_t, S) + jnp.einsum('bhk,hk,bhk,bhv->bhv', r_t, u, k_t, v_t)
            S = jnp.exp(w_t)[..., None] * S + k_t[..., :, None] * v_t[..., None, :]
            return (S, o_t)
        S0 = jnp.zeros((B, N_HEADS, HEAD_QK, HEAD_V), x.dtype)
        xs = tuple((jnp.moveaxis(t, 1, 0) for t in (r, k, v, w)))
        _, o = jax.lax.scan(step, S0, xs)
        o = jnp.moveaxis(o, 0, 1)
        mean = o.mean(-1, keepdims=True)
        var = o.var(-1, keepdims=True)
        o = ((o - mean) * jax.lax.rsqrt(var + EPS)).reshape(B, T, VAL_DIM)
        o = (o * gn_w + gn_b) * (g * jax.nn.sigmoid(g))
        return o @ W_o

    def _L0_attn_b_ref(x, wq, bq, wk, bk, wv, bv, wg, bg, wo, bo, wd, bd, gamma, beta):
        import jax, jax.numpy as jnp
        import numpy as np
        B, T, E, H = (1, 256, 128, 16)
        HD = E // H
        Bx, Tx, Ex = x.shape
        scale = jnp.sqrt(jnp.asarray(HD, jnp.float32))

        def proj(w, b):
            return (x @ w.T + b).reshape(Bx, Tx, H, HD).transpose(0, 2, 1, 3)
        Q, K, V = (proj(wq, bq), proj(wk, bk), proj(wv, bv))
        inv_freq = 1.0 / 10000.0 ** (jnp.arange(0, HD, 2, dtype=jnp.float32) / HD)
        freqs = jnp.arange(Tx, dtype=jnp.float32)[:, None] * inv_freq[None, :]
        emb = jnp.concatenate([freqs, freqs], axis=-1)
        cos, sin = (jnp.cos(emb), jnp.sin(emb))

        def rope(t):
            x1, x2 = (t[..., ::2], t[..., 1::2])
            t_rot = jnp.stack([-x2, x1], axis=-1).reshape(t.shape)
            return t * cos + t_rot * sin
        Q, K = (rope(Q), rope(K))
        scores = jnp.einsum('bhqd,bhkd->bhqk', Q, K) / scale
        pd = jax.nn.sigmoid(x.mean(axis=1) @ wd.T + bd)
        log_decay = jnp.log(1.0 - jnp.exp2(-5.0 - 8.0 * pd))
        idx = jnp.arange(Tx)
        pos_diff = jnp.clip(idx[None, :] - idx[:, None], 0, None).astype(jnp.float32)
        scores = scores + pos_diff[None, None] * log_decay[:, :, None, None]
        attn = jax.nn.softmax(scores, axis=-1)
        out = jnp.einsum('bhqk,bhkd->bhqd', attn, V).transpose(0, 2, 1, 3).reshape(Bx, Tx, Ex)
        og = out.reshape(Bx, Tx, H, HD)
        mu = og.mean(axis=(1, 3), keepdims=True)
        var = ((og - mu) ** 2).mean(axis=(1, 3), keepdims=True)
        on = ((og - mu) / jnp.sqrt(var + 1e-05)).reshape(Bx, Tx, Ex) * gamma + beta
        gate = jax.nn.silu(x @ wg.T + bg)
        return gate * on @ wo.T + bo

    def _L0_ffn_ref(x, router_w, w1, b1, w2, b2):
        import jax, jax.numpy as jnp
        import numpy as np
        DIM = 128
        NUM_EXPERTS = 8
        HIDDEN = 512
        CAP_FACTOR = 2.0
        B, S = (4, 256)
        Bz, Sz, Dz = x.shape
        E = router_w.shape[0]
        capacity = max(1, int(Sz * CAP_FACTOR / E) + 1)
        scores = jax.nn.softmax(jnp.einsum('bsd,ed->bse', x, router_w), axis=-1)
        scores_t = jnp.swapaxes(scores, 1, 2)
        gate_vals, sel_idx = jax.lax.top_k(scores_t, capacity)
        b_idx = jnp.arange(Bz)[:, None, None]
        tokens = x[b_idx, sel_idx]
        h = jnp.einsum('becd,edh->bech', tokens, w1) + b1[None, :, None, :]
        h = jax.nn.gelu(h, approximate=False)
        y = jnp.einsum('bech,ehd->becd', h, w2) + b2[None, :, None, :]
        gated = y * gate_vals[..., None]
        out = jnp.zeros_like(x).at[b_idx, sel_idx].add(gated)
        return out

    def _L1_attn_a_ref(x, A, B_w, C_w, D):
        import jax, jax.numpy as jnp
        import numpy as np
        DIM = 128
        Bsz, L, Dm = x.shape
        bx = jnp.einsum('bld,ed->ble', x, B_w)

        def step(h, inputs):
            bx_t, x_t = inputs
            h = jnp.tanh(h @ A.T + bx_t)
            y = h @ C_w.T + D * x_t
            return (h, y)
        h0 = jnp.zeros((Bsz, Dm), dtype=x.dtype)
        _, ys = jax.lax.scan(step, h0, (jnp.swapaxes(bx, 0, 1), jnp.swapaxes(x, 0, 1)))
        return jnp.swapaxes(ys, 0, 1)

    def _L1_attn_b_ref(x, Wr, br, Wk, bk, Wv, bv, Wo, bo, time_decay, U):
        import math
        import jax, jax.numpy as jnp
        import numpy as np
        N, T, C = (4, 256, 128)
        H, HS = (16, 64)
        LAYER_ID, N_LAYERS = (1, 12)
        _EPS = math.exp(-LAYER_ID / N_LAYERS)
        EPS_R = _EPS / 2.0
        EPS_K = _EPS + 0.3 * LAYER_ID / (N_LAYERS - 1)
        EPS_V = _EPS

        def _time_interp(x, eps):
            Tn = x.shape[1]
            curr = jnp.pad(x, ((0, 0), (1, 0), (0, 0)))[:, :Tn]
            prev = jnp.pad(x, ((0, 0), (0, 1), (0, 0)))[:, 1:]
            return eps * curr + (1.0 - eps) * prev
        n, t, c = x.shape
        R = (_time_interp(x, EPS_R) @ Wr.T + br).reshape(n, t, H, HS)
        K = (_time_interp(x, EPS_K) @ Wk.T + bk).reshape(n, t, H, HS)
        V = (_time_interp(x, EPS_V) @ Wv.T + bv).reshape(n, t, H, HS)
        w = jax.nn.relu(time_decay).reshape(1, 1, H, HS)
        t_rem = (t - jnp.arange(1, t + 1, dtype=x.dtype)).reshape(1, t, 1, 1)
        W = -w * t_rem
        e = jnp.exp(jnp.clip(W + K, -20.0, 10.0))
        past_attention = jnp.cumsum(e * V, axis=1)
        past_energy = jnp.cumsum(e, axis=1)
        shift = lambda a: jnp.pad(a, ((0, 0), (1, 0), (0, 0), (0, 0)))[:, :t]
        eu = jnp.exp(jnp.clip(U.reshape(1, 1, H, HS) + K, -20.0, 10.0))
        A = shift(past_attention) + eu * V
        B = shift(past_energy) + eu
        WKV = A / B
        out = (jax.nn.sigmoid(R) * WKV).reshape(n, t, -1) @ Wo.T + bo
        return out

    def _L1_ffn_ref(x, w1, b1, w2, b2):
        import jax, jax.numpy as jnp
        import numpy as np
        N_EMBD = 128
        N_STATE = 512
        h = jax.nn.gelu(jnp.einsum('bse,eh->bsh', x, w1) + b1, approximate=False)
        return jnp.einsum('bsh,he->bse', h, w2) + b2
    x = L0_attn_a_x
    x = x + _L0_attn_a_ref(_layernorm(x, axis=-1), L0_attn_a_mu_x, L0_attn_a_W_x1, L0_attn_a_W_x2, L0_attn_a_x_bias, L0_attn_a_W_r, L0_attn_a_W_w1, L0_attn_a_W_w2, L0_attn_a_b_w2, L0_attn_a_W_k, L0_attn_a_W_v, L0_attn_a_W_g, L0_attn_a_u, L0_attn_a_gn_w, L0_attn_a_gn_b, L0_attn_a_W_o)
    x = x + _L0_ffn_ref(_layernorm(x, axis=-1), L0_ffn_router_w, L0_ffn_w1, L0_ffn_b1, L0_ffn_w2, L0_ffn_b2)
    x = x + _L0_attn_b_ref(_layernorm(x, axis=-1), L0_attn_b_wq, L0_attn_b_bq, L0_attn_b_wk, L0_attn_b_bk, L0_attn_b_wv, L0_attn_b_bv, L0_attn_b_wg, L0_attn_b_bg, L0_attn_b_wo, L0_attn_b_bo, L0_attn_b_wd, L0_attn_b_bd, L0_attn_b_gamma, L0_attn_b_beta)
    x = x + _L0_ffn_ref(_layernorm(x, axis=-1), L0_ffn_router_w, L0_ffn_w1, L0_ffn_b1, L0_ffn_w2, L0_ffn_b2)
    x = x + _L1_attn_a_ref(_layernorm(x, axis=-1), L1_attn_a_A, L1_attn_a_B_w, L1_attn_a_C_w, L1_attn_a_D)
    x = x + _L1_ffn_ref(_layernorm(x, axis=-1), L1_ffn_w1, L1_ffn_b1, L1_ffn_w2, L1_ffn_b2)
    x = x + _L1_attn_b_ref(_layernorm(x, axis=-1), L1_attn_b_Wr, L1_attn_b_br, L1_attn_b_Wk, L1_attn_b_bk, L1_attn_b_Wv, L1_attn_b_bv, L1_attn_b_Wo, L1_attn_b_bo, L1_attn_b_time_decay, L1_attn_b_U)
    x = x + _L1_ffn_ref(_layernorm(x, axis=-1), L1_ffn_w1, L1_ffn_b1, L1_ffn_w2, L1_ffn_b2)
    return x

_drawn_inputs = setup_inputs


def setup_inputs(seed=0):
    import zlib

    import numpy as np

    out = dict(_drawn_inputs(seed))
    spreads = {'L0_attn_a_gn_w': (1.0, 0.6),
     'L0_attn_a_gn_b': (0.0, 0.8),
     'L0_attn_b_bq': (0.0, 0.8),
     'L0_attn_b_bk': (0.0, 0.8),
     'L0_attn_b_bv': (0.0, 0.709),
     'L0_attn_b_bg': (0.0, 0.668),
     'L0_attn_b_bo': (0.0, 0.1),
     'L0_attn_b_bd': (0.0, 2.0),
     'L0_attn_b_gamma': (1.0, 0.6),
     'L0_attn_b_beta': (0.0, 0.8),
     'L1_attn_a_D': (1.0, 0.2),
     'L1_attn_b_time_decay': (0.10000000149011612, 0.2),
     'L1_attn_b_U': (0.10000000149011612, 0.6)}
    factors = {'L0_attn_a_mu_x': 8.0,
     'L0_attn_a_W_x1': 8.0,
     'L0_attn_a_W_x2': 8.0,
     'L0_attn_a_x_bias': 8.0,
     'L0_attn_a_W_w1': 22.395,
     'L0_attn_a_W_w2': 22.149,
     'L0_attn_a_b_w2': 64.0,
     'L0_attn_a_u': 27.287,
     'L0_attn_b_wq': 8.0,
     'L0_attn_b_wk': 8.0,
     'L0_attn_b_wv': 8.0,
     'L0_attn_b_wd': 200.0,
     'L0_ffn_b1': 4.531,
     'L0_ffn_b2': 3.181,
     'L1_attn_b_br': 27.15,
     'L1_attn_b_bk': 200.0,
     'L1_attn_b_bv': 8.0,
     'L1_attn_b_bo': 8.0,
     'L1_ffn_b1': 5.588,
     'L1_ffn_b2': 3.737}
    for name, (base, spread) in spreads.items():
        noise = np.random.default_rng([zlib.crc32(name.encode()), seed]).standard_normal(out[name].shape)
        drawn = base * np.exp(spread * noise) if base else spread * noise
        out[name] = jnp.asarray(drawn.astype(out[name].dtype))
    for name, factor in factors.items():
        out[name] = (out[name] * factor).astype(out[name].dtype)
    return out
```

```python
import concourse.bass as bass
from concourse import mybir
from contextlib import ExitStack
import numpy as np

F32 = mybir.dt.float32
F16 = mybir.dt.float16
BF16 = mybir.dt.bfloat16
U32 = mybir.dt.uint32
ALU = mybir.AluOpType
ACT = mybir.ActivationFunctionType
AX = mybir.AxisListType

P = 128
D = 128
T = 256
B = 32
TOK = B * T
TILES = TOK // P
GT = 4
NG = TILES // GT
GW = GT * P
LN_EPS = 1e-5


class Core:
    pass


def open_core(nc, ctx):
    k = Core()
    k.nc = nc
    k.sb = lambda name, shape, dt=F32: ctx.enter_context(nc.sbuf_tensor(name, shape, dt))
    k.X = k.sb("X", [P, TILES + 2 * GT, D])
    k.ident = k.sb("ident", [P, P])
    k.neg_half = k.sb("neg_half", [P, GT])
    k.stats = k.sb("stats", [P, GT, 6])
    k.mean = k.sb("mean", [P, GT])
    k.diff = k.sb("diff", [P, GT])
    k.dev = k.sb("dev", [P, GT])
    k.vareps = k.sb("vareps", [P, GT])
    k.rstd = k.sb("rstd", [P, GT])
    k.xn = k.sb("xn", [P, 2, GT, D])
    return k


LN_TICKS = 2 * GT + 7


def layernorm_dve(k, s, dve, g, slot, xn_free):
    nc = k.nc
    base = g * LN_TICKS
    for i in range(GT):
        nc.vector.bn_stats(k.stats[:, i, :], k.X[:, g * GT + i, :]).then_inc(s["ln_tick"], 1)
    dve.wait_ge(s["ln_tick"], base + GT)
    mean_e, dev_e, mean_o, dev_o = (k.stats[:, :, j] for j in (1, 2, 4, 5))
    nc.vector.tensor_tensor(k.diff[:], mean_e, mean_o, ALU.subtract).then_inc(s["ln_tick"], 1)
    nc.vector.scalar_tensor_tensor(out=k.dev[:], in0=dev_e, scalar=D * LN_EPS, in1=dev_o, op0=ALU.add, op1=ALU.add).then_inc(s["ln_tick"], 1)
    nc.vector.tensor_tensor(k.mean[:], mean_e, mean_o, ALU.add).then_inc(s["ln_tick"], 1)
    dve.wait_ge(s["ln_tick"], base + GT + 1)
    nc.vector.scalar_tensor_tensor(out=k.diff[:], in0=k.diff[:], scalar=D / 4, in1=k.diff[:], op0=ALU.mult, op1=ALU.mult).then_inc(s["ln_tick"], 1)
    dve.wait_ge(s["ln_tick"], base + GT + 4)
    nc.vector.tensor_tensor(k.dev[:], k.dev[:], k.diff[:], ALU.add).then_inc(s["ln_tick"], 1)
    nc.vector.tensor_scalar(k.mean[:], k.mean[:], 0.5, None, ALU.mult).then_inc(s["ln_tick"], 1)
    dve.wait_ge(s["ln_tick"], base + GT + 5)
    nc.vector.tensor_scalar(k.vareps[:], k.dev[:], 1.0 / D, None, ALU.mult).then_inc(s["ln_tick"], 1)
    xn_free()
    dve.wait_ge(s["ln_rstd"], g + 1)
    for i in range(GT):
        nc.vector.tensor_scalar(k.xn[:, slot, i, :], k.X[:, g * GT + i, :], k.mean[:, i:i + 1],
                                k.rstd[:, i:i + 1], ALU.subtract, ALU.mult).then_inc(s["ln_tick"], 1)
    dve.wait_ge(s["ln_tick"], base + LN_TICKS)


def layernorm_pool(k, s, pool, g):
    pool.wait_ge(s["ln_tick"], g * LN_TICKS + GT + 7)
    k.nc.gpsimd.tensor_tensor(k.rstd[:], k.vareps[:], k.neg_half[:], ALU.pow).then_inc(s["ln_rstd"], 1)


def sems(nc, ctx, stage, names):
    named = {n: ctx.enter_context(nc.semaphore(stage + n)) for n in names.split()}

    def zero():
        with nc.Block() as block:
            @block.gpsimd
            def _(pool):
                for h in named.values():
                    nc.gpsimd.sem_clear(h)
    ctx.callback(zero)
    return named


def stage_load(nc, k, x, loads):
    with ExitStack() as ctx:
        s = sems(nc, ctx, "ld_", "x w zero ident")
        block = ctx.enter_context(nc.Block())
        xg = x.rearrange("b (h p) d -> p (b h) d", p=P)

        @block.sync
        def _(sp):
            for q in range(4):
                n = TILES // 4
                nc.sync.dma_start(k.X[:, q * n:(q + 1) * n, :], xg[:, q * n:(q + 1) * n, :]).then_inc(s["x"], 16)
            for dst, src in loads:
                nc.sync.dma_start(dst, src).then_inc(s["w"], 16)
            sp.wait_ge(s["x"], 64)
            sp.wait_ge(s["w"], 16 * len(loads))

        @block.gpsimd
        def _(pool):
            nc.gpsimd.memset(k.X[:, TILES:TILES + 2 * GT, :], 0.0)
            nc.gpsimd.memset(k.neg_half[:], -0.5)
            nc.gpsimd.memset(k.ident[:], 0.0).then_inc(s["zero"], 1)
            pool.wait_ge(s["zero"], 1)
            nc.gpsimd.affine_select(out=k.ident[:], in_=k.ident[:], compare_op=ALU.not_equal, fill=1.0,
                                    base=0, pattern=[[-1, P]], channel_multiplier=1).then_inc(s["ident"], 1)
            pool.wait_ge(s["ident"], 1)


def weights(k, args):
    tiles, loads = {}, []
    for name, ap in args.items():
        if name == "x":
            continue
        if name == "c_kaug":
            tiles[name] = ap
            continue
        t = k.sb("w_" + name, list(ap.shape), F32)
        tiles[name] = t
        loads.append((t[:], ap))
    return tiles, loads


def stage_store(nc, k, out):
    with ExitStack() as ctx:
        s = sems(nc, ctx, "st_", "out")
        block = ctx.enter_context(nc.Block())
        og = out.rearrange("b (h p) d -> p (b h) d", p=P)

        @block.sync
        def _(sp):
            for q in range(4):
                n = TILES // 4
                nc.sync.dma_start(og[:, q * n:(q + 1) * n, :], k.X[:, q * n:(q + 1) * n, :]).then_inc(s["out"], 16)
            sp.wait_ge(s["out"], 64)


def stage_ffn(nc, k, tag, w1, b1, w2, b2rep):
    HID = w1.shape[1]
    NJ = HID // P
    with ExitStack() as ctx:
        s = sems(nc, ctx, tag, "ln_tick ln_rstd turned xT_ready up_done gelu_done down_done bias_done res_done")
        ps = lambda name, shape: ctx.enter_context(nc.psum_tensor(tag + name, shape, F32))
        turn = ps("turn", [P, 2, GW])
        hid = ps("hid", [P, NJ, GW])
        y = ps("y", [P, 2, GW])
        xT = ctx.enter_context(nc.sbuf_tensor(tag + "xT", [P, 2, GW], F32))
        hT = ctx.enter_context(nc.sbuf_tensor(tag + "hT", [P, NJ, GW], F32))
        block = ctx.enter_context(nc.Block())

        @block.vector
        def _(dve):
            def ln(g, slot, wait):
                def xn_free():
                    if wait:
                        dve.wait_ge(s["turned"], g - 1)
                layernorm_dve(k, s, dve, g, slot, xn_free)

            def residual(g, slot):
                dve.wait_ge(s["down_done"], g + 1)
                dve.wait_ge(s["bias_done"], g + 1)
                xg = k.X[:, bass.ds(g * GT, GT), :].rearrange("p a b -> p (a b)")
                nc.vector.tensor_tensor(xg, y[:, slot, :], xg, ALU.add).then_inc(s["res_done"], 1)

            ln(0, 0, False)
            ln(1, 1, False)
            residual(0, 0)
            ln(2, 0, True)
            residual(1, 1)
            with dve.Fori(1, NG // 2) as i:
                for u in range(2):
                    g = i * 2 + u
                    ln(g + 1, 1 - u, True)
                    residual(g, u)
            dve.wait_ge(s["res_done"], NG)

        @block.gpsimd
        def _(pool):
            layernorm_pool(k, s, pool, 0)

            def one(g):
                layernorm_pool(k, s, pool, g + 1)
                pool.wait_ge(s["ln_tick"], (g + 1) * LN_TICKS)
                xg = k.X[:, bass.ds(g * GT, GT), :]
                nc.gpsimd.tensor_tensor(xg, xg, b2rep[:, None, :].to_broadcast([P, GT, D]), ALU.add).then_inc(s["bias_done"], 1)
            with pool.Fori(0, NG) as g:
                one(g)

        @block.tensor
        def _(pe):
            def turn_in(g, slot, wait):
                pe.wait_ge(s["ln_tick"], (g + 1) * LN_TICKS)
                if wait:
                    pe.wait_ge(s["xT_ready"], g - 1)
                for i in range(GT):
                    m = nc.tensor.transpose(turn[:, slot, i * P:(i + 1) * P], k.xn[:, slot, i, :], k.ident[:])
                m.then_inc(s["turned"], 1)

            def up(g, slot, wait):
                pe.wait_ge(s["xT_ready"], g + 1)
                for j in range(NJ):
                    if wait:
                        pe.wait_ge(s["gelu_done"], (g - 1) * NJ + j + 1)
                    nc.tensor.matmul(hid[:, j, :], lhsT=w1[:, j * P:(j + 1) * P], rhs=xT[:, slot, :],
                                     start=True, stop=True).then_inc(s["up_done"], 1)

            def down(g, slot, wait):
                if wait:
                    pe.wait_ge(s["res_done"], g - 1)
                for j in range(NJ):
                    pe.wait_ge(s["gelu_done"], g * NJ + j + 1)
                    for i in range(GT):
                        m = nc.tensor.matmul(y[:, slot, i * P:(i + 1) * P], lhsT=hT[:, j, i * P:(i + 1) * P],
                                             rhs=w2[:, j, :], start=(j == 0 and i == 0), stop=(j == NJ - 1),
                                             skip_group_check=True)
                m.then_inc(s["down_done"], 1)

            turn_in(0, 0, False)
            up(0, 0, False)
            turn_in(1, 1, False)
            down(0, 0, False)
            up(1, 1, True)
            turn_in(2, 0, True)
            down(1, 1, False)
            with pe.Fori(1, NG // 2) as i:
                for u in range(2):
                    g = i * 2 + u
                    up(g, u, True)
                    turn_in(g + 1, 1 - u, True)
                    down(g, u, True)

        @block.scalar
        def _(act):
            def evac(g, slot, wait):
                act.wait_ge(s["turned"], g + 1)
                if wait:
                    act.wait_ge(s["up_done"], (g - 1) * NJ)
                nc.scalar.copy(xT[:, slot, :], turn[:, slot, :]).then_inc(s["xT_ready"], 1)

            def gelu(g, slot, wait):
                for j in range(NJ):
                    act.wait_ge(s["up_done"], g * NJ + j + 1)
                    if wait and j == 0:
                        act.wait_ge(s["down_done"], g)
                    nc.scalar.activation(hT[:, j, :], hid[:, j, :], ACT.Gelu, bias=b1[:, j:j + 1]).then_inc(s["gelu_done"], 1)

            evac(0, 0, False)
            gelu(0, 0, False)
            evac(1, 1, False)
            gelu(1, 1, True)
            evac(2, 0, True)
            with act.Fori(1, NG // 2) as i:
                for u in range(2):
                    g = i * 2 + u
                    gelu(g, u, True)
                    evac(g + 1, 1 - u, True)


HA = 16
KD = 4
VD = 8
HK = HA * KD


def stage_rwkv(nc, k, tag, w):
    with ExitStack() as ctx:
        s = sems(nc, ctx, tag, "pre ln_tick ln_rstd turned xT_ready delta_done xm_done low_done low_out mus_done dm_done xi_done "
                 "tw_done tw_out rk_done rk_out w_done ew_done dec_done v_done kv_done gate_done th_done gg_done "
                 "scan_done q_done rs_done oc_done sq_done var_done ln_done y0_done norm z_done y_done res_done zero")
        ps = lambda name, shape: ctx.enter_context(nc.psum_tensor(tag + name, shape, F32))
        sb = lambda name, shape, dt=F32: ctx.enter_context(nc.sbuf_tensor(tag + name, shape, dt))
        bank = ps("bank", [P, 5, GW])
        vp = ps("vp", [P, 2, 2, T])
        xT = sb("xT", [P, 2, T + 1])
        delta = sb("delta", [P, GW])
        xm = sb("xm", [P, GW])
        low = sb("low", [P, 2, GW])
        xi = sb("xi", [P, 5, GW])
        tw = sb("tw", [HK, GW])
        rk = sb("rk", [P, 2, 2, T])
        ew = sb("ew", [P, T])
        dec = sb("dec", [P, 2, T])
        kv = sb("kv", [P, VD, T])
        S = sb("S", [P, VD, T + 1])
        rS = sb("rS", [P, VD, T])
        th = sb("th", [P, GW])
        gg = sb("gg", [P, 2, GW])
        sq = sb("sq", [P, GW])
        lnv = sb("lnv", [P, GW])
        y0 = sb("y0", [P, GW])
        nt = sb("nt", [P, 2, GW])
        z = sb("z", [P, GW])
        gw = sb("gw", [P, 2])
        epsc = sb("epsc", [P, 1])
        seq = lambda ap: ap.rearrange("p (b t) -> p b t", b=2)
        flat = lambda ap: ap.rearrange("p b t -> p (b t)")
        x = xT[:, :, 1:T + 1]
        shifted = xT[:, :, 0:T]
        BANK = {"turn": 0, "oc": 1, "gate": 2, "var": 3, "low0": 4, "low1": 0, "m0": 1, "m1": 2, "m2": 3, "m3": 4, "m4": 0,
                "tw": 1, "y": 2, "rk": 3, "w": 4}
        at = {n: bank[:, b, :] for n, b in BANK.items()}
        block = ctx.enter_context(nc.Block())

        @block.vector
        def _(dve):
            nc.vector.memset(epsc[:], LN_EPS).then_inc(s["pre"], 1)
            nc.vector.tensor_scalar(gw[:, 0:1], w["a_gnw"][:], 0.5, None, ALU.mult).then_inc(s["pre"], 1)
            nc.vector.tensor_scalar(gw[:, 1:2], w["a_gnb"][:], 0.5, None, ALU.mult).then_inc(s["pre"], 1)
            dve.wait_ge(s["pre"], 3)

            def ln(p, slot, wait, between=None):
                def xn_free():
                    if between:
                        between()
                    if wait:
                        dve.wait_ge(s["turned"], p - 1)
                layernorm_dve(k, s, dve, p, slot, xn_free)

            def mix_in(p, later):
                dve.wait_ge(s["delta_done"], p + 1)
                if later:
                    dve.wait_ge(s["low_done"], 2 * p)
                nc.vector.scalar_tensor_tensor(out=seq(xm[:]), in0=seq(delta[:]), scalar=w["a_mux"][:, 0:1], in1=x,
                                               op0=ALU.mult, op1=ALU.add).then_inc(s["xm_done"], 1)

            def mix_out(p, later):
                for i in range(5):
                    dve.wait_ge(s["mus_done"], 5 * p + i + 1)
                    if later and i == 0:
                        dve.wait_ge(s["rk_done"], p)
                    if later and i == 3:
                        dve.wait_ge(s["gate_done"], p)
                    nc.vector.scalar_tensor_tensor(out=xi[:, i, :], in0=at[f"m{i}"], scalar=w["a_xb"][:, i:i + 1],
                                                   in1=delta[:], op0=ALU.add, op1=ALU.mult).then_inc(s["dm_done"], 1)

            def outer(p, slot):
                for v in range(4):
                    dve.wait_ge(s["v_done"], 4 * p + v + 1)
                    if v == 0:
                        dve.wait_ge(s["rk_out"], p + 1)
                    nc.vector.tensor_tensor(kv[:, 2 * v:2 * v + 2, :], vp[:, v % 2, :, :],
                                            rk[:, slot, 1:2, :].to_broadcast([P, 2, T]), ALU.mult).then_inc(s["kv_done"], 1)

            def gate(p, slot):
                dve.wait_ge(s["th_done"], p + 1)
                nc.vector.scalar_tensor_tensor(out=gg[:, slot, :], in0=th[:], scalar=1.0, in1=at["gate"],
                                               op0=ALU.add, op1=ALU.mult).then_inc(s["gg_done"], 1)

            def scans(p, slot, later):
                dve.wait_ge(s["dec_done"], p + 1)
                if later:
                    dve.wait_ge(s["q_done"], 4 * p)
                for v in range(VD):
                    if v % 2 == 0:
                        dve.wait_ge(s["kv_done"], 4 * p + v // 2 + 1)
                    nc.vector.tensor_tensor_scan(S[:, v, 1:T + 1], dec[:, slot, :], kv[:, v, :], 0.0,
                                                 ALU.mult, ALU.add).then_inc(s["scan_done"], 1)
                for v in range(4):
                    dve.wait_ge(s["scan_done"], VD * p + 2 * v + 2)
                    nc.vector.scalar_tensor_tensor(out=kv[:, 2 * v:2 * v + 2, :], in0=kv[:, 2 * v:2 * v + 2, :],
                                                   scalar=w["a_u"][:, 0:1], in1=S[:, 2 * v:2 * v + 2, 0:T],
                                                   op0=ALU.mult, op1=ALU.add).then_inc(s["q_done"], 1)

            def finish(p, slot, later):
                dve.wait_ge(s["y0_done"], p + 1)
                nc.vector.scalar_tensor_tensor(out=nt[:, 0, :], in0=at["var"], scalar=LN_EPS, in1=y0[:],
                                               op0=ALU.add, op1=ALU.mult).then_inc(s["norm"], 1)
                dve.wait_ge(s["norm"], 5 * p + 1)
                nc.vector.scalar_tensor_tensor(out=nt[:, 1, :], in0=nt[:, 0, :], scalar=-0.5, in1=y0[:],
                                               op0=ALU.mult, op1=ALU.mult).then_inc(s["norm"], 1)
                dve.wait_ge(s["norm"], 5 * p + 2)
                nc.vector.scalar_tensor_tensor(out=nt[:, 0, :], in0=nt[:, 1, :], scalar=1.5, in1=y0[:],
                                               op0=ALU.add, op1=ALU.mult).then_inc(s["norm"], 1)
                dve.wait_ge(s["norm"], 5 * p + 3)
                nc.vector.tensor_tensor(nt[:, 1, :], at["oc"], nt[:, 0, :], ALU.mult).then_inc(s["norm"], 1)
                dve.wait_ge(s["norm"], 5 * p + 4)
                nc.vector.tensor_scalar(nt[:, 0, :], nt[:, 1, :], gw[:, 0:1], gw[:, 1:2], ALU.mult, ALU.add).then_inc(s["norm"], 1)
                dve.wait_ge(s["norm"], 5 * p + 5)
                if later:
                    dve.wait_ge(s["y_done"], p)
                nc.vector.tensor_tensor(z[:], nt[:, 0, :], gg[:, slot, :], ALU.mult).then_inc(s["z_done"], 1)
                dve.wait_ge(s["z_done"], p + 1)

            def residual(p):
                dve.wait_ge(s["y_done"], p + 1)
                xg = k.X[:, bass.ds(p * GT, GT), :].rearrange("p a b -> p (a b)")
                nc.vector.tensor_tensor(xg, at["y"], xg, ALU.add).then_inc(s["res_done"], 1)

            def iteration(g, u, first):
                mix_in(g + 1, True)
                outer(g, u)
                gate(g, u)
                if not first:
                    finish(g - 1, 1 - u, not (isinstance(g, int) and g == 1))
                mix_out(g + 1, True)
                ln(g + 2, u, True, lambda: scans(g, u, not first))
                if not first:
                    residual(g - 1)

            dve.wait_ge(s["zero"], 1)
            ln(0, 0, False)
            mix_in(0, False)
            mix_out(0, False)
            ln(1, 1, False)
            iteration(0, 0, True)
            iteration(1, 1, False)
            with dve.Fori(1, NG // 2) as i:
                for u in range(2):
                    iteration(i * 2 + u, u, False)
            finish(NG - 1, 1, True)
            residual(NG - 1)
            dve.wait_ge(s["res_done"], NG)

        @block.gpsimd
        def _(pool):
            nc.gpsimd.memset(S[:, :, 0:1], 0.0)
            nc.gpsimd.memset(xT[:, :, 0:1], 0.0).then_inc(s["zero"], 1)

            def shift(p, later):
                pool.wait_ge(s["xT_ready"], p + 1)
                if later:
                    pool.wait_ge(s["dm_done"], 5 * p)
                nc.gpsimd.tensor_tensor(seq(delta[:]), shifted, x, ALU.subtract).then_inc(s["delta_done"], 1)

            def add_x(p):
                for i in range(5):
                    pool.wait_ge(s["dm_done"], 5 * p + i + 1)
                    nc.gpsimd.tensor_tensor(seq(xi[:, i, :]), seq(xi[:, i, :]), x, ALU.add).then_inc(s["xi_done"], 1)

            def read(p, slot, later):
                if later:
                    pool.wait_ge(s["oc_done"], p)
                for v in range(4):
                    pool.wait_ge(s["q_done"], 4 * p + v + 1)
                    nc.gpsimd.tensor_tensor(rS[:, 2 * v:2 * v + 2, :], kv[:, 2 * v:2 * v + 2, :],
                                            rk[:, slot, 0:1, :].to_broadcast([P, 2, T]), ALU.mult).then_inc(s["rs_done"], 1)

            def iteration(g, u, first):
                shift(g + 1, True)
                add_x(g + 1)
                layernorm_pool(k, s, pool, g + 2)
                read(g, u, not first)

            layernorm_pool(k, s, pool, 0)
            shift(0, False)
            add_x(0)
            layernorm_pool(k, s, pool, 1)
            iteration(0, 0, True)
            iteration(1, 1, False)
            with pool.Fori(1, NG // 2) as i:
                for u in range(2):
                    iteration(i * 2 + u, u, False)

        @block.tensor
        def _(pe):
            def turn_in(p, slot):
                pe.wait_ge(s["ln_tick"], (p + 1) * LN_TICKS)
                for i in range(GT):
                    mm = nc.tensor.transpose(at["turn"][:, i * P:(i + 1) * P], k.xn[:, slot, i, :], k.ident[:])
                mm.then_inc(s["turned"], 1)

            def front(p, banks_busy):
                pe.wait_ge(s["xm_done"], p + 1)
                for i in range(2):
                    if i == 0 and banks_busy:
                        pe.wait_ge(s["ew_done"], p)
                    nc.tensor.matmul(at[f"low{i}"], lhsT=w["a_wx1"][:, 32 * i:32 * i + P], rhs=xm[:], start=True, stop=True)\
                        .then_inc(s["low_done"], 1)
                for i in range(5):
                    pe.wait_ge(s["low_out"], 2 * p + (1 if i < 4 else 2))
                    if i == 3:
                        pe.wait_ge(s["low_out"], 2 * p + 1)
                    if i < 3 and banks_busy:
                        banks_busy(i)
                    nc.tensor.matmul(at[f"m{i}"], lhsT=w["a_wx2"][:, i, :], rhs=low[:, i // 4, :], start=True, stop=True)\
                        .then_inc(s["mus_done"], 1)
                pe.wait_ge(s["xi_done"], 5 * p + 2)
                nc.tensor.matmul(at["tw"][0:HK, :], lhsT=w["a_ww1"][:], rhs=xi[:, 1, :], start=True, stop=True)\
                    .then_inc(s["tw_done"], 1)

            def front2(p):
                pe.wait_ge(s["xi_done"], 5 * p + 3)
                for j, (wn, i) in enumerate((("a_wr", 0), ("a_wk", 2))):
                    if j == 1:
                        pe.wait_ge(s["tw_out"], p + 1)
                        pe.wait_ge(s["dm_done"], 5 * p + 4)
                    for b in range(2):
                        mm = nc.tensor.matmul(at["rk"][b * HK:(b + 1) * HK, j * T:(j + 1) * T], lhsT=w[wn][:],
                                              rhs=xi[:, i, b * T:(b + 1) * T], start=True, stop=True, skip_group_check=True)
                mm.then_inc(s["rk_done"], 1)
                for b in range(2):
                    mm = nc.tensor.matmul(at["w"][b * HK:(b + 1) * HK, 0:T], lhsT=w["a_ww2"][:], rhs=tw[:, b * T:(b + 1) * T],
                                          start=True, stop=True, skip_group_check=True)
                mm.then_inc(s["w_done"], 1)

            def values(p):
                pe.wait_ge(s["xi_done"], 5 * p + 5)
                for v in range(4):
                    pe.wait_ge(s["kv_done"], 4 * p + v - 1) if not (isinstance(p, int) and p == 0 and v < 2) else None
                    for a in range(2):
                        for b in range(2):
                            mm = nc.tensor.matmul(vp[b * HK:(b + 1) * HK, v % 2, a, :], lhsT=w["a_wv"][:, 2 * v + a, :],
                                                  rhs=xi[:, 3, b * T:(b + 1) * T], start=True, stop=True, skip_group_check=True)
                    mm.then_inc(s["v_done"], 1)

            def gate(p, first):
                if first:
                    pe.wait_ge(s["dm_done"], 5 * p + 2)
                else:
                    pe.wait_ge(s["res_done"], p - 1) if not (isinstance(p, int) and p == 1) else pe.wait_ge(s["dm_done"], 5 * p + 2)
                nc.tensor.matmul(at["gate"], lhsT=w["a_wg"][:], rhs=xi[:, 4, :], start=True, stop=True).then_inc(s["gate_done"], 1)

            def heads(p):
                pe.wait_ge(s["rs_done"], 4 * (p + 1))
                for b in range(2):
                    for v in range(VD):
                        mm = nc.tensor.matmul(at["oc"][:, b * T:(b + 1) * T], lhsT=w["a_sel"][:, b, v, :], rhs=rS[:, v, :],
                                              start=(v == 0), stop=(v == VD - 1))
                mm.then_inc(s["oc_done"], 1)

            def variance(p):
                pe.wait_ge(s["sq_done"], p + 1)
                nc.tensor.matmul(at["var"], lhsT=w["a_bo"][:], rhs=sq[:], start=True, stop=True).then_inc(s["var_done"], 1)

            def out(p):
                pe.wait_ge(s["z_done"], p + 1)
                for i in range(GT):
                    mm = nc.tensor.matmul(at["y"][:, i * P:(i + 1) * P], lhsT=z[:, i * P:(i + 1) * P], rhs=w["a_wo"][:],
                                          start=True, stop=True)
                mm.then_inc(s["y_done"], 1)

            def iteration(g, u, first):
                pe.wait_ge(s["dm_done"], 5 * (g + 1))
                turn_in(g + 1, 1 - u)
                if not first:
                    pe.wait_ge(s["tw_out"], g + 1)
                    heads(g - 1)
                values(g)
                gate(g, first)
                if not first:
                    pe.wait_ge(s["rk_out"], g + 1)
                    variance(g - 1)

                def busy(i):
                    if first:
                        pe.wait_ge((s["tw_out"], s["gg_done"], s["rk_out"])[i], 1)
                    elif i == 1:
                        pe.wait_ge(s["gg_done"], g + 1)
                    elif i == 0:
                        pe.wait_ge(s["norm"], 5 * g - 1)
                front(g + 1, busy)
                if not first:
                    pe.wait_ge(s["dm_done"], 5 * (g + 1) + 2)
                    out(g - 1)
                front2(g + 1)

            turn_in(0, 0)
            front(0, None)
            front2(0)
            iteration(0, 0, True)
            iteration(1, 1, False)
            with pe.Fori(1, NG // 2) as i:
                for u in range(2):
                    iteration(i * 2 + u, u, False)
            pe.wait_ge(s["tw_out"], NG + 1)
            heads(NG - 1)
            pe.wait_ge(s["rk_out"], NG + 1)
            variance(NG - 1)
            out(NG - 1)

        @block.scalar
        def _(act):
            act.wait_ge(s["pre"], 3)
            act.wait_ge(s["zero"], 1)

            def evac(p, later):
                act.wait_ge(s["turned"], p + 1)
                if later:
                    act.wait_ge(s["xi_done"], 5 * p)
                nc.scalar.copy(x, seq(at["turn"])).then_inc(s["xT_ready"], 1)

            def front(p, slot):
                for i in range(2):
                    act.wait_ge(s["low_done"], 2 * p + i + 1)
                    nc.scalar.activation(low[:, i, :], at[f"low{i}"], ACT.Tanh).then_inc(s["low_out"], 1)
                act.wait_ge(s["tw_done"], p + 1)
                nc.scalar.activation(tw[:], at["tw"][0:HK, :], ACT.Tanh).then_inc(s["tw_out"], 1)
                act.wait_ge(s["rk_done"], p + 1)
                nc.scalar.copy(rk[:, slot, :, :].rearrange("p j t -> p (j t)"), at["rk"]).then_inc(s["rk_out"], 1)
                act.wait_ge(s["w_done"], p + 1)
                nc.scalar.activation(ew[:], at["w"][:, 0:T], ACT.Exp, bias=w["a_bw2"][:, 0:1]).then_inc(s["ew_done"], 1)
                act.wait_ge(s["ew_done"], p + 1)
                nc.scalar.activation(dec[:, slot, :], ew[:], ACT.Exp, scale=-1.0).then_inc(s["dec_done"], 1)

            def gate(p, later):
                act.wait_ge(s["gate_done"], p + 1)
                if later:
                    act.wait_ge(s["gg_done"], p)
                nc.scalar.activation(th[:], at["gate"], ACT.Tanh, scale=0.5).then_inc(s["th_done"], 1)

            def norm(p, later):
                act.wait_ge(s["oc_done"], p + 1)
                nc.scalar.activation(sq[:], at["oc"], ACT.Square).then_inc(s["sq_done"], 1)
                nc.scalar.preload_act_table_set("natural_log_exp_and_others")
                act.wait_ge(s["var_done"], p + 1)
                nc.scalar.activation(lnv[:], at["var"], ACT.Ln, bias=epsc[:, 0:1]).then_inc(s["ln_done"], 1)
                act.wait_ge(s["ln_done"], p + 1)
                if later:
                    act.wait_ge(s["norm"], 5 * p)
                nc.scalar.activation(y0[:], lnv[:], ACT.Exp, scale=-0.5).then_inc(s["y0_done"], 1)

            def iteration(g, u, first):
                evac(g + 1, True)
                gate(g, not first)
                if not first:
                    norm(g - 1, not (isinstance(g, int) and g == 1))
                front(g + 1, 1 - u)

            evac(0, False)
            front(0, 0)
            iteration(0, 0, True)
            iteration(1, 1, False)
            with act.Fori(1, NG // 2) as i:
                for u in range(2):
                    iteration(i * 2 + u, u, False)
            norm(NG - 1, True)


HB = 16
HG = 4
HD = D // HB
QROWS = 3 * HG * HD
AUG = 5
KROWS = QROWS + AUG


def at_least(eng, sem, v):
    if not (isinstance(v, int) and v <= 0):
        eng.wait_ge(sem, v)


def stage_retention(nc, k, tag, w, scr):
    with ExitStack() as ctx:
        VO = ctx.enter_context(nc.sbuf_tensor(tag + "VO", [P, TILES, D], F32))
        XM = ctx.enter_context(nc.sbuf_tensor(tag + "XM", [P, B], F32))
        LD = ctx.enter_context(nc.sbuf_tensor(tag + "LD", [P, B * HB], F32))
        retention_project(nc, k, tag + "p", w, scr, VO, XM)
        retention_decay(nc, k, tag + "d", w, scr, XM, LD)
        retention_attend(nc, k, tag + "t", w, scr, VO, LD)
        retention_finish(nc, k, tag + "f", w, scr, VO)


def retention_project(nc, k, tag, w, scr, VO, XM):
    with ExitStack() as ctx:
        s = sems(nc, ctx, tag, "ln_tick ln_rstd turned xT_ready sum_done qk_done cs_done rot_done hi_done lo_done "
                 "g_done th_done gate_done v_done v_out half out0 out1")
        out_sem = (s["out0"], s["out1"])
        ps = lambda name, shape: ctx.enter_context(nc.psum_tensor(tag + name, shape, F32))
        sb = lambda name, shape, dt=F32: ctx.enter_context(nc.sbuf_tensor(tag + name, shape, dt))
        turn = ps("turn", [P, GW])
        qk = ps("qk", [P, 4, GW])
        gp = ps("gp", [P, GW])
        vp = ps("vp", [P, GW])
        xT = sb("xT", [P, 2, GW])
        cs = sb("cs", [P, 4, GW])
        rot = sb("rot", [P, 2, GW])
        hi = sb("hi", [P, 2, 2, GW], F16)
        lo = sb("lo", [P, 2, 2, GW], F16)
        th = sb("th", [P, GW])
        gateb = sb("gateb", [P, GW])
        hbg = sb("hbg", [P, 1])
        gate = sb("gate", [P, 2, GW])
        two = lambda ap: ap.rearrange("p (b t) -> p b t", b=2)
        OUTS = 16 * 7
        block = ctx.enter_context(nc.Block())

        @block.vector
        def _(dve):
            def ln(g, slot, wait):
                def xn_free():
                    if wait:
                        dve.wait_ge(s["turned"], g - 1)
                layernorm_dve(k, s, dve, g, slot, xn_free)

            def work(g, slot, i):
                dve.wait_ge(s["xT_ready"], g + 1)
                nc.vector.tensor_reduce(out=XM[:, bass.ds(g * 2, 2)], in_=two(xT[:, slot, :]), axis=AX.X, op=ALU.add).then_inc(s["sum_done"], 1)
                for j in range(4):
                    dve.wait_ge(s["qk_done"], 4 * g + j + 1)
                    if j % 2 == 0:
                        at_least(dve, s["rot_done"], 2 * g - 1 + j // 2)
                    nc.vector.scalar_tensor_tensor(out=two(cs[:, j, :]), in0=two(qk[:, j, :]), scalar=w["c_bqk"][:, j:j + 1],
                                                   in1=w["c_tab"][:, j:j + 1, :].to_broadcast([P, 2, T]),
                                                   op0=ALU.add, op1=ALU.mult).then_inc(s["cs_done"], 1)
                dve.wait_ge(s["v_done"], g + 1)
                nc.vector.tensor_tensor(VO[:, bass.ds(g * GT, GT), :], vp[:].rearrange("p (a d) -> p a d", a=GT),
                                        w["c_bv"][:, None, :].to_broadcast([P, GT, D]), ALU.add).then_inc(s["v_out"], 1)
                dve.wait_ge(s["th_done"], g + 1)
                at_least(dve, out_sem[slot], OUTS * i)
                nc.vector.scalar_tensor_tensor(out=gate[:, slot, :], in0=th[:], scalar=1.0, in1=gateb[:], op0=ALU.add,
                                               op1=ALU.mult).then_inc(s["gate_done"], 1)
                for j in range(2):
                    dve.wait_ge(s["hi_done"], 2 * g + j + 1)
                    nc.vector.tensor_tensor(lo[:, slot, j, :], rot[:, j, :], hi[:, slot, j, :], ALU.subtract).then_inc(s["lo_done"], 1)

            ln(0, 0, False)
            for u in range(2):
                ln(u + 1, 1 - u, u == 1)
                work(u, u, 0)
            with dve.Fori(1, NG // 2) as i:
                for u in range(2):
                    g = i * 2 + u
                    ln(g + 1, 1 - u, True)
                    work(g, u, i)

        @block.gpsimd
        def _(pool):
            layernorm_pool(k, s, pool, 0)

            def one(g):
                layernorm_pool(k, s, pool, g + 1)
                for j in range(2):
                    pool.wait_ge(s["cs_done"], 4 * g + 2 * j + 2)
                    at_least(pool, s["lo_done"], 2 * g - 1 + j)
                    nc.gpsimd.tensor_tensor(rot[:, j, :], cs[:, 2 * j, :], cs[:, 2 * j + 1, :], ALU.add).then_inc(s["rot_done"], 1)
            one(0)
            with pool.Fori(1, NG) as g:
                one(g)

        @block.scalar
        def _(act):
            def evac(g, slot, wait):
                act.wait_ge(s["turned"], g + 1)
                if wait:
                    act.wait_ge(s["v_done"], g - 1)
                    act.wait_ge(s["sum_done"], g - 1)
                nc.scalar.copy(xT[:, slot, :], turn[:]).then_inc(s["xT_ready"], 1)

            def work(g, slot, i):
                act.wait_ge(s["g_done"], g + 1)
                at_least(act, s["gate_done"], g)
                nc.scalar.activation(th[:], gp[:], ACT.Tanh, scale=0.5, bias=hbg[:, 0:1])
                nc.scalar.activation(gateb[:], gp[:], ACT.Identity, bias=w["c_bg"][:, 0:1]).then_inc(s["th_done"], 1)
                at_least(act, out_sem[slot], OUTS * i)
                for j in range(2):
                    act.wait_ge(s["rot_done"], 2 * g + j + 1)
                    nc.scalar.copy(hi[:, slot, j, :], rot[:, j, :]).then_inc(s["hi_done"], 1)

            nc.scalar.mul(hbg[:], w["c_bg"][:], 0.5).then_inc(s["half"], 1)
            act.wait_ge(s["half"], 1)
            evac(0, 0, False)
            for u in range(2):
                evac(u + 1, 1 - u, u == 1)
                work(u, u, 0)
            with act.Fori(1, NG // 2) as i:
                for u in range(2):
                    g = i * 2 + u
                    evac(g + 1, 1 - u, True)
                    work(g, u, i)

        @block.tensor
        def _(pe):
            def turn_in(g, slot):
                pe.wait_ge(s["ln_tick"], (g + 1) * LN_TICKS)
                at_least(pe, s["xT_ready"], g)
                for i in range(GT):
                    m = nc.tensor.transpose(turn[:, i * P:(i + 1) * P], k.xn[:, slot, i, :], k.ident[:])
                m.then_inc(s["turned"], 1)

            def project(g, slot):
                pe.wait_ge(s["xT_ready"], g + 1)
                for j in range(4):
                    at_least(pe, s["cs_done"], 4 * g - 3 + j)
                    nc.tensor.matmul(qk[:, j, :], lhsT=w["c_wqk"][:, j, :], rhs=xT[:, slot, :], start=True, stop=True)\
                        .then_inc(s["qk_done"], 1)
                at_least(pe, s["th_done"], g)
                nc.tensor.matmul(gp[:], lhsT=w["c_wg"][:], rhs=xT[:, slot, :], start=True, stop=True).then_inc(s["g_done"], 1)
                at_least(pe, s["v_out"], g)
                for i in range(GT):
                    m = nc.tensor.matmul(vp[:, i * P:(i + 1) * P], lhsT=xT[:, slot, i * P:(i + 1) * P], rhs=w["c_wv"][:],
                                         start=True, stop=True, skip_group_check=True)
                m.then_inc(s["v_done"], 1)

            turn_in(0, 0)
            for u in range(2):
                turn_in(u + 1, 1 - u)
                project(u, u)
            with pe.Fori(1, NG // 2) as i:
                for u in range(2):
                    g = i * 2 + u
                    turn_in(g + 1, 1 - u)
                    project(g, u)

        @block.sync
        def _(sp):
            def store(g, slot):
                at = bass.ds(g * GW, GW)
                sp.wait_ge(s["gate_done"], g + 1)
                sp.wait_ge(s["lo_done"], 2 * g + 2)
                nc.sync.dma_start(scr["gate"][:, at], gate[:, slot, :]).then_inc(out_sem[slot], 16)
                for term, (qs, ks) in enumerate(((hi, hi), (lo, hi), (hi, lo))):
                    nc.sync.dma_start(scr["q"][term, :, at], qs[:, slot, 0, :]).then_inc(out_sem[slot], 16)
                    nc.sync.dma_start(scr["k"][term, :, at], ks[:, slot, 1, :]).then_inc(out_sem[slot], 16)
            with sp.Fori(0, NG // 2) as i:
                for u in range(2):
                    store(i * 2 + u, u)
            for q in out_sem:
                sp.wait_ge(q, OUTS * NG // 2)


def retention_decay(nc, k, tag, w, scr, XM, LD):
    with ExitStack() as ctx:
        s = sems(nc, ctx, tag, "pre mm th e ld ldd back parts r_out")
        BL = B * HB // P
        ps = ctx.enter_context(nc.psum_tensor(tag + "ps", [HB, B], F32))
        sb = lambda name, shape, dt=F32: ctx.enter_context(nc.sbuf_tensor(tag + name, shape, dt))
        hb = sb("hb", [HB, 1])
        ec = sb("ec", [HB, 1])
        t = sb("t", [HB, B])
        L4 = sb("L4", [P, BL])
        full = sb("full", [P, 2, BL, P])
        part = sb("part", [P, 4, BL, P], F16)
        LN2 = float(np.log(2.0))
        block = ctx.enter_context(nc.Block())

        @block.tensor
        def _(pe):
            nc.tensor.matmul(ps[:], lhsT=w["c_wd"][:], rhs=XM[:], start=True, stop=True).then_inc(s["mm"], 1)

        @block.scalar
        def _(act):
            act.wait_ge(s["pre"], 2)
            act.wait_ge(s["mm"], 1)
            nc.scalar.activation(t[:], ps[:], ACT.Tanh, scale=0.5 / T, bias=hb[:, 0:1]).then_inc(s["th"], 1)
            act.wait_ge(s["th"], 1)
            nc.scalar.activation(t[:], t[:], ACT.Exp, scale=-4 * LN2, bias=ec[:, 0:1]).then_inc(s["e"], 1)
            act.wait_ge(s["e"], 1)
            nc.scalar.preload_act_table_set("natural_log_exp_and_others")
            nc.scalar.activation(t[:], t[:], ACT.Ln, scale=-1.0, bias=1.0).then_inc(s["ld"], 1)

        @block.sync
        def _(sp):
            sp.wait_ge(s["ld"], 1)
            nc.sync.dma_start(scr["ld"].rearrange("b h -> h b"), t[:], allow_slow_non_contiguous=True).then_inc(s["ldd"], 16)
            sp.wait_ge(s["ldd"], 16)
            flat = scr["ld"].rearrange("b h -> (b h)")
            nc.sync.dma_start(L4[:], flat.rearrange("(l p) -> p l", p=P), allow_slow_non_contiguous=True).then_inc(s["back"], 16)
            nc.sync.dma_start(LD[:], flat[None, :].to_broadcast([P, B * HB])).then_inc(s["back"], 16)
            sp.wait_ge(s["back"], 32)
            for r in range(4):
                sp.wait_ge(s["parts"], 6)
                nc.sync.dma_start(scr["aug"][r].rearrange("(l b) h q -> (b h) l q", l=BL), part[:, r]).then_inc(s["r_out"], 16)
            sp.wait_ge(s["r_out"], 64)

        @block.vector
        def _(dve):
            nc.vector.memset(ec[:], -9 * LN2).then_inc(s["pre"], 1)
            nc.vector.tensor_scalar(hb[:], w["c_bd"][:], 0.5, None, ALU.mult).then_inc(s["pre"], 1)
            dve.wait_ge(s["back"], 32)
            rep = L4[:][:, :, None].to_broadcast([P, BL, P])
            for r in range(2):
                nc.vector.tensor_tensor(full[:, r], rep, w["c_row"][:, r:r + 1, :].to_broadcast([P, BL, P]), ALU.mult).then_inc(s["parts"], 1)
            for r in range(2):
                dve.wait_ge(s["parts"], r + 1)
                nc.vector.tensor_copy(part[:, 2 * r], full[:, r]).then_inc(s["parts"], 1)
            for r in range(2):
                dve.wait_ge(s["parts"], r + 3)
                nc.vector.tensor_tensor(part[:, 2 * r + 1], full[:, r], part[:, 2 * r], ALU.subtract).then_inc(s["parts"], 1)


def retention_attend(nc, k, tag, w, scr, VO, LD):
    with ExitStack() as ctx:
        s = sems(nc, ctx, tag, "init ka_in0 ka_in1 kb_in0 kb_in1 m_in0 m_in1 const masked a_done max_done mt_done neg_done b_done exp_done "
                 "dmul_done pv_done ev_done t_done rec_done on_done o_done vo_done dprod dexp vs_done")
        ka_in, kb_in, m_in = (s["ka_in0"], s["ka_in1"]), (s["kb_in0"], s["kb_in1"]), (s["m_in0"], s["m_in1"])
        ps = lambda name, shape: ctx.enter_context(nc.psum_tensor(tag + name, shape, F32))
        sb = lambda name, shape, dt=F32: ctx.enter_context(nc.sbuf_tensor(tag + name, shape, dt))
        pa = ps("pa", [P, 2, 2, T])
        pb = ps("pb", [P, 2, 2 * T])
        pv = ps("pv", [P, 2, 2 * T])
        tb = ps("tb", [P, HG, HG, 32])
        misc = ps("misc", [P, 4, P])
        KA = sb("KA", [QROWS, 2, HG, T], F16)
        KB = sb("KB", [KROWS, 2, HG, T], F16)
        Q = sb("Q", [QROWS, 2, HG, T], F16)
        Qm = sb("Qm", [KROWS, 2, HB, T], F16)
        M = sb("M", [P, 2, 2 * HB])
        MT = sb("MT", [2 * HB, 2, P], F16)
        E = sb("E", [P, 4, 4, P])
        Dm = sb("Dm", [P, 2, HB, P])
        Vs = sb("Vs", [P, 2, 2, HB, 32])
        pvs = sb("pvs", [P, HG, T])
        rec = sb("rec", [P, HG, HG])
        O = sb("O", [P, 2, HB, HD])
        LEAD = 6
        block = ctx.enter_context(nc.Block())

        def load_ka(sp, i, u):
            b = i * 2 + u
            at_least(sp, s["a_done"], HB * (b - 1))
            at = bass.ds(b * T, T)
            nc.sync.dma_start(KA[:, u], scr["k"][:, :, at].rearrange("m (r g) t -> (m r) g t", g=HG)).then_inc(ka_in[u], 16)
            nc.sync.dma_start(Q[:, u], scr["q"][:, :, at].rearrange("m (r g) t -> (m r) g t", g=HG)).then_inc(ka_in[u], 16)

        def load_kb(sp, i, u):
            b = i * 2 + u
            at_least(sp, s["b_done"], HB * (b - 1))
            nc.sync.dma_start(KB[0:QROWS, u], scr["k"][:, :, bass.ds(b * T, T)].rearrange("m (r g) t -> (m r) g t", g=HG)).then_inc(kb_in[u], 16)
            nc.sync.dma_start(Qm[QROWS + 1:KROWS, u, :, 0:P], scr["aug"][:, bass.ds(b, 1)].rearrange("r b h q -> r (b h) q")).then_inc(kb_in[u], 16)

        @block.sync
        def _(sp):
            def put_max(i, u):
                b = i * 2 + u
                sp.wait_ge(s["neg_done"], b + 1)
                nc.sync.dma_start(Qm[QROWS:QROWS + 1, u].rearrange("o h (a q) -> o (h a) q", a=2), MT[:, u, :]).then_inc(m_in[u], 16)

            def iteration(i, u, last=False):
                if not last:
                    nxt = (i, 1) if u == 0 else (i + 1, 0)
                    if not (isinstance(i, int) and i == 0 and u == 0):
                        load_kb(sp, *nxt)
                    if not (isinstance(i, int) and i == B // 2 - 1):
                        load_ka(sp, i + 1, u)
                    put_max(*nxt)

            sp.wait_ge(s["init"], 4)
            for u in range(2):
                nc.sync.dma_start(KB[QROWS:KROWS, u].rearrange("r g t -> r (g t)"), w["c_kaug"]).then_inc(s["const"], 16)
            for u in range(2):
                load_ka(sp, 0, u)
                load_kb(sp, 0, u)
            put_max(0, 0)
            iteration(0, 0)
            iteration(0, 1)
            with sp.Fori(1, B // 2 - 1) as i:
                for u in range(2):
                    iteration(i, u)
            iteration(B // 2 - 1, 0)

        @block.tensor
        def _(pe):
            pe.wait_ge(s["const"], 32)

            def scores_q(i, u, h):
                b = i * 2 + u
                if h == 0:
                    pe.wait_ge(ka_in[u], 32 * (i + 1))
                if h % HG == 0:
                    pe.wait_ge(s["masked"], HG * b + h // HG + 1)
                at_least(pe, s["max_done"], HB * b + h - 1)
                for qt in range(2):
                    m = nc.tensor.matmul(pa[:, h % 2, qt, :], lhsT=Qm[0:QROWS, u, h, qt * P:(qt + 1) * P], rhs=KA[:, u, h // HG, :],
                                         start=True, stop=True, skip_group_check=True)
                m.then_inc(s["a_done"], 1)

            def turn_max(i, u):
                b = i * 2 + u
                pe.wait_ge(s["max_done"], HB * (b + 1))
                at_least(pe, s["neg_done"], b)
                at_least(pe, s["vo_done"], b - 1)
                nc.tensor.transpose(misc[0:2 * HB, 0, :], M[:, u, :], k.ident[:]).then_inc(s["mt_done"], 1)

            def scores_k(i, u, h):
                b = i * 2 + u
                if h == 0:
                    pe.wait_ge(kb_in[u], 32 * (i + 1))
                    pe.wait_ge(m_in[u], 16 * (i + 1))
                at_least(pe, s["exp_done"], HB * b + h - 1)
                for kt in range(2):
                    m = nc.tensor.matmul(pb[:, h % 2, kt * T:(kt + 1) * T], lhsT=KB[:, u, h // HG, kt * P:(kt + 1) * P],
                                         rhs=Qm[:, u, h, :], start=True, stop=True, skip_group_check=True)
                m.then_inc(s["b_done"], 1)

            def values(i, u, h):
                b = i * 2 + u
                g, hh = h // HG, h % HG
                if h == 0:
                    pe.wait_ge(s["vs_done"], b + 1)
                if hh == 0:
                    at_least(pe, s["ev_done"], HG * b + g - 1)
                pe.wait_ge(s["dmul_done"], HB * b + h + 1)
                for kt in range(2):
                    m = nc.tensor.matmul(pv[32 * hh:32 * (hh + 1), g % 2, 0:T], lhsT=Vs[:, u, kt, h, :],
                                         rhs=E[:, h % 4, 2 * kt:2 * kt + 2, :].rearrange("p a q -> p (a q)"),
                                         start=(kt == 0), stop=(kt == 1), skip_group_check=True)
                m.then_inc(s["pv_done"], 1)

            def turn_out(b, qt):
                pe.wait_ge(s["ev_done"], HG * (b + 1))
                at_least(pe, s["on_done"], 2 * b + qt)
                for g in range(HG):
                    m = nc.tensor.transpose(tb[:, g].rearrange("p a b -> p (a b)"), pvs[:, g, qt * P:(qt + 1) * P], k.ident[:])
                m.then_inc(s["t_done"], 1)

            def turn_back(b):
                at_least(pe, s["vo_done"], b)
                if not (isinstance(b, int) and b == B - 1):
                    pe.wait_ge(s["neg_done"], b + 2)
                for qt in range(2):
                    pe.wait_ge(s["on_done"], 2 * b + qt + 1)
                    m = nc.tensor.transpose(misc[:, 1 + qt, :], O[:, qt].rearrange("p h d -> p (h d)"), k.ident[:])
                m.then_inc(s["o_done"], 1)

            def iteration(i, u, first=False, last=False):
                b = i * 2 + u
                for t in range(HB + LEAD + 2):
                    if t == 0 and not first:
                        turn_out(b - 1, 0)
                    if t < HB and not last:
                        scores_q(*((i, 1) if u == 0 else (i + 1, 0)), t)
                    if t == 3 and not first:
                        turn_out(b - 1, 1)
                    if t == 5 and not first:
                        turn_back(b - 1)
                    if t == HB + 2 and not last:
                        turn_max(*((i, 1) if u == 0 else (i + 1, 0)))
                    if 0 <= t - LEAD < HB:
                        scores_k(i, u, t - LEAD)
                    if 0 <= t - LEAD - 2:
                        values(i, u, t - LEAD - 2)

            for h in range(HB):
                scores_q(0, 0, h)
            turn_max(0, 0)
            iteration(0, 0, first=True)
            iteration(0, 1)
            with pe.Fori(1, B // 2 - 1) as i:
                for u in range(2):
                    iteration(i, u)
            iteration(B // 2 - 1, 0)
            iteration(B // 2 - 1, 1, last=True)
            turn_out(B - 1, 0)
            turn_out(B - 1, 1)
            turn_back(B - 1)

        @block.vector
        def _(dve):
            nc.vector.memset(Vs[:], 0.0).then_inc(s["init"], 1)
            nc.vector.memset(Qm[96:KROWS], 0.0).then_inc(s["init"], 1)
            nc.vector.memset(KB[96:KROWS], 0.0).then_inc(s["init"], 1)
            dve.wait_ge(s["init"], 3)
            nc.vector.memset(Vs[:, :, :, :, HD:HD + 1], 1.0).then_inc(s["init"], 1)

            def mask(i, u, g):
                b = i * 2 + u
                if g == 0:
                    dve.wait_ge(ka_in[u], 32 * (i + 1))
                at_least(dve, s["b_done"], HB * (b - 2) + HG * (g + 1))
                for hh in range(HG):
                    m = nc.vector.tensor_scalar(Qm[0:QROWS, u, HG * g + hh, :], Q[:, u, g, :], w["c_mask"][0:QROWS, hh:hh + 1],
                                                None, ALU.mult)
                m.then_inc(s["masked"], 1)

            def maximum(i, u, h):
                b = i * 2 + u
                dve.wait_ge(s["a_done"], HB * b + h + 1)
                if h == 0:
                    at_least(dve, s["mt_done"], b - 1)
                nc.vector.tensor_reduce(out=M[:, u, 2 * h:2 * h + 2], in_=pa[:, h % 2], axis=AX.X, op=ALU.max).then_inc(s["max_done"], 1)

            def negate(i, u):
                b = i * 2 + u
                dve.wait_ge(s["mt_done"], b + 1)
                at_least(dve, m_in[u], 16 * i)
                nc.vector.tensor_scalar(MT[:, u, :], misc[0:2 * HB, 0, :], -1.0, None, ALU.mult).then_inc(s["neg_done"], 1)

            def evac(b, g):
                dve.wait_ge(s["pv_done"], HB * b + HG * (g + 1))
                at_least(dve, s["t_done"], 2 * b)
                nc.vector.tensor_copy(pvs[:, g, :], pv[:, g % 2, 0:T]).then_inc(s["ev_done"], 1)

            def normalise(b, qt):
                dve.wait_ge(s["t_done"], 2 * b + qt + 1)
                at_least(dve, s["on_done"], 2 * b + qt)
                nc.vector.reciprocal(rec[:], tb[:, :, :, HD]).then_inc(s["rec_done"], 1)
                dve.wait_ge(s["rec_done"], 2 * b + qt + 1)
                at_least(dve, s["o_done"], b)
                nc.vector.tensor_tensor(O[:, qt], tb[:, :, :, 0:HD].rearrange("p a b d -> p (a b) d"),
                                        rec[:].rearrange("p a b -> p (a b)")[:, :, None].to_broadcast([P, HB, HD]), ALU.mult).then_inc(s["on_done"], 1)

            def iteration(i, u, first=False, last=False, mask_next=True):
                b = i * 2 + u
                nxt = (i, 1) if u == 0 else (i + 1, 0)
                for t in range(HB + LEAD + 3):
                    if t < HB and not last:
                        maximum(*nxt, t)
                    if t in (1, 4) and not first:
                        normalise(b - 1, t // 4)
                    r = t - LEAD
                    if mask_next and r >= 3 and r % 4 == 3 and r < HB:
                        mask(i + 1, u, r // 4)
                    if r >= 6 and r % 4 == 2 and r <= HB + 2:
                        evac(b, r // 4 - 1)
                    if t == HB + 3 and not last:
                        negate(*nxt)

            dve.wait_ge(s["init"], 4)
            for u in range(2):
                for g in range(HG):
                    mask(0, u, g)
            for h in range(HB):
                maximum(0, 0, h)
            negate(0, 0)
            iteration(0, 0, first=True)
            iteration(0, 1)
            with dve.Fori(1, B // 2 - 1) as i:
                for u in range(2):
                    iteration(i, u)
            iteration(B // 2 - 1, 0, mask_next=False)
            iteration(B // 2 - 1, 1, last=True, mask_next=False)
            for qt in range(2):
                normalise(B - 1, qt)

        @block.scalar
        def _(act):
            def decay(b, u):
                act.wait_ge(s["dprod"], b + 1)
                nc.scalar.activation(Dm[:, u], Dm[:, u], ACT.Exp).then_inc(s["dexp"], 1)

            def place(b):
                act.wait_ge(s["o_done"], b + 1)
                act.wait_ge(s["vs_done"], b + 1)
                nc.scalar.copy(VO[:, bass.ds(b * 2, 2), :], misc[:, 1:3, :]).then_inc(s["vo_done"], 1)

            def iteration(i, u, first=False, last=False):
                b = i * 2 + u
                if not first:
                    place(b - 1)
                for h in range(HB):
                    act.wait_ge(s["b_done"], HB * b + h + 1)
                    at_least(act, s["pv_done"], HB * b + h - 3)
                    nc.scalar.activation(E[:, h % 4].rearrange("p a q -> p (a q)"), pb[:, h % 2, :], ACT.Exp).then_inc(s["exp_done"], 1)
                if not last:
                    decay(b + 1, 1 - u)

            decay(0, 0)
            iteration(0, 0, first=True)
            iteration(0, 1)
            with act.Fori(1, B // 2 - 1) as i:
                for u in range(2):
                    iteration(i, u)
            iteration(B // 2 - 1, 0)
            iteration(B // 2 - 1, 1, last=True)
            place(B - 1)

        @block.gpsimd
        def _(pool):
            pool.wait_ge(s["init"], 4)

            def prepare(b, u):
                at_least(pool, s["dmul_done"], HB * (b - 1))
                nc.gpsimd.tensor_tensor(Dm[:, u], w["c_pos"][:, None, :].to_broadcast([P, HB, P]),
                                        LD[:, bass.ds(b * HB, HB)][:, :, None].to_broadcast([P, HB, P]), ALU.mult).then_inc(s["dprod"], 1)
                at_least(pool, s["pv_done"], HB * (b - 1))
                nc.gpsimd.tensor_copy(Vs[:, u, :, :, 0:HD], VO[:, bass.ds(b * 2, 2), :].rearrange("p a (h d) -> p a h d", d=HD))\
                    .then_inc(s["vs_done"], 1)

            def iteration(i, u, last=False):
                b = i * 2 + u
                if not last:
                    prepare(b + 1, 1 - u)
                for h in range(HB):
                    if h == 0:
                        pool.wait_ge(s["dexp"], b + 1)
                    pool.wait_ge(s["exp_done"], HB * b + h + 1)
                    diag = E[:, h % 4, 0:4:3, :]
                    nc.gpsimd.tensor_tensor(diag, diag, Dm[:, u, h:h + 1, :].to_broadcast([P, 2, P]), ALU.mult).then_inc(s["dmul_done"], 1)

            prepare(0, 0)
            iteration(0, 0)
            iteration(0, 1)
            with pool.Fori(1, B // 2 - 1) as i:
                for u in range(2):
                    iteration(i, u)
            iteration(B // 2 - 1, 0)
            iteration(B // 2 - 1, 1, last=True)


def retention_finish(nc, k, tag, w, scr, VO):
    with ExitStack() as ctx:
        s = sems(nc, ctx, tag, "st mv mm dm sqd var ve rst ab gin0 gin1 za_done zb_done z_done y_done bias_done res_done nh")
        gin = (s["gin0"], s["gin1"])
        ps = lambda name, shape: ctx.enter_context(nc.psum_tensor(tag + name, shape, F32))
        sb = lambda name, shape, dt=F32: ctx.enter_context(nc.sbuf_tensor(tag + name, shape, dt))
        mu = ps("mu", [P, B])
        vr = ps("vr", [P, B])
        y = ps("y", [P, 2, GW])
        st = sb("st", [P, B, 6])
        mv = sb("mv", [P, B, 2])
        dm = sb("dm", [P, B])
        sq = sb("sq", [P, B])
        ve = sb("ve", [P, B])
        rs = sb("rs", [P, B])
        nh = sb("nh", [P, B])
        a = sb("a", [P, B])
        sh = sb("sh", [P, B])
        gate = sb("gate", [P, 2, GW])
        z = sb("z", [P, 3, GW])
        block = ctx.enter_context(nc.Block())
        seq = lambda ap: ap.rearrange("p (b t) -> p b t", b=2)

        @block.sync
        def _(sp):
            def load(g, slot):
                at_least(sp, s["z_done"], g - 1)
                nc.sync.dma_start(gate[:, slot, :], scr["gate"][:, bass.ds(g * GW, GW)]).then_inc(gin[slot], 16)
            for u in range(2):
                load(u, u)
            with sp.Fori(1, NG // 2) as i:
                for u in range(2):
                    load(i * 2 + u, u)

        @block.tensor
        def _(pe):
            pe.wait_ge(s["mv"], B)
            nc.tensor.matmul(mu[:], lhsT=w["c_avg"][:], rhs=mv[:, :, 0], start=True, stop=True).then_inc(s["mm"], 1)
            pe.wait_ge(s["var"], 1)
            nc.tensor.matmul(vr[:], lhsT=w["c_avg"][:], rhs=sq[:], start=True, stop=True).then_inc(s["mm"], 1)

            def out(g, slot):
                pe.wait_ge(s["z_done"], g + 1)
                at_least(pe, s["res_done"], g - 1)
                for i in range(GT):
                    m = nc.tensor.matmul(y[:, slot, i * P:(i + 1) * P], lhsT=z[:, 2, i * P:(i + 1) * P], rhs=w["c_wo"][:],
                                         start=True, stop=True, skip_group_check=True)
                m.then_inc(s["y_done"], 1)
            out(0, 0)
            out(1, 1)
            with pe.Fori(1, NG // 2) as i:
                for u in range(2):
                    out(i * 2 + u, u)

        @block.vector
        def _(dve):
            for b in range(B):
                nc.vector.bn_stats(st[:, b, :], VO[:, 2 * b:2 * b + 2, :].rearrange("p a q -> p (a q)")).then_inc(s["st"], 1)
            for b in range(B):
                dve.wait_ge(s["st"], b + 1)
                nc.vector.bn_aggr(mv[:, b, :], st[:, b, :]).then_inc(s["mv"], 1)
            dve.wait_ge(s["mm"], 1)
            dve.wait_ge(s["mv"], B)
            nc.vector.tensor_tensor(dm[:], mv[:, :, 0], mu[:], ALU.subtract).then_inc(s["dm"], 1)
            dve.wait_ge(s["dm"], 1)
            nc.vector.tensor_tensor(sq[:], dm[:], dm[:], ALU.mult).then_inc(s["sqd"], 1)
            dve.wait_ge(s["sqd"], 1)
            nc.vector.tensor_tensor(sq[:], sq[:], mv[:, :, 1], ALU.add).then_inc(s["var"], 1)
            dve.wait_ge(s["mm"], 2)
            nc.vector.tensor_scalar(ve[:], vr[:], LN_EPS, None, ALU.add).then_inc(s["ve"], 1)
            dve.wait_ge(s["rst"], 1)
            nc.vector.tensor_scalar(a[:], rs[:], w["c_gamma"][:, 0:1], 0.5, ALU.mult, ALU.mult).then_inc(s["ab"], 1)
            nc.vector.tensor_scalar(sh[:], dm[:], 0.0, w["c_beta"][:, 0:1], ALU.mult, ALU.add).then_inc(s["ab"], 1)
            dve.wait_ge(s["ab"], 2)
            nc.vector.tensor_tensor(dm[:], mu[:], a[:], ALU.mult).then_inc(s["ab"], 1)
            dve.wait_ge(s["ab"], 3)
            nc.vector.scalar_tensor_tensor(out=sh[:], in0=sh[:], scalar=0.5, in1=dm[:], op0=ALU.mult, op1=ALU.subtract).then_inc(s["ab"], 1)
            dve.wait_ge(s["ab"], 4)

            def scale(g):
                at_least(dve, s["zb_done"], g)
                nc.vector.tensor_tensor(seq(z[:, 0, :]), VO[:, bass.ds(g * GT, GT), :].rearrange("p (b a) q -> p b (a q)", b=2),
                                        a[:, bass.ds(g * 2, 2)][:, :, None].to_broadcast([P, 2, T]), ALU.mult).then_inc(s["za_done"], 1)

            def apply(g, slot, i):
                dve.wait_ge(s["zb_done"], g + 1)
                dve.wait_ge(gin[slot], 16 * (i + 1))
                at_least(dve, s["y_done"], g)
                nc.vector.tensor_tensor(z[:, 2, :], z[:, 1, :], gate[:, slot, :], ALU.mult).then_inc(s["z_done"], 1)

            def residual(g, slot):
                dve.wait_ge(s["y_done"], g + 1)
                dve.wait_ge(s["bias_done"], g + 1)
                xg = k.X[:, bass.ds(g * GT, GT), :].rearrange("p a b -> p (a b)")
                nc.vector.tensor_tensor(xg, y[:, slot, :], xg, ALU.add).then_inc(s["res_done"], 1)
            scale(0)
            apply(0, 0, 0)
            scale(1)
            apply(1, 1, 0)
            residual(0, 0)
            with dve.Fori(1, NG // 2) as i:
                for u in range(2):
                    g = i * 2 + u
                    scale(g)
                    apply(g, u, i)
                    residual(g - 1, 1 - u)
            residual(NG - 1, 1)
            dve.wait_ge(s["res_done"], NG)

        @block.gpsimd
        def _(pool):
            nc.gpsimd.memset(nh[:], -0.5).then_inc(s["nh"], 1)
            pool.wait_ge(s["nh"], 1)
            pool.wait_ge(s["ve"], 1)
            nc.gpsimd.tensor_tensor(rs[:], ve[:], nh[:], ALU.pow).then_inc(s["rst"], 1)
            pool.wait_ge(s["ab"], 4)

            def one(g):
                xg = k.X[:, bass.ds(g * GT, GT), :]
                nc.gpsimd.tensor_tensor(xg, xg, w["c_bo"][:, None, :].to_broadcast([P, GT, D]), ALU.add).then_inc(s["bias_done"], 1)
                pool.wait_ge(s["za_done"], g + 1)
                at_least(pool, s["z_done"], g)
                nc.gpsimd.tensor_tensor(seq(z[:, 1, :]), seq(z[:, 0, :]), sh[:, bass.ds(g * 2, 2)][:, :, None].to_broadcast([P, 2, T]),
                                        ALU.add).then_inc(s["zb_done"], 1)
            one(0)
            with pool.Fori(1, NG) as g:
                one(g)


def retention_scratch(nc):
    d = lambda name, shape, dt=F32: nc.dram_tensor(name, shape, dt).ap()
    return {"q": d("q_d", [3, P, TOK], F16), "k": d("k_d", [3, P, TOK], F16), "gate": d("gate_d", [P, TOK]),
            "ld": d("ld_d", [B, HB]), "aug": d("aug_d", [4, B, HB, P], F16)}


def stage_wkv(nc, k, tag, w):
    import math
    eps = math.exp(-1 / 12)
    EPS = {"r": eps / 2.0, "k": eps + 0.3 * 1 / 11, "v": eps}
    LO, HI = math.exp(-20.0), math.exp(10.0)
    NM = w["b_wk"].shape[1] // P
    MID = NM // 2
    with ExitStack() as ctx:
        s = sems(nc, ctx, tag, "ln_tick ln_rstd turned xT_ready mixed k_done kw_done v_done r_done y_done "
                 "eu_done e_done th_done act_tick y0_done head tail b_done a_done t_done bias_done res_done "
                 "pre_v pre_p pre_dma")
        ps = lambda name, shape: ctx.enter_context(nc.psum_tensor(tag + name, shape, F32))
        sb = lambda name, shape, dt=F32: ctx.enter_context(nc.sbuf_tensor(tag + name, shape, dt))
        turn = ps("turn", [P, GW])
        kp = ps("kp", [P, 2, GW])
        vp = ps("vp", [P, 2, GW])
        rp = ps("rp", [P, 2, GW])
        y = ps("y", [P, GW])
        xT = sb("xT", [P, 2, T + 1])
        part = sb("part", [P, 3, GW])
        mix = sb("mix", [P, 2, 3, GW])
        NS = 4
        ee = sb("ee", [P, NS, 2, GW])
        ev = sb("ev", [P, 2, GW])
        euv = sb("euv", [P, NS, GW])
        ce = sb("ce", [P, NS, 2, T + 1])
        cev = sb("cev", [P, NS, 2, T + 1])
        lnb = sb("lnb", [P, GW])
        y0 = sb("y0", [P, NS, GW])
        rec = sb("rec", [P, GW])
        num = sb("num", [P, GW])
        wkv = sb("wkv", [P, 2, GW])
        th = sb("th", [P, 2, NM, GW])
        ones = sb("ones", [P, T])
        ub = sb("ub", [P, NM])
        hbr = sb("hbr", [P, NM])
        wos = sb("wos", [P, NM, D])
        nw = sb("nw", [1, NM * P])
        nwp = sb("nwp", [1, 3, NM * P], BF16)
        decay = sb("decay", [P, NM * P], BF16)
        left = sb("left", [P, 2, T], BF16)
        lefti = sb("lefti", [P, 2, T])
        block = ctx.enter_context(nc.Block())
        seq = lambda ap: ap.rearrange("p (b t) -> p b t", b=2)

        @block.sync
        def _(sp):
            sp.wait_ge(s["pre_v"], 9)
            sp.wait_ge(s["pre_p"], 3)
            for i in range(3):
                nc.sync.dma_start(decay[i:i + 1, :], nwp[0:1, i, :]).then_inc(s["pre_dma"], 16)
            sp.wait_ge(s["pre_dma"], 48)

        @block.vector
        def _(dve):
            nc.vector.memset(ones[:], 1.0).then_inc(s["pre_v"], 1)
            nc.vector.tensor_tensor(ub[:], w["b_u"][:], w["b_bk"][:], ALU.add).then_inc(s["pre_v"], 1)
            nc.vector.tensor_scalar(hbr[:], w["b_br"][:], 0.5, None, ALU.mult).then_inc(s["pre_v"], 1)
            nc.vector.tensor_scalar(wos[:], w["b_wo"][:], -0.5, None, ALU.mult).then_inc(s["pre_v"], 1)
            nc.vector.tensor_scalar(nw[:], w["b_td"][0:1, :], 0.0, -1.0, ALU.max, ALU.mult).then_inc(s["pre_v"], 1)
            dve.wait_ge(s["pre_v"], 5)
            nc.vector.tensor_copy(nwp[:, 0, :], nw[:]).then_inc(s["pre_v"], 1)
            dve.wait_ge(s["pre_v"], 6)
            nc.vector.tensor_tensor(nw[:], nw[:], nwp[:, 0, :], ALU.subtract).then_inc(s["pre_v"], 1)
            dve.wait_ge(s["pre_v"], 7)
            nc.vector.tensor_copy(nwp[:, 1, :], nw[:]).then_inc(s["pre_v"], 1)
            dve.wait_ge(s["pre_v"], 8)
            nc.vector.tensor_tensor(nwp[:, 2, :], nw[:], nwp[:, 1, :], ALU.subtract).then_inc(s["pre_v"], 1)
            dve.wait_ge(s["pre_v"], 9)
            dve.wait_ge(s["pre_p"], 3)

            def ln(g, slot, wait):
                def xn_free():
                    if wait:
                        dve.wait_ge(s["turned"], g - 1)
                layernorm_dve(k, s, dve, g, slot, xn_free)

            def mixes(g, slot, wait):
                dve.wait_ge(s["xT_ready"], g + 1)
                if wait:
                    dve.wait_ge(s["v_done"], (g - 1) * NM)
                    dve.wait_ge(s["r_done"], (g - 1) * NM)
                for i, n in enumerate("rkv"):
                    nc.vector.scalar_tensor_tensor(out=seq(mix[:, slot, i, :]), in0=xT[:, :, 0:T], scalar=EPS[n],
                                                   in1=seq(part[:, i, :]), op0=ALU.mult, op1=ALU.add).then_inc(s["mixed"], 1)

            def head(n, m, later):
                q = m % NS
                dve.wait_ge(s["e_done"], n + 1)
                if later:
                    dve.wait_ge(s["a_done"], n - NS + 1)
                nc.vector.tensor_scalar(ee[:, q, :, :], ee[:, q, :, :], LO, HI, ALU.max, ALU.min).then_inc(s["head"], 1)
                dve.wait_ge(s["v_done"], n + 1)
                dve.wait_ge(s["head"], 7 * n + 1)
                nc.vector.scalar_tensor_tensor(out=ev[:, m % 2, :], in0=vp[:, m % 2, :], scalar=w["b_bv"][:, m:m + 1],
                                               in1=ee[:, q, 0, :], op0=ALU.add, op1=ALU.mult).then_inc(s["head"], 1)
                nc.vector.scalar_tensor_tensor(out=euv[:, q, :], in0=vp[:, m % 2, :], scalar=w["b_bv"][:, m:m + 1],
                                               in1=ee[:, q, 1, :], op0=ALU.add, op1=ALU.mult).then_inc(s["head"], 1)
                for b in range(2):
                    nc.vector.tensor_tensor_scan(ce[:, q, b, 1:T + 1], ones[:], ee[:, q, 0, b * T:(b + 1) * T], 0.0,
                                                 ALU.mult, ALU.add).then_inc(s["head"], 1)
                dve.wait_ge(s["head"], 7 * n + 2)
                for b in range(2):
                    nc.vector.tensor_tensor_scan(cev[:, q, b, 1:T + 1], ones[:], ev[:, m % 2, b * T:(b + 1) * T], 0.0,
                                                 ALU.mult, ALU.add).then_inc(s["head"], 1)

            def tail(n, m, slot, later):
                q = m % NS
                dve.wait_ge(s["t_done"], n + 1)
                nc.vector.scalar_tensor_tensor(out=rec[:], in0=ee[:, q, 1, :], scalar=2.0, in1=y0[:, q, :],
                                               op0=ALU.subtract, op1=ALU.mult).then_inc(s["tail"], 1)
                dve.wait_ge(s["a_done"], n + 1)
                nc.vector.scalar_tensor_tensor(out=num[:], in0=th[:, slot, m, :], scalar=1.0, in1=euv[:, q, :],
                                               op0=ALU.add, op1=ALU.mult).then_inc(s["tail"], 1)
                dve.wait_ge(s["tail"], 3 * n + 2)
                if later:
                    dve.wait_ge(s["y_done"], n - 1)
                nc.vector.tensor_tensor(wkv[:, m % 2, :], num[:], rec[:], ALU.mult).then_inc(s["tail"], 1)
                dve.wait_ge(s["tail"], 3 * n + 3)

            def residual(g):
                dve.wait_ge(s["y_done"], (g + 1) * NM)
                dve.wait_ge(s["bias_done"], g + 1)
                xg = k.X[:, bass.ds(g * GT, GT), :].rearrange("p a b -> p (a b)")
                nc.vector.tensor_tensor(xg, y[:], xg, ALU.add).then_inc(s["res_done"], 1)

            def group(g, u, first, early):
                for m in range(NM):
                    n = g * NM + m
                    if m == 0:
                        ln(g + 1, 1 - u, not first)
                    if m == 2:
                        mixes(g + 1, 1 - u, not first)
                    if m == 4 and not first:
                        residual(g - 1)
                    if not first or m >= 3:
                        tail(n - 3, (m - 3) % NM, u if m >= 3 else 1 - u, not first or m >= 5)
                    head(n, m, not first or m >= NS)

            ln(0, 0, False)
            mixes(0, 0, False)
            group(0, 0, True, True)
            group(1, 1, False, True)
            with dve.Fori(1, NG // 2) as i:
                for u in range(2):
                    group(i * 2 + u, u, False, False)
            tail(NG * NM - 3, NM - 3, 1, True)
            tail(NG * NM - 2, NM - 2, 1, True)
            tail(NG * NM - 1, NM - 1, 1, True)
            residual(NG - 1)
            dve.wait_ge(s["res_done"], NG)

        @block.gpsimd
        def _(pool):
            nc.gpsimd.memset(decay[:], 0.0).then_inc(s["pre_p"], 1)
            nc.gpsimd.memset(ce[:, :, :, 0:1], 0.0)
            nc.gpsimd.memset(xT[:, :, 0:1], 0.0)
            for i in range(3):
                nc.gpsimd.memset(seq(part[:, i, :])[:, :, T - 1:T], 0.0)
            nc.gpsimd.memset(cev[:, :, :, 0:1], 0.0).then_inc(s["pre_p"], 1)
            nc.gpsimd.iota(lefti[:], pattern=[[0, 2], [-1, T]], base=T - 1, channel_multiplier=0,
                           allow_small_or_imprecise_dtypes=True).then_inc(s["pre_p"], 1)
            pool.wait_ge(s["pre_p"], 3)
            nc.gpsimd.tensor_copy(left[:], lefti[:]).then_inc(s["pre_p"], 1)
            layernorm_pool(k, s, pool, 0)

            def sums(n, m):
                q = m % NS
                pool.wait_ge(s["head"], 7 * n + 7)
                nc.gpsimd.tensor_tensor(seq(ee[:, q, 1, :]), ce[:, q, :, 0:T], seq(ee[:, q, 1, :]), ALU.add).then_inc(s["b_done"], 1)
                nc.gpsimd.tensor_tensor(seq(euv[:, q, :]), cev[:, q, :, 0:T], seq(euv[:, q, :]), ALU.add).then_inc(s["a_done"], 1)

            def prod(n, m):
                q = m % NS
                pool.wait_ge(s["y0_done"], n + 1)
                nc.gpsimd.tensor_tensor(ee[:, q, 1, :], ee[:, q, 1, :], y0[:, q, :], ALU.mult).then_inc(s["t_done"], 1)

            def group(g, first):
                for m in range(NM):
                    n = g * NM + m
                    if m == 0:
                        layernorm_pool(k, s, pool, g + 1)
                        pool.wait_ge(s["ln_tick"], (g + 1) * LN_TICKS)
                        xg = k.X[:, bass.ds(g * GT, GT), :]
                        nc.gpsimd.tensor_tensor(xg, xg, w["b_bo"][:, None, :].to_broadcast([P, GT, D]),
                                                ALU.add).then_inc(s["bias_done"], 1)
                    if not first or m >= 2:
                        prod(n - 2, (m - 2) % NM)
                    sums(n, m)
            group(0, True)
            with pool.Fori(1, NG) as g:
                group(g, False)
            prod(NG * NM - 2, NM - 2)
            prod(NG * NM - 1, NM - 1)

        @block.tensor
        def _(pe):
            pe.wait_ge(s["pre_p"], 4)
            pe.wait_ge(s["pre_v"], 9)
            pe.wait_ge(s["pre_dma"], 48)

            def turn_in(g, slot, wait):
                pe.wait_ge(s["ln_tick"], (g + 1) * LN_TICKS)
                if wait:
                    pe.wait_ge(s["xT_ready"], g)
                for i in range(GT):
                    mm = nc.tensor.transpose(turn[:, i * P:(i + 1) * P], k.xn[:, slot, i, :], k.ident[:])
                mm.then_inc(s["turned"], 1)

            def gate(g, slot, wait):
                pe.wait_ge(s["mixed"], 3 * g + 1)
                for m in range(NM):
                    if wait or m >= 2:
                        pe.wait_ge(s["th_done"], g * NM + m - 1)
                    nc.tensor.matmul(rp[:, m % 2, :], lhsT=w["b_wr"][:, m * P:(m + 1) * P], rhs=mix[:, slot, 0, :],
                                     start=True, stop=True).then_inc(s["r_done"], 1)

            def kv(n, m, slot, later):
                q = m % 2
                if later:
                    pe.wait_ge(s["e_done"], n - 1)
                nc.tensor.matmul(kp[:, q, :], lhsT=w["b_wk"][:, m * P:(m + 1) * P], rhs=mix[:, slot, 1, :],
                                 start=True, stop=True, skip_group_check=True).then_inc(s["k_done"], 1)
                if later:
                    pe.wait_ge(s["head"], 7 * (n - 2) + 3)
                nc.tensor.matmul(vp[:, q, :], lhsT=w["b_wv"][:, m * P:(m + 1) * P], rhs=mix[:, slot, 2, :],
                                 start=True, stop=True).then_inc(s["v_done"], 1)

            def add_decay(n, m):
                pe.wait_ge(s["eu_done"], n + 1)
                nc.tensor.matmul(kp[:, m % 2, :], lhsT=decay[:, m * P:(m + 1) * P], rhs=left[:].rearrange("p b t -> p (b t)"),
                                 start=False, stop=True, skip_group_check=True).then_inc(s["kw_done"], 1)

            def out(n, m, g_free):
                pe.wait_ge(s["tail"], 3 * (n + 1))
                if g_free is not None:
                    pe.wait_ge(s["res_done"], g_free)
                for i in range(GT):
                    mm = nc.tensor.matmul(y[:, i * P:(i + 1) * P], lhsT=wkv[:, m % 2, i * P:(i + 1) * P],
                                          rhs=wos[:, m, :], start=(m == 0 and i == 0), stop=(m == NM - 1),
                                          skip_group_check=True)
                mm.then_inc(s["y_done"], 1)

            def group(g, u, first):
                for m in range(NM):
                    n = g * NM + m
                    if m == 0:
                        pe.wait_ge(s["mixed"], 3 * (g + 1))
                    kv(n, m, u, not first or m >= 2)
                    if m == MID:
                        gate(g + 1, 1 - u, True)
                    if not first or m >= 1:
                        add_decay(n - 1, (m - 1) % NM)
                    if not first or m >= 4:
                        out(n - 4, (m - 4) % NM, g if m == 4 and not first else None)
                    if m == 0:
                        turn_in(g + 1, 1 - u, True)

            turn_in(0, 0, False)
            gate(0, 0, False)
            group(0, 0, True)
            group(1, 1, False)
            with pe.Fori(1, NG // 2) as i:
                for u in range(2):
                    group(i * 2 + u, u, False)
            N = NG * NM
            add_decay(N - 1, NM - 1)
            for j in (4, 3, 2, 1):
                out(N - j, NM - j, None)

        @block.scalar
        def _(act):
            act.wait_ge(s["pre_v"], 3)
            act.wait_ge(s["pre_p"], 2)

            def evac(g, wait):
                act.wait_ge(s["turned"], g + 1)
                if wait:
                    act.wait_ge(s["mixed"], 3 * g)
                nc.scalar.copy(xT[:, :, 1:T + 1], seq(turn[:])).then_inc(s["act_tick"], 1)
                for i, n in enumerate("rkv"):
                    mm = nc.scalar.activation(seq(part[:, i, :])[:, :, 0:T - 1], seq(turn[:])[:, :, 1:T], ACT.Copy,
                                              scale=1.0 - EPS[n])
                mm.then_inc(s["xT_ready"], 1)

            def gate(g, slot, wait):
                for m in range(NM):
                    act.wait_ge(s["r_done"], g * NM + m + 1)
                    if wait and m == 0:
                        act.wait_ge(s["tail"], 3 * (g - 1) * NM)
                    nc.scalar.activation(th[:, slot, m, :], rp[:, m % 2, :], ACT.Tanh, bias=hbr[:, m:m + 1],
                                         scale=0.5).then_inc(s["th_done"], 1)
                nc.scalar.preload_act_table_set("natural_log_exp_and_others")

            def eu(n, m, later):
                q = m % NS
                act.wait_ge(s["k_done"], n + 1)
                if later:
                    act.wait_ge(s["tail"], 3 * (n - NS + 1))
                nc.scalar.activation(ee[:, q, 1, :], kp[:, m % 2, :], ACT.Exp, bias=ub[:, m:m + 1]).then_inc(s["eu_done"], 1)

            def e(n, m):
                q = m % NS
                act.wait_ge(s["kw_done"], n + 1)
                nc.scalar.activation(ee[:, q, 0, :], kp[:, m % 2, :], ACT.Exp, bias=w["b_bk"][:, m:m + 1]).then_inc(s["e_done"], 1)

            def recip(n, m, ticks, later):
                act.wait_ge(s["b_done"], n + 1)
                if later:
                    act.wait_ge(s["y0_done"], n)
                nc.scalar.activation(lnb[:], ee[:, m % NS, 1, :], ACT.Ln).then_inc(s["act_tick"], 1)
                act.wait_ge(s["act_tick"], ticks)
                nc.scalar.activation(y0[:, m % NS, :], lnb[:], ACT.Exp, scale=-1.0).then_inc(s["y0_done"], 1)

            def group(g, u, first):
                for m in range(NM):
                    n = g * NM + m
                    if m == 1:
                        evac(g + 1, True)
                    if m == MID:
                        gate(g + 1, 1 - u, not first)
                    if not first or m >= 1:
                        e(n - 1, (m - 1) % NM)
                    eu(n, m, not first or m >= NS)
                    if not first or m >= 2:
                        recip(n - 2, (m - 2) % NM, n - 1 + g + (2 if m >= 1 else 1), not first or m >= 3)

            evac(0, False)
            gate(0, 0, False)
            group(0, 0, True)
            group(1, 1, False)
            with act.Fori(1, NG // 2) as i:
                for u in range(2):
                    group(i * 2 + u, u, False)
            N = NG * NM
            e(N - 1, NM - 1)
            for j in (2, 1):
                recip(N - j, NM - j, N - j + 1 + NG + 1, True)


NE = 8
CAP = 2 * T // NE + 1
ROUNDS = -(-CAP // 8)
NJH = 4
QB = 4
NQ = B // QB
SL = NE * CAP
NCH = 5
CH = SL // NCH
QW = QB * CAP
RB = P // NE


def stage_route(nc, k, tag, w, xn_d, val_d, idx_d):
    with ExitStack() as ctx:
        s = sems(nc, ctx, tag, "ln_tick ln_rstd turned xT_ready logits stored0 stored1 soft exp_done rows work top0 top1 out")
        ps = lambda name, shape: ctx.enter_context(nc.psum_tensor(tag + name, shape, F32))
        sb = lambda name, shape, dt=F32: ctx.enter_context(nc.sbuf_tensor(tag + name, shape, dt))
        turn = ps("turn", [P, 2, GW])
        lg = ps("lg", [P, TILES, NE])
        rows = ps("rows", [P, 2, T])
        xT = sb("xT", [P, 2, GW])
        mx = sb("mx", [P, TILES])
        dl = sb("dl", [P, TILES, NE])
        ex = sb("ex", [P, TILES, NE])
        sm = sb("sm", [P, TILES])
        rs = sb("rs", [P, TILES])
        sc = sb("sc", [P, 2, B, NE])
        work = sb("work", [P, 2, T])
        val = sb("val", [P, 2, ROUNDS * 8])
        idx = sb("idx", [P, 2, ROUNDS * 8], U32)
        idf = sb("idf", [P, 2, ROUNDS * 8])
        stored = (s["stored0"], s["stored1"])
        block = ctx.enter_context(nc.Block())

        @block.sync
        def _(sp):
            with sp.Fori(0, NG // 2) as i:
                for u in range(2):
                    g = i * 2 + u
                    sp.wait_ge(s["ln_tick"], (g + 1) * LN_TICKS)
                    nc.sync.dma_start(xn_d[bass.ds(g * GT, GT), :, :].rearrange("a p d -> p a d"),
                                      k.xn[:, u, :, :]).then_inc(stored[u], 16)
            for u in range(2):
                sp.wait_ge(stored[u], 16 * (NG // 2))
            for r, top in enumerate((s["top0"], s["top1"])):
                sp.wait_ge(top, 3 * ROUNDS)
                nc.sync.dma_start(val_d[r * P:(r + 1) * P, :], val[:, r, 0:CAP]).then_inc(s["out"], 16)
                nc.sync.dma_start(idx_d[r * P:(r + 1) * P, :], idf[:, r, 0:CAP]).then_inc(s["out"], 16)
            sp.wait_ge(s["out"], 64)

        @block.vector
        def _(dve):
            def ln(g, slot, wait):
                def xn_free():
                    if wait:
                        dve.wait_ge(s["turned"], g - 1)
                        dve.wait_ge(stored[slot], (g - slot) * 8)
                layernorm_dve(k, s, dve, g, slot, xn_free)
            ln(0, 0, False)
            ln(1, 1, False)
            with dve.Fori(1, NG // 2) as i:
                for u in range(2):
                    ln(i * 2 + u, u, True)
            bc = lambda v: v[:, :, None].to_broadcast([P, TILES, NE])
            dve.wait_ge(s["logits"], NG)
            nc.vector.tensor_reduce(mx[:], lg[:], AX.X, ALU.max).then_inc(s["soft"], 1)
            dve.wait_ge(s["soft"], 1)
            nc.vector.tensor_tensor(dl[:], lg[:], bc(mx), ALU.subtract).then_inc(s["soft"], 1)
            dve.wait_ge(s["exp_done"], 1)
            nc.vector.tensor_reduce(sm[:], ex[:], AX.X, ALU.add).then_inc(s["soft"], 1)
            dve.wait_ge(s["soft"], 3)
            nc.vector.reciprocal(rs[:], sm[:]).then_inc(s["soft"], 1)
            dve.wait_ge(s["soft"], 4)
            nc.vector.tensor_tensor(sc[:].rearrange("p h b e -> p b h e"), ex[:].rearrange("p (b h) e -> p b h e", h=2),
                                    rs[:].rearrange("p (b h) -> p b h", h=2)[:, :, :, None].to_broadcast([P, B, 2, NE]),
                                    ALU.mult).then_inc(s["soft"], 1)
            dve.wait_ge(s["rows"], 1)
            nc.vector.tensor_copy(work[:], rows[:]).then_inc(s["work"], 1)
            dve.wait_ge(s["work"], 1)
            for n in range(ROUNDS):
                eight = slice(8 * n, 8 * n + 8)
                for r, top in enumerate((s["top0"], s["top1"])):
                    if n:
                        dve.wait_ge(top, 3 * n)
                    nc.vector.max(val[:, r, eight], work[:, r, :]).then_inc(top, 1)
                for r, top in enumerate((s["top0"], s["top1"])):
                    dve.wait_ge(top, 3 * n + 1)
                    nc.vector.max_index(idx[:, r, eight], val[:, r, eight], work[:, r, :]).then_inc(top, 1)
                for r, top in enumerate((s["top0"], s["top1"])):
                    if n < ROUNDS - 1:
                        dve.wait_ge(top, 3 * n + 2)
                        nc.vector.match_replace(work[:, r, :], val[:, r, eight], work[:, r, :], -1.0).then_inc(top, 1)
            for r, top in enumerate((s["top0"], s["top1"])):
                dve.wait_ge(top, 3 * ROUNDS - 1)
                nc.vector.tensor_copy(idf[:, r, :], idx[:, r, :]).then_inc(top, 1)

        @block.gpsimd
        def _(pool):
            with pool.Fori(0, NG) as g:
                layernorm_pool(k, s, pool, g)

        @block.tensor
        def _(pe):
            def turn_in(g, slot, wait):
                pe.wait_ge(s["ln_tick"], (g + 1) * LN_TICKS)
                if wait:
                    pe.wait_ge(s["xT_ready"], g - 1)
                for i in range(GT):
                    mm = nc.tensor.transpose(turn[:, slot, i * P:(i + 1) * P], k.xn[:, slot, i, :], k.ident[:])
                mm.then_inc(s["turned"], 1)

            def logits(g, slot):
                pe.wait_ge(s["xT_ready"], g + 1)
                for i in range(GT):
                    mm = nc.tensor.matmul(lg[:, g * GT + i, :], lhsT=xT[:, slot, i * P:(i + 1) * P], rhs=w["m_router"][:],
                                          start=True, stop=True)
                mm.then_inc(s["logits"], 1)
            turn_in(0, 0, False)
            turn_in(1, 1, False)
            with pe.Fori(0, NG // 2 - 1) as i:
                for u in range(2):
                    g = i * 2 + u
                    logits(g, u)
                    turn_in(g + 2, u, True)
            logits(NG - 2, 0)
            logits(NG - 1, 1)
            pe.wait_ge(s["soft"], 5)
            for r in range(2):
                for h in range(2):
                    mm = nc.tensor.transpose(rows[:, r, h * P:(h + 1) * P],
                                             sc[:, h, r * RB:(r + 1) * RB, :].rearrange("p b e -> p (b e)"), k.ident[:])
            mm.then_inc(s["rows"], 1)

        @block.scalar
        def _(act):
            def evac(g, slot, wait):
                act.wait_ge(s["turned"], g + 1)
                if wait:
                    act.wait_ge(s["logits"], g - 1)
                nc.scalar.copy(xT[:, slot, :], turn[:, slot, :]).then_inc(s["xT_ready"], 1)
            evac(0, 0, False)
            evac(1, 1, False)
            with act.Fori(1, NG // 2) as i:
                for u in range(2):
                    evac(i * 2 + u, u, True)
            act.wait_ge(s["soft"], 2)
            nc.scalar.activation(ex[:], dl[:], ACT.Exp).then_inc(s["exp_done"], 1)


def stage_experts(nc, k, tag, w, xn_d, val_d, idx_d):
    with ExitStack() as ctx:
        s = sems(nc, ctx, tag, "const slots cols_ps cols stage0 stage1 onehot misc misc_free up_done gelu_done "
                 "down_done y_done sel_done")
        ps = lambda name, shape: ctx.enter_context(nc.psum_tensor(tag + name, shape, F32))
        sb = lambda name, shape, dt=F32: ctx.enter_context(nc.sbuf_tensor(tag + name, shape, dt))
        misc = ps("misc", [P, 4, 512])
        hid = ps("hid", [P, 2, 512])
        yp = ps("yp", [P, 2, 512])
        tok = sb("tok", [P, 2])
        steps = sb("steps", [P, T])
        both = sb("both", [B, 2, SL])
        cols = sb("cols", [CH, 2, NCH, B])
        xs = sb("xs", [P, 2, 2 * QB, D])
        ir = sb("ir", [P, 2, QB, SL])
        oh = sb("oh", [P, 2, 2, SL])
        xg = sb("xg", [P, 2, NE, QB, CAP])
        hT = sb("hT", [P, 2, NJH, QW])
        yT = sb("yT", [P, QB, NE, CAP])
        ys = sb("ys", [CH, 2, NCH, D])
        sel = sb("sel", [CH, QB, NCH, T])
        stage = (s["stage0"], s["stage1"])
        block = ctx.enter_context(nc.Block())
        UNITS = 8 + 3 * QB
        first_unit = lambda q: q * UNITS + 8
        tail_order = [("t", 0, 0), ("t", 0, 1), ("t", 1, 0), ("t", 1, 1), ("o", 0, 0), ("t", 2, 0), ("t", 2, 1),
                      ("o", 1, 0), ("t", 3, 0), ("t", 3, 1), ("o", 2, 0), ("o", 3, 0)]
        split = ((0, 3), (3, 5))

        @block.sync
        def _(sp):
            for i, d in enumerate((val_d, idx_d)):
                nc.sync.dma_start(both[:, i, :], d.rearrange("(b e) c -> b (e c)", e=NE)).then_inc(s["slots"], 16)

            def load(q, slot, wait):
                if wait == 2:
                    sp.wait_ge(s["misc"], 8)
                if wait > 2:
                    sp.wait_ge(s["misc"], first_unit(q - 3) + 8)
                nc.sync.dma_start(xs[:, slot, :, :], xn_d[bass.ds(q * 2 * QB, 2 * QB), :, :].rearrange("a p d -> p a d"))\
                    .then_inc(stage[slot], 16)
                nc.sync.dma_start(ir[:, slot, :, :].rearrange("p b s -> p (b s)"),
                                  idx_d[bass.ds(q * QB * NE, QB * NE), :].rearrange("r c -> (r c)").partition_broadcast(P))\
                    .then_inc(stage[slot], 16)
            for q in range(4):
                load(q, q % 2, q)
            with sp.Fori(2, NQ // 2) as i:
                for u in range(2):
                    load(i * 2 + u, u, 4)
            sp.wait_ge(s["slots"], 32)
            for u in range(2):
                sp.wait_ge(stage[u], 32 * (NQ // 2))

        @block.gpsimd
        def _(pool):
            nc.gpsimd.iota(tok[:], pattern=[[P, 2]], base=0, channel_multiplier=1,
                           allow_small_or_imprecise_dtypes=True).then_inc(s["const"], 1)
            nc.gpsimd.iota(steps[:], pattern=[[1, T]], base=0, channel_multiplier=0,
                           allow_small_or_imprecise_dtypes=True).then_inc(s["const"], 1)

        @block.vector
        def _(dve):
            dve.wait_ge(s["const"], 2)
            dve.wait_ge(s["cols_ps"], 1)
            nc.vector.tensor_copy(cols[:].rearrange("p i c b -> p (i c b)"), misc[0:CH, 0, 0:2 * NCH * B]).then_inc(s["cols"], 1)
            dve.wait_ge(s["cols"], 1)

            def onehot(q, slot, b):
                if b == 0:
                    dve.wait_ge(stage[slot], 16 * (q - slot) + 32)
                for h in range(2):
                    nc.vector.tensor_scalar(oh[:, b % 2, h, :], ir[:, slot, b, :], tok[:, h:h + 1], None,
                                            ALU.is_equal).then_inc(s["onehot"], 1)

            def take(slot, unit, number):
                b, er = unit // 2, unit % 2
                dve.wait_ge(s["misc"], number + 1)
                n = NE // 2
                nc.vector.tensor_copy(xg[:, slot, er * n:(er + 1) * n, b, :],
                                      misc[:, unit % 4, 0:n * CAP]
                                      .rearrange("p (e c) -> p e c", e=n)).then_inc(s["misc_free"], 1)

            def y_out(q, e):
                dve.wait_ge(s["down_done"], q * NE + e + 1)
                nc.vector.tensor_scalar(yT[:, :, e, :], yp[:, e % 2, 0:QW].rearrange("p (b c) -> p b c", b=QB),
                                        w["m_b2"][:, e:e + 1], None, ALU.add).then_inc(s["y_done"], 1)

            def select(q, n):
                b, c = n // NCH, n % NCH
                nc.vector.tensor_scalar(sel[:, b, c, :], steps[0:CH, :], cols[:, 1, c, bass.ds(q * QB + b, 1)],
                                        cols[:, 0, c, bass.ds(q * QB + b, 1)], ALU.is_equal, ALU.mult).then_inc(s["sel_done"], 1)

            def tail(q, number):
                for i, (kind, b, part) in enumerate(tail_order):
                    bank = (8 + i) % 4
                    dve.wait_ge(s["misc"], number + i + 1)
                    if kind == "t":
                        c0, c1 = split[part]
                        nc.vector.tensor_copy(ys[:, b % 2, c0:c1, :].rearrange("p c d -> p (c d)"),
                                              misc[0:CH, bank, 0:(c1 - c0) * D]).then_inc(s["misc_free"], 1)
                    else:
                        xb = k.X[:, bass.ds((q * QB + b) * 2, 2), :].rearrange("p a d -> p (a d)")
                        nc.vector.tensor_tensor(xb, misc[:, bank, 0:2 * D], xb, ALU.add).then_inc(s["misc_free"], 1)

            def quad(q, u, first, last):
                number = first_unit(q)
                if not last:
                    onehot(q + 1, 1 - u, 0)
                for e in range(NE):
                    if not last and e % 2 == 0 and e // 2 + 1 < QB:
                        onehot(q + 1, 1 - u, e // 2 + 1)
                    if not last:
                        take(1 - u, e, number + e)
                    for m in range(QB * NCH * e // NE, QB * NCH * (e + 1) // NE):
                        select(q, m)
                    y_out(q, e)
                tail(q, number if last else number + 8)

            onehot(0, 0, 0)
            for unit in range(8):
                if unit % 2 == 0 and unit // 2 + 1 < QB:
                    onehot(0, 0, unit // 2 + 1)
                take(0, unit, unit)
            quad(0, 0, True, False)
            quad(1, 1, False, False)
            with dve.Fori(1, NQ // 2 - 1) as i:
                for u in range(2):
                    quad(i * 2 + u, u, False, False)
            quad(NQ - 2, 0, False, False)
            quad(NQ - 1, 1, False, True)
            dve.wait_ge(s["misc_free"], 8 + NQ * UNITS - 8)

        @block.tensor
        def _(pe):
            pe.wait_ge(s["slots"], 32)
            for i in range(2):
                for c in range(NCH):
                    at = (i * NCH + c) * B
                    mm = nc.tensor.transpose(misc[0:CH, 0, at:at + B], both[:, i, c * CH:(c + 1) * CH], k.ident[0:B, 0:B])
            mm.then_inc(s["cols_ps"], 1)
            pe.wait_ge(s["cols"], 1)

            def gather(q, slot, unit, number, later):
                b, er = unit // 2, unit % 2
                n = NE // 2 * CAP
                if unit == 0:
                    pe.wait_ge(stage[slot], 16 * (q - slot) + 32)
                pe.wait_ge(s["onehot"], 2 * (QB * q + b + 1))
                if later:
                    pe.wait_ge(s["misc_free"], number - 3)
                for h in range(2):
                    mm = nc.tensor.matmul(misc[:, unit % 4, 0:n], lhsT=xs[:, slot, 2 * b + h, :],
                                          rhs=oh[:, b % 2, h, er * n:(er + 1) * n], start=(h == 0), stop=(h == 1))
                mm.then_inc(s["misc"], 1)

            def up(q, slot, e, j, later):
                c = e * NJH + j
                if e == 0 and j == 0:
                    pe.wait_ge(s["misc_free"], first_unit(q - 1) + 8 if later else 8)
                if later or c >= 2:
                    pe.wait_ge(s["gelu_done"], q * NE * NJH + c - 1)
                nc.tensor.matmul(hid[:, c % 2, 0:QW], lhsT=w["m_w1"][:, e, j * P:(j + 1) * P],
                                 rhs=xg[:, slot, e, :, :].rearrange("p b c -> p (b c)"), start=True, stop=True)\
                    .then_inc(s["up_done"], 1)

            def down(q, e, j, later):
                pe.wait_ge(s["gelu_done"], q * NE * NJH + e * NJH + j + 1)
                if j == 0 and (later or e >= 2):
                    pe.wait_ge(s["y_done"], q * NE + e - 1)
                mm = nc.tensor.matmul(yp[:, e % 2, 0:QW], lhsT=w["m_w2"][:, e, j, :], rhs=hT[:, e % 2, j, :],
                                      start=(j == 0), stop=(j == NJH - 1))
                if j == NJH - 1:
                    mm.then_inc(s["down_done"], 1)

            def quad(q, u, first, last):
                number = first_unit(q)
                for j in range(NJH):
                    up(q, u, 0, j, not first)
                for e in range(NE):
                    if not last:
                        gather(q + 1, 1 - u, e, number + e, True)
                    for j in range(NJH):
                        if e + 1 < NE:
                            up(q, u, e + 1, j, True)
                        down(q, e, j, not first)
                pe.wait_ge(s["y_done"], (q + 1) * NE)
                number = number if last else number + 8
                for i, (kind, b, part) in enumerate(tail_order):
                    bank = (8 + i) % 4
                    pe.wait_ge(s["misc_free"], number + i - 3)
                    if kind == "t":
                        c0, c1 = split[part]
                        for c in range(c0, c1):
                            mm = nc.tensor.transpose(misc[0:CH, bank, (c - c0) * D:(c - c0 + 1) * D],
                                                     yT[:, b, :, :].rearrange("p e c -> p (e c)")[:, c * CH:(c + 1) * CH], k.ident[:])
                    else:
                        at = max(n for n, (kk, bb, _) in enumerate(tail_order) if kk == "t" and bb == b)
                        pe.wait_ge(s["misc_free"], number + at + 1)
                        pe.wait_ge(s["sel_done"], (q * QB + b + 1) * NCH)
                        for h in range(2):
                            for c in range(NCH):
                                mm = nc.tensor.matmul(misc[:, bank, h * D:(h + 1) * D], lhsT=sel[:, b, c, h * P:(h + 1) * P],
                                                      rhs=ys[:, b % 2, c, :], start=(c == 0), stop=(c == NCH - 1))
                    mm.then_inc(s["misc"], 1)

            for unit in range(8):
                gather(0, 0, unit, unit, unit >= 4)
            quad(0, 0, True, False)
            quad(1, 1, False, False)
            with pe.Fori(1, NQ // 2 - 1) as i:
                for u in range(2):
                    quad(i * 2 + u, u, False, False)
            quad(NQ - 2, 0, False, False)
            quad(NQ - 1, 1, False, True)

        @block.scalar
        def _(act):
            def quad(q, u, first):
                for e in range(NE):
                    for j in range(NJH):
                        c = e * NJH + j
                        act.wait_ge(s["up_done"], q * NE * NJH + c + 1)
                        if j == 0 and (not first or e >= 2):
                            act.wait_ge(s["down_done"], q * NE + e - 1)
                        nc.scalar.activation(hT[:, e % 2, j, :], hid[:, c % 2, 0:QW], ACT.Gelu,
                                             bias=w["m_b1"][:, c:c + 1]).then_inc(s["gelu_done"], 1)
            quad(0, 0, True)
            with act.Fori(1, NQ) as q:
                quad(q, 0, False)


def stage_moe(nc, k, tag, w, xn_d, val_d, idx_d):
    stage_route(nc, k, tag + "r_", w, xn_d, val_d, idx_d)
    stage_experts(nc, k, tag + "x_", w, xn_d, val_d, idx_d)


def stage_rnn(nc, k, tag, w):
    CK = GW // B
    with ExitStack() as outer:
        osb = lambda name, shape, dt=F32: outer.enter_context(nc.sbuf_tensor(tag + name, shape, dt))
        bx = osb("bx", [P, T, B])
        H = osb("H", [P, B, T])

        with ExitStack() as ctx:
            s = sems(nc, ctx, tag + "p_", "ln_tick ln_rstd diag turned xT_ready bx_done bx_out dx_done res_done")
            ps = lambda name, shape: ctx.enter_context(nc.psum_tensor(tag + name, shape, F32))
            turn = ps("turn", [P, 2, GW])
            bxp = ps("bxp", [P, 2, GW])
            dx = ps("dx", [P, 2, GW])
            xT = ctx.enter_context(nc.sbuf_tensor(tag + "xT", [P, 2, GW], F32))
            diag = ctx.enter_context(nc.sbuf_tensor(tag + "diag", [P, P], F32))
            block = ctx.enter_context(nc.Block())

            @block.vector
            def _(dve):
                nc.vector.tensor_scalar(diag[:], k.ident[:], w["r_d"][:, 0:1], None, ALU.mult).then_inc(s["diag"], 1)

                def ln(g, slot, wait):
                    def xn_free():
                        if wait:
                            dve.wait_ge(s["turned"], g - 1)
                    layernorm_dve(k, s, dve, g, slot, xn_free)

                def residual(g, slot):
                    dve.wait_ge(s["dx_done"], g + 1)
                    xg = k.X[:, bass.ds(g * GT, GT), :].rearrange("p a b -> p (a b)")
                    nc.vector.tensor_tensor(xg, dx[:, slot, :], xg, ALU.add).then_inc(s["res_done"], 1)
                ln(0, 0, False)
                ln(1, 1, False)
                residual(0, 0)
                ln(2, 0, True)
                residual(1, 1)
                with dve.Fori(1, NG // 2) as i:
                    for u in range(2):
                        g = i * 2 + u
                        ln(g + 1, 1 - u, True)
                        residual(g, u)
                dve.wait_ge(s["res_done"], NG)

            @block.gpsimd
            def _(pool):
                with pool.Fori(0, NG + 1) as g:
                    layernorm_pool(k, s, pool, g)

            @block.tensor
            def _(pe):
                pe.wait_ge(s["diag"], 1)

                def turn_in(g, slot, wait):
                    pe.wait_ge(s["ln_tick"], (g + 1) * LN_TICKS)
                    if wait:
                        pe.wait_ge(s["xT_ready"], g - 1)
                    for i in range(GT):
                        mm = nc.tensor.transpose(turn[:, slot, i * P:(i + 1) * P], k.xn[:, slot, i, :], k.ident[:])
                    mm.then_inc(s["turned"], 1)

                def products(g, slot, wait):
                    pe.wait_ge(s["xT_ready"], g + 1)
                    if wait:
                        pe.wait_ge(s["bx_out"], g - 1)
                    nc.tensor.matmul(bxp[:, slot, :], lhsT=w["r_b"][:], rhs=xT[:, slot, :], start=True, stop=True)\
                        .then_inc(s["bx_done"], 1)
                    if wait:
                        pe.wait_ge(s["res_done"], g - 1)
                    for i in range(GT):
                        mm = nc.tensor.matmul(dx[:, slot, i * P:(i + 1) * P], lhsT=xT[:, slot, i * P:(i + 1) * P],
                                              rhs=diag[:], start=True, stop=True)
                    mm.then_inc(s["dx_done"], 1)
                turn_in(0, 0, False)
                turn_in(1, 1, False)
                products(0, 0, False)
                turn_in(2, 0, True)
                products(1, 1, False)
                with pe.Fori(1, NG // 2) as i:
                    for u in range(2):
                        g = i * 2 + u
                        turn_in(g + 1, 1 - u, True)
                        products(g, u, True)

            @block.scalar
            def _(act):
                def evac(g, slot, wait):
                    act.wait_ge(s["turned"], g + 1)
                    if wait:
                        act.wait_ge(s["dx_done"], g - 1)
                    nc.scalar.copy(xT[:, slot, :], turn[:, slot, :]).then_inc(s["xT_ready"], 1)

                def bx_out(g, slot):
                    act.wait_ge(s["bx_done"], g + 1)
                    nc.scalar.copy(bx[:, :, bass.ds(g * 2, 2)].rearrange("p t b -> p b t"),
                                   bxp[:, slot, :].rearrange("p (b t) -> p b t", b=2)).then_inc(s["bx_out"], 1)
                evac(0, 0, False)
                evac(1, 1, False)
                bx_out(0, 0)
                evac(2, 0, True)
                bx_out(1, 1)
                with act.Fori(1, NG // 2) as i:
                    for u in range(2):
                        g = i * 2 + u
                        evac(g + 1, 1 - u, True)
                        bx_out(g, u)
                act.wait_ge(s["bx_out"], NG)

        with ExitStack() as ctx:
            s = sems(nc, ctx, tag + "s_", "h_done p_done kept seeded")
            rec = ctx.enter_context(nc.psum_tensor(tag + "rec", [P, 2, GW], F32))
            ring = ctx.enter_context(nc.sbuf_tensor(tag + "ring", [P, 2, CK, B], F32))
            block = ctx.enter_context(nc.Block())
            SEEDS = 4
            SW = GW // SEEDS

            @block.gpsimd
            def _(pool):
                nc.gpsimd.memset(ring[:, 1, CK - 1, :], 0.0).then_inc(s["h_done"], 1)

                def keep(c, slot):
                    pool.wait_ge(s["h_done"], c * CK + CK + 1)
                    nc.gpsimd.tensor_copy(H[:, :, bass.ds(c * CK, CK)].rearrange("p b t -> p t b"),
                                          ring[:, slot, :, :]).then_inc(s["kept"], 1)
                with pool.Fori(0, T // CK // 2) as i:
                    for u in range(2):
                        keep(i * 2 + u, u)
                pool.wait_ge(s["kept"], T // CK)

            @block.tensor
            def _(pe):
                def seed(c, slot, piece):
                    mm = nc.tensor.matmul(rec[:, slot, piece * SW:(piece + 1) * SW], lhsT=k.ident[:],
                                          rhs=bx[:, bass.ds(c * CK + piece * (CK // SEEDS), CK // SEEDS), :].rearrange("p t b -> p (t b)"),
                                          start=(piece == 0), stop=False, skip_group_check=True)
                    if piece == SEEDS - 1:
                        mm.then_inc(s["seeded"], 1)

                def chunk(c, slot, last):
                    for t in range(CK):
                        pe.wait_ge(s["h_done"], c * CK + t + 1)
                        prev = ring[:, slot, t - 1, :] if t else ring[:, 1 - slot, CK - 1, :]
                        nc.tensor.matmul(rec[:, slot, t * B:(t + 1) * B], lhsT=w["r_a"][:], rhs=prev,
                                         start=False, stop=True, skip_group_check=True).then_inc(s["p_done"], 1)
                        if not last and t % (CK // SEEDS) == 0:
                            seed(c + 1, 1 - slot, t // (CK // SEEDS))
                for piece in range(SEEDS):
                    seed(0, 0, piece)
                NC = T // CK
                with pe.Fori(0, NC // 2 - 1) as i:
                    for u in range(2):
                        chunk(i * 2 + u, u, False)
                chunk(NC - 2, 0, False)
                chunk(NC - 1, 1, True)

            @block.scalar
            def _(act):
                def chunk(c, slot, wait):
                    if wait:
                        act.wait_ge(s["kept"], c - 1)
                    for t in range(CK):
                        act.wait_ge(s["p_done"], c * CK + t + 1)
                        nc.scalar.activation(ring[:, slot, t, :], rec[:, slot, t * B:(t + 1) * B], ACT.Tanh).then_inc(s["h_done"], 1)
                chunk(0, 0, False)
                chunk(1, 1, False)
                with act.Fori(1, T // CK // 2) as i:
                    for u in range(2):
                        chunk(i * 2 + u, u, True)

        with ExitStack() as ctx:
            s = sems(nc, ctx, tag + "c_", "h_ready y_done res_done")
            y = ctx.enter_context(nc.psum_tensor(tag + "y", [P, 2, GW], F32))
            hs = ctx.enter_context(nc.sbuf_tensor(tag + "hs", [P, 2, GW], F32))
            block = ctx.enter_context(nc.Block())

            @block.scalar
            def _(act):
                def stage(g, slot, wait):
                    if wait:
                        act.wait_ge(s["y_done"], g - 1)
                    nc.scalar.copy(hs[:, slot, :], H[:, bass.ds(g * 2, 2), :].rearrange("p b t -> p (b t)")).then_inc(s["h_ready"], 1)
                stage(0, 0, False)
                stage(1, 1, False)
                with act.Fori(1, NG // 2) as i:
                    for u in range(2):
                        stage(i * 2 + u, u, True)

            @block.tensor
            def _(pe):
                def product(g, slot, wait):
                    pe.wait_ge(s["h_ready"], g + 1)
                    if wait:
                        pe.wait_ge(s["res_done"], g - 1)
                    for i in range(GT):
                        mm = nc.tensor.matmul(y[:, slot, i * P:(i + 1) * P], lhsT=hs[:, slot, i * P:(i + 1) * P],
                                              rhs=w["r_c"][:], start=True, stop=True)
                    mm.then_inc(s["y_done"], 1)
                product(0, 0, False)
                product(1, 1, False)
                with pe.Fori(1, NG // 2) as i:
                    for u in range(2):
                        product(i * 2 + u, u, True)

            @block.vector
            def _(dve):
                with dve.Fori(0, NG // 2) as i:
                    for u in range(2):
                        g = i * 2 + u
                        dve.wait_ge(s["y_done"], g + 1)
                        xg = k.X[:, bass.ds(g * GT, GT), :].rearrange("p a b -> p (a b)")
                        nc.vector.tensor_tensor(xg, y[:, u, :], xg, ALU.add).then_inc(s["res_done"], 1)
                dve.wait_ge(s["res_done"], NG)


def lay_out(a):
    c = np.ascontiguousarray
    col = lambda v: c(v.reshape(-1, P).T)
    rows = lambda w: c(w.reshape(-1, P, w.shape[-1]).transpose(1, 0, 2))
    o = {"x": a["L0_attn_a_x"]}
    o["f_w1"] = a["L1_ffn_w1"]
    o["f_b1"] = col(a["L1_ffn_b1"])
    o["f_w2"] = rows(a["L1_ffn_w2"])
    o["f_b2"] = c(np.broadcast_to(a["L1_ffn_b2"], (P, D)))
    for n, src in (("wr", "Wr"), ("wk", "Wk"), ("wv", "Wv")):
        o["b_" + n] = c(a["L1_attn_b_" + src].T)
    o["b_wo"] = rows(c(a["L1_attn_b_Wo"].T))
    for n in ("br", "bk", "bv"):
        o["b_" + n] = col(a["L1_attn_b_" + n])
    o["b_u"] = col(a["L1_attn_b_U"])
    o["b_td"] = a["L1_attn_b_time_decay"].reshape(1, -1)
    o["b_bo"] = c(np.broadcast_to(a["L1_attn_b_bo"], (P, D)))
    o["m_router"] = c(a["L0_ffn_router_w"].T)
    o["m_w1"] = c(a["L0_ffn_w1"].transpose(1, 0, 2))
    o["m_b1"] = col(a["L0_ffn_b1"].reshape(-1))
    o["m_w2"] = c(a["L0_ffn_w2"].reshape(NE, NJH, P, D).transpose(2, 0, 1, 3))
    o["m_b2"] = c(a["L0_ffn_b2"].T)
    o["r_a"] = c(a["L1_attn_a_A"].T)
    o["r_b"] = c(a["L1_attn_a_B_w"].T)
    o["r_c"] = c(a["L1_attn_a_C_w"].T)
    o["r_d"] = col(a["L1_attn_a_D"])
    o["a_mux"] = col(a["L0_attn_a_mu_x"])
    o["a_wx1"] = a["L0_attn_a_W_x1"]
    LR = a["L0_attn_a_W_x2"].shape[2]
    wx2 = np.zeros((P, 5, D), np.float32)
    for i in range(5):
        at = LR * min(i, 3)
        wx2[at:at + LR, i, :] = a["L0_attn_a_W_x2"][:, i, :].T
    o["a_wx2"] = wx2
    o["a_xb"] = c(a["L0_attn_a_x_bias"].T)
    o["a_ww1"] = a["L0_attn_a_W_w1"]
    o["a_ww2"] = a["L0_attn_a_W_w2"]
    o["a_bw2"] = c(np.tile(a["L0_attn_a_b_w2"], 2).reshape(P, 1))
    o["a_wr"] = a["L0_attn_a_W_r"]
    o["a_wk"] = a["L0_attn_a_W_k"]
    o["a_wv"] = c(np.repeat(a["L0_attn_a_W_v"].reshape(D, HA, VD).transpose(0, 2, 1), KD, axis=2))
    o["a_wg"] = a["L0_attn_a_W_g"]
    o["a_u"] = c(np.tile(a["L0_attn_a_u"].reshape(-1), 2).reshape(P, 1))
    o["a_gnw"] = col(a["L0_attn_a_gn_w"])
    o["a_gnb"] = col(a["L0_attn_a_gn_b"])
    o["a_wo"] = a["L0_attn_a_W_o"]
    sel = np.zeros((2, HA, KD, 2, VD, HA, VD), np.float32)
    for b in range(2):
        for h in range(HA):
            for v in range(VD):
                sel[b, h, :, b, v, h, :] = -1.0 / VD
                sel[b, h, :, b, v, h, v] += 1.0
    o["a_sel"] = sel.reshape(P, 2, VD, P)
    o["a_bo"] = np.kron(np.eye(HA), np.full((VD, VD), 1.0 / VD)).astype(np.float32)
    p = np.arange(P)
    hh, dd, g = p // (HD * HG), (p // HG) % HD, p % HG
    feat = (HG * g + hh) * HD + dd
    swap = (HG * g + hh) * HD + (dd ^ 1)
    q, kk, bq, bk = (a["L0_attn_b_" + n] for n in ("wq", "wk", "bq", "bk"))
    o["c_wqk"] = c(np.stack([q[feat].T, q[swap].T, kk[feat].T, kk[swap].T], axis=1))
    o["c_bqk"] = c(np.stack([bq[feat], bq[swap], bk[feat], bk[swap]], axis=1))
    inv = 1.0 / 10000.0 ** (np.arange(0, HD, 2) / HD)
    ang = np.arange(T)[None, :] * inv[dd % (HD // 2)][:, None]
    cos, sin = np.cos(ang), np.sin(ang) * np.where(dd % 2 == 0, -1.0, 1.0)[:, None]
    o["c_tab"] = np.stack([cos, sin, cos / HD ** 0.5, sin / HD ** 0.5], axis=1).astype(np.float32)
    for n in ("wv", "wg", "wo", "wd"):
        o["c_" + n] = c(a["L0_attn_b_" + n].T)
    for n in ("bv", "bo"):
        o["c_" + n] = c(np.broadcast_to(a["L0_attn_b_" + n], (P, D)))
    for n in ("bg", "gamma", "beta"):
        o["c_" + n] = col(a["L0_attn_b_" + n])
    o["c_bd"] = c(a["L0_attn_b_bd"].reshape(HB, 1))
    o["c_avg"] = np.kron(np.eye(HB), np.full((HD, HD), 1.0 / HD)).astype(np.float32)
    o["c_mask"] = (((p // HD) % HG)[:, None] == np.arange(HG)[None, :]).astype(np.float32)
    o["c_pos"] = np.maximum(p[:, None] - p[None, :], 0).astype(np.float32)
    o["c_row"] = c(np.broadcast_to(np.stack([np.full(P, 256.0), -p]), (P, 2, P)).astype(np.float32))
    late = (np.arange(T) >= P).astype(np.float32)
    kaug = np.stack([np.ones(T), late * np.arange(T) / 256, late * np.arange(T) / 256, late, late])
    o["c_kaug"] = np.tile(kaug, (1, HG)).astype(np.float16)
    return o


def stage_weights(nc, k, ctx, tag, args, prefix):
    tiles, loads = {}, []
    for name, ap in args.items():
        if not name.startswith(prefix):
            continue
        if name == "c_kaug":
            tiles[name] = ap
            continue
        t = ctx.enter_context(nc.sbuf_tensor(tag + name, list(ap.shape), F32))
        tiles[name] = t
        loads.append((t[:], ap))
    return tiles, loads


def load_weights(nc, tag, loads):
    with ExitStack() as ctx:
        s = sems(nc, ctx, tag, "w")
        block = ctx.enter_context(nc.Block())

        @block.sync
        def _(sp):
            for dst, src in loads:
                nc.sync.dma_start(dst, src).then_inc(s["w"], 16)
            sp.wait_ge(s["w"], 16 * len(loads))


def hybrid_program(nc, args, out):
    with ExitStack() as top:
        k = open_core(nc, top)
        wf, loads_f = stage_weights(nc, k, top, "w", args, "f_")
        xn_d = nc.dram_tensor("xn_d", [TILES, P, D], F32).ap()
        val_d = nc.dram_tensor("val_d", [B * NE, CAP], F32).ap()
        idx_d = nc.dram_tensor("idx_d", [B * NE, CAP], F32).ap()
        scr = retention_scratch(nc)

        with ExitStack() as moe:
            wm, loads_m = stage_weights(nc, k, moe, "w", args, "m_")
            with ExitStack() as ctx:
                wa, loads_a = stage_weights(nc, k, ctx, "w", args, "a_")
                stage_load(nc, k, args["x"], loads_a + loads_m + loads_f)
                stage_rwkv(nc, k, "a_", wa)
            stage_moe(nc, k, "m0_", wm, xn_d, val_d, idx_d)
            with ExitStack() as ctx:
                wc, loads_c = stage_weights(nc, k, ctx, "w", args, "c_")
                load_weights(nc, "lc_", loads_c)
                stage_retention(nc, k, "c_", wc, scr)
            stage_moe(nc, k, "m1_", wm, xn_d, val_d, idx_d)
        with ExitStack() as ctx:
            wr, loads_r = stage_weights(nc, k, ctx, "w", args, "r_")
            load_weights(nc, "lr_", loads_r)
            stage_rnn(nc, k, "r_", wr)
        stage_ffn(nc, k, "f0_", wf["f_w1"], wf["f_b1"], wf["f_w2"], wf["f_b2"])
        with ExitStack() as ctx:
            wb, loads_b = stage_weights(nc, k, ctx, "w", args, "b_")
            load_weights(nc, "lb_", loads_b)
            stage_wkv(nc, k, "b_", wb)
        stage_ffn(nc, k, "f1_", wf["f_w1"], wf["f_b1"], wf["f_w2"], wf["f_b2"])
        stage_store(nc, k, out)


def kernel(**inputs):
    import concourse.bacc as _bacc
    from concourse import mybir as _mybir
    from concourse.bass_utils import run_bass_kernel_spmd as _run

    nc = _bacc.Bacc("TRN2", target_bir_lowering=False, num_devices=1)
    arrays, args = {}, {}
    for name, a in lay_out({n: np.asarray(v) for n, v in inputs.items()}).items():
        a = np.ascontiguousarray(a)
        arrays["in_" + name] = a
        args[name] = nc.dram_tensor("in_" + name, a.shape, _mybir.dt.from_np(a.dtype), kind="ExternalInput").ap()
    out = nc.dram_tensor("out_x", (B, T, D), F32, kind="ExternalOutput").ap()
    hybrid_program(nc, args, out)
    r = _run(nc, [arrays], core_ids=[0])
    return r.results[0]["out_x"]
```

```python
import concourse.bass as bass
from concourse import mybir
from contextlib import ExitStack
import numpy as np

F32 = mybir.dt.float32
F16 = mybir.dt.float16
BF16 = mybir.dt.bfloat16
U32 = mybir.dt.uint32
ALU = mybir.AluOpType
ACT = mybir.ActivationFunctionType
AX = mybir.AxisListType

P = 128
D = 128
T = 256
B = 32
TOK = B * T
TILES = TOK // P
GT = 4
NG = TILES // GT
GW = GT * P
LN_EPS = 1e-5


class Core:
    pass


def open_core(nc, ctx):
    k = Core()
    k.nc = nc
    k.sb = lambda name, shape, dt=F32: ctx.enter_context(nc.sbuf_tensor(name, shape, dt))
    k.X = k.sb("X", [P, TILES + 2 * GT, D])
    k.ident = k.sb("ident", [P, P])
    k.neg_half = k.sb("neg_half", [P, GT])
    k.stats = k.sb("stats", [P, GT, 6])
    k.mean = k.sb("mean", [P, GT])
    k.diff = k.sb("diff", [P, GT])
    k.dev = k.sb("dev", [P, GT])
    k.vareps = k.sb("vareps", [P, GT])
    k.rstd = k.sb("rstd", [P, GT])
    k.xn = k.sb("xn", [P, 2, GT, D])
    return k


LN_TICKS = 2 * GT + 7


def layernorm_dve(k, s, dve, g, slot, xn_free):
    nc = k.nc
    base = g * LN_TICKS
    for i in range(GT):
        nc.vector.bn_stats(k.stats[:, i, :], k.X[:, g * GT + i, :]).then_inc(s["ln_tick"], 1)
    dve.wait_ge(s["ln_tick"], base + GT)
    mean_e, dev_e, mean_o, dev_o = (k.stats[:, :, j] for j in (1, 2, 4, 5))
    nc.vector.tensor_tensor(k.diff[:], mean_e, mean_o, ALU.subtract).then_inc(s["ln_tick"], 1)
    nc.vector.scalar_tensor_tensor(out=k.dev[:], in0=dev_e, scalar=D * LN_EPS, in1=dev_o, op0=ALU.add, op1=ALU.add).then_inc(s["ln_tick"], 1)
    nc.vector.tensor_tensor(k.mean[:], mean_e, mean_o, ALU.add).then_inc(s["ln_tick"], 1)
    dve.wait_ge(s["ln_tick"], base + GT + 1)
    nc.vector.scalar_tensor_tensor(out=k.diff[:], in0=k.diff[:], scalar=D / 4, in1=k.diff[:], op0=ALU.mult, op1=ALU.mult).then_inc(s["ln_tick"], 1)
    dve.wait_ge(s["ln_tick"], base + GT + 4)
    nc.vector.tensor_tensor(k.dev[:], k.dev[:], k.diff[:], ALU.add).then_inc(s["ln_tick"], 1)
    nc.vector.tensor_scalar(k.mean[:], k.mean[:], 0.5, None, ALU.mult).then_inc(s["ln_tick"], 1)
    dve.wait_ge(s["ln_tick"], base + GT + 5)
    nc.vector.tensor_scalar(k.vareps[:], k.dev[:], 1.0 / D, None, ALU.mult).then_inc(s["ln_tick"], 1)
    xn_free()
    dve.wait_ge(s["ln_rstd"], g + 1)
    for i in range(GT):
        nc.vector.tensor_scalar(k.xn[:, slot, i, :], k.X[:, g * GT + i, :], k.mean[:, i:i + 1],
                                k.rstd[:, i:i + 1], ALU.subtract, ALU.mult).then_inc(s["ln_tick"], 1)
    dve.wait_ge(s["ln_tick"], base + LN_TICKS)


def layernorm_pool(k, s, pool, g):
    pool.wait_ge(s["ln_tick"], g * LN_TICKS + GT + 7)
    k.nc.gpsimd.tensor_tensor(k.rstd[:], k.vareps[:], k.neg_half[:], ALU.pow).then_inc(s["ln_rstd"], 1)


def at_least(eng, sem, v):
    if not (isinstance(v, int) and v <= 0):
        eng.wait_ge(sem, v)


def sems(nc, ctx, stage, names):
    named = {n: ctx.enter_context(nc.semaphore(stage + n)) for n in names.split()}

    def zero():
        with nc.Block() as block:
            @block.gpsimd
            def _(pool):
                runs = []
                for n in sorted(h.num for h in named.values()):
                    if runs and runs[-1].stop == n:
                        runs[-1] = range(runs[-1].start, n + 1)
                    else:
                        runs.append(range(n, n + 1))
                for run in runs:
                    nc.gpsimd.sem_clear(run)
    ctx.callback(zero)
    return named


def stage_load(nc, k, x, loads):
    with ExitStack() as ctx:
        s = sems(nc, ctx, "ld_", "x w zero ident")
        block = ctx.enter_context(nc.Block())
        xg = x.rearrange("b (h p) d -> p (b h) d", p=P)

        @block.sync
        def _(sp):
            for q in range(4):
                n = TILES // 4
                nc.sync.dma_start(k.X[:, q * n:(q + 1) * n, :], xg[:, q * n:(q + 1) * n, :]).then_inc(s["x"], 16)
            for dst, src in loads:
                nc.sync.dma_start(dst, src).then_inc(s["w"], 16)
            sp.wait_ge(s["x"], 64)
            sp.wait_ge(s["w"], 16 * len(loads))

        @block.gpsimd
        def _(pool):
            nc.gpsimd.memset(k.X[:, TILES:TILES + 2 * GT, :], 0.0)
            nc.gpsimd.memset(k.neg_half[:], -0.5)
            nc.gpsimd.memset(k.ident[:], 0.0).then_inc(s["zero"], 1)
            pool.wait_ge(s["zero"], 1)
            nc.gpsimd.affine_select(out=k.ident[:], in_=k.ident[:], compare_op=ALU.not_equal, fill=1.0,
                                    base=0, pattern=[[-1, P]], channel_multiplier=1).then_inc(s["ident"], 1)
            pool.wait_ge(s["ident"], 1)


def stage_store(nc, k, out):
    with ExitStack() as ctx:
        s = sems(nc, ctx, "st_", "out")
        block = ctx.enter_context(nc.Block())
        og = out.rearrange("b (h p) d -> p (b h) d", p=P)

        @block.sync
        def _(sp):
            for q in range(4):
                n = TILES // 4
                nc.sync.dma_start(og[:, q * n:(q + 1) * n, :], k.X[:, q * n:(q + 1) * n, :]).then_inc(s["out"], 16)
            sp.wait_ge(s["out"], 64)


def stage_ffn(nc, k, tag, w1, b1, w2, b2rep):
    HID = w1.shape[1]
    NJ = HID // P
    with ExitStack() as ctx:
        s = sems(nc, ctx, tag, "ln_tick ln_rstd turned xT_ready up_done gelu_done down_done bias_done res_done")
        ps = lambda name, shape: ctx.enter_context(nc.psum_tensor(tag + name, shape, F32))
        turn = ps("turn", [P, 2, GW])
        hid = ps("hid", [P, NJ, GW])
        y = ps("y", [P, 2, GW])
        xT = ctx.enter_context(nc.sbuf_tensor(tag + "xT", [P, 2, GW], F32))
        hT = ctx.enter_context(nc.sbuf_tensor(tag + "hT", [P, NJ, GW], F32))
        block = ctx.enter_context(nc.Block())

        @block.vector
        def _(dve):
            def ln(g, slot, wait):
                def xn_free():
                    if wait:
                        dve.wait_ge(s["turned"], g - 1)
                layernorm_dve(k, s, dve, g, slot, xn_free)

            def residual(g, slot):
                dve.wait_ge(s["down_done"], g + 1)
                dve.wait_ge(s["bias_done"], g + 1)
                xg = k.X[:, bass.ds(g * GT, GT), :].rearrange("p a b -> p (a b)")
                nc.vector.tensor_tensor(xg, y[:, slot, :], xg, ALU.add).then_inc(s["res_done"], 1)

            ln(0, 0, False)
            ln(1, 1, False)
            for u in range(2):
                ln(u + 2, u, True)
                residual(u, u)
            with dve.Fori(1, NG // 2) as i:
                for u in range(2):
                    g = i * 2 + u
                    ln(g + 2, u, True)
                    residual(g, u)
            dve.wait_ge(s["res_done"], NG)

        @block.gpsimd
        def _(pool):
            layernorm_pool(k, s, pool, 0)
            layernorm_pool(k, s, pool, 1)

            def one(g):
                layernorm_pool(k, s, pool, g + 2)
                pool.wait_ge(s["ln_tick"], (g + 1) * LN_TICKS)
                xg = k.X[:, bass.ds(g * GT, GT), :]
                nc.gpsimd.tensor_tensor(xg, xg, b2rep[:, None, :].to_broadcast([P, GT, D]), ALU.add).then_inc(s["bias_done"], 1)
            with pool.Fori(0, NG) as g:
                one(g)

        @block.tensor
        def _(pe):
            def turn_in(g, slot, wait):
                pe.wait_ge(s["ln_tick"], (g + 1) * LN_TICKS)
                if wait:
                    pe.wait_ge(s["xT_ready"], g - 1)
                for i in range(GT):
                    m = nc.tensor.transpose(turn[:, slot, i * P:(i + 1) * P], k.xn[:, slot, i, :], k.ident[:])
                m.then_inc(s["turned"], 1)

            def up(g, slot, wait):
                pe.wait_ge(s["xT_ready"], g + 1)
                for j in range(NJ):
                    if wait:
                        pe.wait_ge(s["gelu_done"], (g - 1) * NJ + j + 1)
                    nc.tensor.matmul(hid[:, j, :], lhsT=w1[:, j * P:(j + 1) * P], rhs=xT[:, slot, :],
                                     start=True, stop=True).then_inc(s["up_done"], 1)

            def down(g, slot, wait):
                if wait:
                    pe.wait_ge(s["res_done"], g - 1)
                for j in range(NJ):
                    pe.wait_ge(s["gelu_done"], g * NJ + j + 1)
                    for i in range(GT):
                        m = nc.tensor.matmul(y[:, slot, i * P:(i + 1) * P], lhsT=hT[:, j, i * P:(i + 1) * P],
                                             rhs=w2[:, j, :], start=(j == 0 and i == 0), stop=(j == NJ - 1),
                                             skip_group_check=True)
                m.then_inc(s["down_done"], 1)

            turn_in(0, 0, False)
            up(0, 0, False)
            turn_in(1, 1, False)
            down(0, 0, False)
            up(1, 1, True)
            turn_in(2, 0, True)
            down(1, 1, False)
            with pe.Fori(1, NG // 2) as i:
                for u in range(2):
                    g = i * 2 + u
                    up(g, u, True)
                    turn_in(g + 1, 1 - u, True)
                    down(g, u, True)

        @block.scalar
        def _(act):
            def evac(g, slot, wait):
                act.wait_ge(s["turned"], g + 1)
                if wait:
                    act.wait_ge(s["up_done"], (g - 1) * NJ)
                nc.scalar.copy(xT[:, slot, :], turn[:, slot, :]).then_inc(s["xT_ready"], 1)

            def gelu(g, slot, wait):
                for j in range(NJ):
                    act.wait_ge(s["up_done"], g * NJ + j + 1)
                    if wait and j == 0:
                        act.wait_ge(s["down_done"], g)
                    nc.scalar.activation(hT[:, j, :], hid[:, j, :], ACT.Gelu, bias=b1[:, j:j + 1]).then_inc(s["gelu_done"], 1)

            evac(0, 0, False)
            gelu(0, 0, False)
            evac(1, 1, False)
            gelu(1, 1, True)
            evac(2, 0, True)
            with act.Fori(1, NG // 2) as i:
                for u in range(2):
                    g = i * 2 + u
                    gelu(g, u, True)
                    evac(g + 1, 1 - u, True)


HA = 16
KD = 4
VD = 8
HK = HA * KD


def stage_rwkv(nc, k, tag, w):
    with ExitStack() as ctx:
        s = sems(nc, ctx, tag, "pre ln_tick ln_rstd turned xT_ready delta_done xm_done low_done low_out mus_done dm_done xi_done xk_done "
                 "tw_done tw_out rk_done rk_out w_done ew_done dec_done v_done kv_done gate_done th_done gg_done "
                 "scan_done q_done rs_done oc_done sq_done var_done ln_done y0_done norm z_done y_done res_done zero")
        ps = lambda name, shape: ctx.enter_context(nc.psum_tensor(tag + name, shape, F32))
        sb = lambda name, shape, dt=F32: ctx.enter_context(nc.sbuf_tensor(tag + name, shape, dt))
        bank = ps("bank", [P, 5, GW])
        vp = ps("vp", [P, 2, 2, T])
        xT = sb("xT", [P, 2, T + 1])
        delta = sb("delta", [P, GW])
        xm = sb("xm", [P, GW])
        low = sb("low", [P, 2, GW])
        xi = sb("xi", [P, 5, GW])
        tw = sb("tw", [HK, GW])
        rk = sb("rk", [P, 2, 2, T])
        ew = sb("ew", [P, T])
        dec = sb("dec", [P, 2, T])
        kv = sb("kv", [P, VD, T])
        S = sb("S", [P, VD, T + 1])
        rS = sb("rS", [P, VD, T])
        th = sb("th", [P, GW])
        gg = sb("gg", [P, 2, GW])
        sq = sb("sq", [P, GW])
        lnv = sb("lnv", [P, GW])
        y0 = sb("y0", [P, GW])
        nt = sb("nt", [P, 2, GW])
        z = sb("z", [P, GW])
        gw = sb("gw", [P, 2])
        epsc = sb("epsc", [P, 1])
        seq = lambda ap: ap.rearrange("p (b t) -> p b t", b=2)
        flat = lambda ap: ap.rearrange("p b t -> p (b t)")
        x = xT[:, :, 1:T + 1]
        shifted = xT[:, :, 0:T]
        BANK = {"turn": 0, "oc": 1, "gate": 2, "var": 3, "low0": 4, "low1": 0, "m0": 1, "m1": 2, "m2": 3, "m3": 4, "m4": 0,
                "tw": 2, "y": 1, "rk": 3, "w": 4}
        ORDER = (3, 4, 1, 0, 2)
        at = {n: bank[:, b, :] for n, b in BANK.items()}
        block = ctx.enter_context(nc.Block())

        @block.vector
        def _(dve):
            nc.vector.memset(epsc[:], LN_EPS).then_inc(s["pre"], 1)
            nc.vector.tensor_scalar(gw[:, 0:1], w["a_gnw"][:], 0.5, None, ALU.mult).then_inc(s["pre"], 1)
            nc.vector.tensor_scalar(gw[:, 1:2], w["a_gnb"][:], 0.5, None, ALU.mult).then_inc(s["pre"], 1)
            dve.wait_ge(s["pre"], 3)

            def ln(p, slot, wait):
                def xn_free():
                    if wait:
                        dve.wait_ge(s["turned"], p - 1)
                layernorm_dve(k, s, dve, p, slot, xn_free)

            def mix_in(p, later):
                dve.wait_ge(s["delta_done"], p + 1)
                if later:
                    dve.wait_ge(s["low_done"], 2 * p)
                nc.vector.scalar_tensor_tensor(out=seq(xm[:]), in0=seq(delta[:]), scalar=w["a_mux"][:, 0:1], in1=x,
                                               op0=ALU.mult, op1=ALU.add).then_inc(s["xm_done"], 1)

            def mix_out(p, later, places):
                if later and places[0] == 0:
                    dve.wait_ge(s["rk_done"], p)
                    dve.wait_ge(s["gate_done"], p)
                for at_place in places:
                    i = ORDER[at_place]
                    dve.wait_ge(s["mus_done"], 5 * p + at_place + 1)
                    nc.vector.scalar_tensor_tensor(out=xi[:, i, :], in0=at[f"m{i}"], scalar=w["a_xb"][:, i:i + 1],
                                                   in1=delta[:], op0=ALU.add, op1=ALU.mult).then_inc(s["dm_done"], 1)
                for at_place in places:
                    if at_place >= 3:
                        i = ORDER[at_place]
                        dve.wait_ge(s["dm_done"], 5 * p + at_place + 1)
                        nc.vector.tensor_tensor(seq(xi[:, i, :]), seq(xi[:, i, :]), x, ALU.add).then_inc(s["xk_done"], 1)

            def outer(p, slot):
                for v in range(4):
                    dve.wait_ge(s["v_done"], 4 * p + v + 1)
                    if v == 0:
                        dve.wait_ge(s["rk_out"], p + 1)
                    nc.vector.tensor_tensor(kv[:, 2 * v:2 * v + 2, :], vp[:, v % 2, :, :],
                                            rk[:, slot, 1:2, :].to_broadcast([P, 2, T]), ALU.mult).then_inc(s["kv_done"], 1)

            def gate(p, slot):
                dve.wait_ge(s["th_done"], p + 1)
                nc.vector.scalar_tensor_tensor(out=gg[:, slot, :], in0=th[:], scalar=1.0, in1=at["gate"],
                                               op0=ALU.add, op1=ALU.mult).then_inc(s["gg_done"], 1)

            def scans(p, slot, later):
                dve.wait_ge(s["dec_done"], p + 1)
                if later:
                    dve.wait_ge(s["q_done"], 4 * p)
                for v in range(VD):
                    if v % 2 == 0:
                        dve.wait_ge(s["kv_done"], 4 * p + v // 2 + 1)
                    nc.vector.tensor_tensor_scan(S[:, v, 1:T + 1], dec[:, slot, :], kv[:, v, :], 0.0,
                                                 ALU.mult, ALU.add).then_inc(s["scan_done"], 1)

            def bonus(p):
                for v in range(4):
                    dve.wait_ge(s["scan_done"], VD * p + 2 * v + 2)
                    nc.vector.scalar_tensor_tensor(out=kv[:, 2 * v:2 * v + 2, :], in0=kv[:, 2 * v:2 * v + 2, :],
                                                   scalar=w["a_u"][:, 0:1], in1=S[:, 2 * v:2 * v + 2, 0:T],
                                                   op0=ALU.mult, op1=ALU.add).then_inc(s["q_done"], 1)

            def finish(p, slot, later):
                dve.wait_ge(s["y0_done"], p + 1)
                nc.vector.scalar_tensor_tensor(out=nt[:, 0, :], in0=at["var"], scalar=LN_EPS, in1=y0[:],
                                               op0=ALU.add, op1=ALU.mult).then_inc(s["norm"], 1)
                dve.wait_ge(s["norm"], 5 * p + 1)
                nc.vector.scalar_tensor_tensor(out=nt[:, 1, :], in0=nt[:, 0, :], scalar=-0.5, in1=y0[:],
                                               op0=ALU.mult, op1=ALU.mult).then_inc(s["norm"], 1)
                dve.wait_ge(s["norm"], 5 * p + 2)
                nc.vector.scalar_tensor_tensor(out=nt[:, 0, :], in0=nt[:, 1, :], scalar=1.5, in1=y0[:],
                                               op0=ALU.add, op1=ALU.mult).then_inc(s["norm"], 1)
                dve.wait_ge(s["norm"], 5 * p + 3)
                nc.vector.tensor_tensor(nt[:, 1, :], at["oc"], nt[:, 0, :], ALU.mult).then_inc(s["norm"], 1)
                dve.wait_ge(s["norm"], 5 * p + 4)
                nc.vector.tensor_scalar(nt[:, 0, :], nt[:, 1, :], gw[:, 0:1], gw[:, 1:2], ALU.mult, ALU.add).then_inc(s["norm"], 1)
                dve.wait_ge(s["norm"], 5 * p + 5)
                if later:
                    dve.wait_ge(s["y_done"], p)
                nc.vector.tensor_tensor(z[:], nt[:, 0, :], gg[:, slot, :], ALU.mult).then_inc(s["z_done"], 1)
                dve.wait_ge(s["z_done"], p + 1)

            def residual(p):
                dve.wait_ge(s["y_done"], p + 1)
                xg = k.X[:, bass.ds(p * GT, GT), :].rearrange("p a b -> p (a b)")
                nc.vector.tensor_tensor(xg, at["y"], xg, ALU.add).then_inc(s["res_done"], 1)

            def iteration(g, u, first):
                ln(g + 2, u, True)
                outer(g, u)
                gate(g, u)
                scans(g, u, not first)
                mix_out(g + 1, True, (0, 1, 2))
                if not first:
                    finish(g - 1, 1 - u, not (isinstance(g, int) and g == 1))
                bonus(g)
                mix_out(g + 1, True, (3, 4))
                if not first:
                    residual(g - 1)
                mix_in(g + 2, True)

            dve.wait_ge(s["zero"], 1)
            ln(0, 0, False)
            ln(1, 1, False)
            mix_in(0, False)
            mix_out(0, False, range(5))
            mix_in(1, True)
            iteration(0, 0, True)
            iteration(1, 1, False)
            with dve.Fori(1, NG // 2) as i:
                for u in range(2):
                    iteration(i * 2 + u, u, False)
            finish(NG - 1, 1, True)
            residual(NG - 1)
            dve.wait_ge(s["res_done"], NG)

        @block.gpsimd
        def _(pool):
            nc.gpsimd.memset(S[:, :, 0:1], 0.0)
            nc.gpsimd.memset(xT[:, :, 0:1], 0.0).then_inc(s["zero"], 1)

            def shift(p, later):
                pool.wait_ge(s["xT_ready"], p + 1)
                if later:
                    pool.wait_ge(s["dm_done"], 5 * p)
                nc.gpsimd.tensor_tensor(seq(delta[:]), shifted, x, ALU.subtract).then_inc(s["delta_done"], 1)

            def add_x(p):
                for at_place, i in enumerate(ORDER[:3]):
                    pool.wait_ge(s["dm_done"], 5 * p + at_place + 1)
                    nc.gpsimd.tensor_tensor(seq(xi[:, i, :]), seq(xi[:, i, :]), x, ALU.add).then_inc(s["xi_done"], 1)

            def read(p, slot, later):
                if later:
                    pool.wait_ge(s["oc_done"], p)
                for v in range(4):
                    pool.wait_ge(s["q_done"], 4 * p + v + 1)
                    nc.gpsimd.tensor_tensor(rS[:, 2 * v:2 * v + 2, :], kv[:, 2 * v:2 * v + 2, :],
                                            rk[:, slot, 0:1, :].to_broadcast([P, 2, T]), ALU.mult).then_inc(s["rs_done"], 1)

            def iteration(g, u, first):
                layernorm_pool(k, s, pool, g + 2)
                add_x(g + 1)
                read(g, u, not first)
                shift(g + 2, True)

            layernorm_pool(k, s, pool, 0)
            layernorm_pool(k, s, pool, 1)
            shift(0, False)
            add_x(0)
            shift(1, True)
            iteration(0, 0, True)
            iteration(1, 1, False)
            with pool.Fori(1, NG // 2) as i:
                for u in range(2):
                    iteration(i * 2 + u, u, False)

        @block.tensor
        def _(pe):
            def turn_in(p, slot):
                pe.wait_ge(s["ln_tick"], (p + 1) * LN_TICKS)
                for i in range(GT):
                    mm = nc.tensor.transpose(at["turn"][:, i * P:(i + 1) * P], k.xn[:, slot, i, :], k.ident[:])
                mm.then_inc(s["turned"], 1)

            def low_rank(p, busy):
                pe.wait_ge(s["xm_done"], p + 1)
                if busy:
                    pe.wait_ge(s["ew_done"], p)
                for i in range(2):
                    nc.tensor.matmul(at[f"low{i}"], lhsT=w["a_wx1"][:, 32 * i:32 * i + P], rhs=xm[:], start=True, stop=True)\
                        .then_inc(s["low_done"], 1)

            def front(p, banks_busy):
                pe.wait_ge(s["low_out"], 2 * p + 2)
                for i in ORDER:
                    if i < 3 and banks_busy:
                        banks_busy(i)
                    nc.tensor.matmul(at[f"m{i}"], lhsT=w["a_wx2"][:, i, :], rhs=low[:, i // 4, :], start=True, stop=True)\
                        .then_inc(s["mus_done"], 1)
                pe.wait_ge(s["xi_done"], 3 * p + 3)
                nc.tensor.matmul(at["tw"][0:HK, :], lhsT=w["a_ww1"][:], rhs=xi[:, 1, :], start=True, stop=True)\
                    .then_inc(s["tw_done"], 1)

            def front2(p):
                pe.wait_ge(s["xk_done"], 2 * p + 2)
                for j, (wn, i) in enumerate((("a_wr", 0), ("a_wk", 2))):
                    if j == 1:
                        pe.wait_ge(s["tw_out"], p + 1)
                    for b in range(2):
                        mm = nc.tensor.matmul(at["rk"][b * HK:(b + 1) * HK, j * T:(j + 1) * T], lhsT=w[wn][:],
                                              rhs=xi[:, i, b * T:(b + 1) * T], start=True, stop=True, skip_group_check=True)
                mm.then_inc(s["rk_done"], 1)
                for b in range(2):
                    mm = nc.tensor.matmul(at["w"][b * HK:(b + 1) * HK, 0:T], lhsT=w["a_ww2"][:], rhs=tw[:, b * T:(b + 1) * T],
                                          start=True, stop=True, skip_group_check=True)
                mm.then_inc(s["w_done"], 1)

            def values(p):
                pe.wait_ge(s["xi_done"], 3 * p + 2)
                for v in range(4):
                    pe.wait_ge(s["kv_done"], 4 * p + v - 1) if not (isinstance(p, int) and p == 0 and v < 2) else None
                    for a in range(2):
                        for b in range(2):
                            mm = nc.tensor.matmul(vp[b * HK:(b + 1) * HK, v % 2, a, :], lhsT=w["a_wv"][:, 2 * v + a, :],
                                                  rhs=xi[:, 3, b * T:(b + 1) * T], start=True, stop=True, skip_group_check=True)
                    mm.then_inc(s["v_done"], 1)

            def gate(p):
                pe.wait_ge(s["tw_out"], p + 1)
                nc.tensor.matmul(at["gate"], lhsT=w["a_wg"][:], rhs=xi[:, 4, :], start=True, stop=True).then_inc(s["gate_done"], 1)

            def heads(p):
                at_least(pe, s["res_done"], p)
                for v in range(4):
                    pe.wait_ge(s["rs_done"], 4 * p + v + 1)
                    for a in range(2):
                        for b in range(2):
                            mm = nc.tensor.matmul(at["oc"][:, b * T:(b + 1) * T], lhsT=w["a_sel"][:, b, 2 * v + a, :],
                                                  rhs=rS[:, 2 * v + a, :], start=(v + a + b == 0), stop=(v == 3 and a == 1),
                                                  skip_group_check=True)
                mm.then_inc(s["oc_done"], 1)

            def variance(p):
                pe.wait_ge(s["sq_done"], p + 1)
                nc.tensor.matmul(at["var"], lhsT=w["a_bo"][:], rhs=sq[:], start=True, stop=True).then_inc(s["var_done"], 1)

            def out(p):
                pe.wait_ge(s["z_done"], p + 1)
                for i in range(GT):
                    mm = nc.tensor.matmul(at["y"][:, i * P:(i + 1) * P], lhsT=z[:, i * P:(i + 1) * P], rhs=w["a_wo"][:],
                                          start=True, stop=True)
                mm.then_inc(s["y_done"], 1)

            def iteration(g, u, first):
                pe.wait_ge(s["dm_done"], 5 * (g + 1))
                if not first:
                    heads(g - 1)
                low_rank(g + 1, True)
                values(g)
                gate(g)
                if not first:
                    pe.wait_ge(s["rk_out"], g + 1)
                    variance(g - 1)

                def busy(i):
                    if i == 1:
                        pe.wait_ge(s["gg_done"], g + 1)
                    elif first:
                        pe.wait_ge(s["rk_out"], 1)
                    elif i == 0:
                        pe.wait_ge(s["norm"], 5 * g - 1)
                front(g + 1, busy)
                pe.wait_ge(s["dm_done"], 5 * (g + 1) + 2)
                turn_in(g + 2, u)
                if not first:
                    pe.wait_ge(s["dm_done"], 5 * (g + 1) + 4)
                    out(g - 1)
                front2(g + 1)

            turn_in(0, 0)
            low_rank(0, False)
            front(0, None)
            pe.wait_ge(s["dm_done"], 2)
            turn_in(1, 1)
            front2(0)
            iteration(0, 0, True)
            iteration(1, 1, False)
            with pe.Fori(1, NG // 2) as i:
                for u in range(2):
                    iteration(i * 2 + u, u, False)
            heads(NG - 1)
            pe.wait_ge(s["rk_out"], NG + 1)
            variance(NG - 1)
            out(NG - 1)

        @block.scalar
        def _(act):
            act.wait_ge(s["pre"], 3)
            act.wait_ge(s["zero"], 1)

            def evac(p, later):
                act.wait_ge(s["turned"], p + 1)
                if later:
                    act.wait_ge(s["xk_done"], 2 * p)
                    act.wait_ge(s["xi_done"], 3 * p)
                nc.scalar.copy(x, seq(at["turn"])).then_inc(s["xT_ready"], 1)

            def low_rank(p):
                for i in range(2):
                    act.wait_ge(s["low_done"], 2 * p + i + 1)
                    nc.scalar.activation(low[:, i, :], at[f"low{i}"], ACT.Tanh).then_inc(s["low_out"], 1)

            def front(p, slot):
                act.wait_ge(s["tw_done"], p + 1)
                nc.scalar.activation(tw[:], at["tw"][0:HK, :], ACT.Tanh).then_inc(s["tw_out"], 1)
                evac(p + 1, True)
                act.wait_ge(s["rk_done"], p + 1)
                nc.scalar.copy(rk[:, slot, :, :].rearrange("p j t -> p (j t)"), at["rk"]).then_inc(s["rk_out"], 1)
                act.wait_ge(s["w_done"], p + 1)
                nc.scalar.activation(ew[:], at["w"][:, 0:T], ACT.Exp, bias=w["a_bw2"][:, 0:1]).then_inc(s["ew_done"], 1)
                act.wait_ge(s["ew_done"], p + 1)
                nc.scalar.activation(dec[:, slot, :], ew[:], ACT.Exp, scale=-1.0).then_inc(s["dec_done"], 1)

            def gate(p, later):
                act.wait_ge(s["gate_done"], p + 1)
                if later:
                    act.wait_ge(s["gg_done"], p)
                nc.scalar.activation(th[:], at["gate"], ACT.Tanh, scale=0.5).then_inc(s["th_done"], 1)

            def norm(p, later):
                act.wait_ge(s["oc_done"], p + 1)
                nc.scalar.activation(sq[:], at["oc"], ACT.Square).then_inc(s["sq_done"], 1)
                nc.scalar.preload_act_table_set("natural_log_exp_and_others")
                act.wait_ge(s["var_done"], p + 1)
                nc.scalar.activation(lnv[:], at["var"], ACT.Ln, bias=epsc[:, 0:1]).then_inc(s["ln_done"], 1)
                act.wait_ge(s["ln_done"], p + 1)
                if later:
                    act.wait_ge(s["norm"], 5 * p)
                nc.scalar.activation(y0[:], lnv[:], ACT.Exp, scale=-0.5).then_inc(s["y0_done"], 1)

            def iteration(g, u, first):
                low_rank(g + 1)
                gate(g, not first)
                if not first:
                    norm(g - 1, not (isinstance(g, int) and g == 1))
                front(g + 1, 1 - u)

            evac(0, False)
            low_rank(0)
            front(0, 0)
            iteration(0, 0, True)
            iteration(1, 1, False)
            with act.Fori(1, NG // 2) as i:
                for u in range(2):
                    iteration(i * 2 + u, u, False)
            norm(NG - 1, True)


HB = 16
HG = 4
HD = D // HB
QROWS = 3 * HG * HD
AUG = 5
KROWS = QROWS + AUG


def stage_retention(nc, k, tag, w, scr):
    with ExitStack() as ctx:
        VO = ctx.enter_context(nc.sbuf_tensor(tag + "VO", [P, TILES, D], F32))
        XM = ctx.enter_context(nc.sbuf_tensor(tag + "XM", [P, B], F32))
        LD = ctx.enter_context(nc.sbuf_tensor(tag + "LD", [P, B * HB], F32))
        retention_project(nc, k, tag + "p", w, scr, VO, XM)
        retention_decay(nc, k, tag + "d", w, scr, XM, LD)
        retention_attend(nc, k, tag + "t", w, scr, VO, LD)
        retention_finish(nc, k, tag + "f", w, scr, VO)


def retention_project(nc, k, tag, w, scr, VO, XM):
    with ExitStack() as ctx:
        s = sems(nc, ctx, tag, "ln_tick ln_rstd turned xT_ready sum_done qk_done cs_done rot_done hi_done lo_done "
                 "g_done th_done gate_done v_done v_out half out0 out1")
        out_sem = (s["out0"], s["out1"])
        ps = lambda name, shape: ctx.enter_context(nc.psum_tensor(tag + name, shape, F32))
        sb = lambda name, shape, dt=F32: ctx.enter_context(nc.sbuf_tensor(tag + name, shape, dt))
        turn = ps("turn", [P, GW])
        qk = ps("qk", [P, 4, GW])
        gp = ps("gp", [P, GW])
        vp = ps("vp", [P, GW])
        xT = sb("xT", [P, 2, GW])
        cs = sb("cs", [P, 4, GW])
        rot = sb("rot", [P, 2, GW])
        hi = sb("hi", [P, 2, 2, GW], F16)
        lo = sb("lo", [P, 2, 2, GW], F16)
        th = sb("th", [P, GW])
        gateb = sb("gateb", [P, GW])
        hbg = sb("hbg", [P, 1])
        gate = sb("gate", [P, 2, GW])
        two = lambda ap: ap.rearrange("p (b t) -> p b t", b=2)
        OUTS = 16 * 7
        block = ctx.enter_context(nc.Block())

        @block.vector
        def _(dve):
            def ln(g, slot, wait, between=None):
                def xn_free():
                    if between:
                        between()
                    if wait:
                        dve.wait_ge(s["turned"], g - 1)
                layernorm_dve(k, s, dve, g, slot, xn_free)

            def turn_pairs(g, slot):
                dve.wait_ge(s["xT_ready"], g + 1)
                nc.vector.tensor_reduce(out=XM[:, bass.ds(g * 2, 2)], in_=two(xT[:, slot, :]), axis=AX.X, op=ALU.add).then_inc(s["sum_done"], 1)
                for j in range(4):
                    dve.wait_ge(s["qk_done"], 4 * g + j + 1)
                    if j % 2 == 0:
                        at_least(dve, s["rot_done"], 2 * g - 1 + j // 2)
                    nc.vector.scalar_tensor_tensor(out=two(cs[:, j, :]), in0=two(qk[:, j, :]), scalar=w["c_bqk"][:, j:j + 1],
                                                   in1=w["c_tab"][:, j:j + 1, :].to_broadcast([P, 2, T]),
                                                   op0=ALU.add, op1=ALU.mult).then_inc(s["cs_done"], 1)

            def work(g, slot, i):
                dve.wait_ge(s["v_done"], g + 1)
                nc.vector.tensor_tensor(VO[:, bass.ds(g * GT, GT), :], vp[:].rearrange("p (a d) -> p a d", a=GT),
                                        w["c_bv"][:, None, :].to_broadcast([P, GT, D]), ALU.add).then_inc(s["v_out"], 1)
                dve.wait_ge(s["th_done"], g + 1)
                at_least(dve, out_sem[slot], OUTS * i)
                nc.vector.scalar_tensor_tensor(out=gate[:, slot, :], in0=th[:], scalar=1.0, in1=gateb[:], op0=ALU.add,
                                               op1=ALU.mult).then_inc(s["gate_done"], 1)
                for j in range(2):
                    dve.wait_ge(s["hi_done"], 2 * g + j + 1)
                    nc.vector.tensor_tensor(lo[:, slot, j, :], rot[:, j, :], hi[:, slot, j, :], ALU.subtract).then_inc(s["lo_done"], 1)

            ln(0, 0, False)
            ln(1, 1, False)
            for u in range(2):
                ln(u + 2, u, True, lambda: turn_pairs(u, u))
                work(u, u, 0)
            with dve.Fori(1, NG // 2) as i:
                for u in range(2):
                    g = i * 2 + u
                    ln(g + 2, u, True, lambda: turn_pairs(g, u))
                    work(g, u, i)

        @block.gpsimd
        def _(pool):
            layernorm_pool(k, s, pool, 0)
            layernorm_pool(k, s, pool, 1)

            def one(g):
                layernorm_pool(k, s, pool, g + 2)
                for j in range(2):
                    pool.wait_ge(s["cs_done"], 4 * g + 2 * j + 2)
                    at_least(pool, s["lo_done"], 2 * g - 1 + j)
                    nc.gpsimd.tensor_tensor(rot[:, j, :], cs[:, 2 * j, :], cs[:, 2 * j + 1, :], ALU.add).then_inc(s["rot_done"], 1)
            one(0)
            with pool.Fori(1, NG) as g:
                one(g)

        @block.scalar
        def _(act):
            def evac(g, slot, wait):
                act.wait_ge(s["turned"], g + 1)
                if wait:
                    act.wait_ge(s["v_done"], g - 1)
                    act.wait_ge(s["sum_done"], g - 1)
                nc.scalar.copy(xT[:, slot, :], turn[:]).then_inc(s["xT_ready"], 1)

            def gates(g):
                act.wait_ge(s["g_done"], g + 1)
                at_least(act, s["gate_done"], g)
                nc.scalar.activation(th[:], gp[:], ACT.Tanh, scale=0.5, bias=hbg[:, 0:1])
                nc.scalar.activation(gateb[:], gp[:], ACT.Identity, bias=w["c_bg"][:, 0:1]).then_inc(s["th_done"], 1)

            def split(g, slot, i):
                at_least(act, out_sem[slot], OUTS * i)
                for j in range(2):
                    act.wait_ge(s["rot_done"], 2 * g + j + 1)
                    nc.scalar.copy(hi[:, slot, j, :], rot[:, j, :]).then_inc(s["hi_done"], 1)

            nc.scalar.mul(hbg[:], w["c_bg"][:], 0.5).then_inc(s["half"], 1)
            act.wait_ge(s["half"], 1)
            evac(0, 0, False)
            for u in range(2):
                gates(u)
                evac(u + 1, 1 - u, u == 1)
                split(u, u, 0)
            with act.Fori(1, NG // 2) as i:
                for u in range(2):
                    g = i * 2 + u
                    gates(g)
                    evac(g + 1, 1 - u, True)
                    split(g, u, i)

        @block.tensor
        def _(pe):
            def turn_in(g, slot):
                pe.wait_ge(s["ln_tick"], (g + 1) * LN_TICKS)
                at_least(pe, s["xT_ready"], g)
                for i in range(GT):
                    m = nc.tensor.transpose(turn[:, i * P:(i + 1) * P], k.xn[:, slot, i, :], k.ident[:])
                m.then_inc(s["turned"], 1)

            def project(g, slot):
                pe.wait_ge(s["xT_ready"], g + 1)
                for j in range(4):
                    at_least(pe, s["cs_done"], 4 * g - 3 + j)
                    nc.tensor.matmul(qk[:, j, :], lhsT=w["c_wqk"][:, j, :], rhs=xT[:, slot, :], start=True, stop=True)\
                        .then_inc(s["qk_done"], 1)
                at_least(pe, s["th_done"], g)
                nc.tensor.matmul(gp[:], lhsT=w["c_wg"][:], rhs=xT[:, slot, :], start=True, stop=True).then_inc(s["g_done"], 1)
                at_least(pe, s["v_out"], g)
                for i in range(GT):
                    m = nc.tensor.matmul(vp[:, i * P:(i + 1) * P], lhsT=xT[:, slot, i * P:(i + 1) * P], rhs=w["c_wv"][:],
                                         start=True, stop=True, skip_group_check=True)
                m.then_inc(s["v_done"], 1)

            turn_in(0, 0)
            for u in range(2):
                project(u, u)
                turn_in(u + 1, 1 - u)
            with pe.Fori(1, NG // 2) as i:
                for u in range(2):
                    g = i * 2 + u
                    project(g, u)
                    turn_in(g + 1, 1 - u)

        @block.sync
        def _(sp):
            def store(g, slot):
                at = bass.ds(g * GW, GW)
                sp.wait_ge(s["gate_done"], g + 1)
                sp.wait_ge(s["lo_done"], 2 * g + 2)
                nc.sync.dma_start(scr["gate"][:, at], gate[:, slot, :]).then_inc(out_sem[slot], 16)
                for term, (qs, ks) in enumerate(((hi, hi), (lo, hi), (hi, lo))):
                    nc.sync.dma_start(scr["q"][term, :, at], qs[:, slot, 0, :]).then_inc(out_sem[slot], 16)
                    nc.sync.dma_start(scr["k"][term, :, at], ks[:, slot, 1, :]).then_inc(out_sem[slot], 16)
            with sp.Fori(0, NG // 2) as i:
                for u in range(2):
                    store(i * 2 + u, u)
            for q in out_sem:
                sp.wait_ge(q, OUTS * NG // 2)


def retention_decay(nc, k, tag, w, scr, XM, LD):
    with ExitStack() as ctx:
        s = sems(nc, ctx, tag, "pre mm th e ld ldd back parts r_out")
        BL = B * HB // P
        ps = ctx.enter_context(nc.psum_tensor(tag + "ps", [HB, B], F32))
        sb = lambda name, shape, dt=F32: ctx.enter_context(nc.sbuf_tensor(tag + name, shape, dt))
        hb = sb("hb", [HB, 1])
        ec = sb("ec", [HB, 1])
        t = sb("t", [HB, B])
        L4 = sb("L4", [P, BL])
        full = sb("full", [P, 2, BL, P])
        part = sb("part", [P, 4, BL, P], F16)
        LN2 = float(np.log(2.0))
        block = ctx.enter_context(nc.Block())

        @block.tensor
        def _(pe):
            nc.tensor.matmul(ps[:], lhsT=w["c_wd"][:], rhs=XM[:], start=True, stop=True).then_inc(s["mm"], 1)

        @block.scalar
        def _(act):
            act.wait_ge(s["pre"], 2)
            act.wait_ge(s["mm"], 1)
            nc.scalar.activation(t[:], ps[:], ACT.Tanh, scale=0.5 / T, bias=hb[:, 0:1]).then_inc(s["th"], 1)
            act.wait_ge(s["th"], 1)
            nc.scalar.activation(t[:], t[:], ACT.Exp, scale=-4 * LN2, bias=ec[:, 0:1]).then_inc(s["e"], 1)
            act.wait_ge(s["e"], 1)
            nc.scalar.preload_act_table_set("natural_log_exp_and_others")
            nc.scalar.activation(t[:], t[:], ACT.Ln, scale=-1.0, bias=1.0).then_inc(s["ld"], 1)

        @block.sync
        def _(sp):
            sp.wait_ge(s["ld"], 1)
            nc.sync.dma_start(scr["ld"].rearrange("b h -> h b"), t[:], allow_slow_non_contiguous=True).then_inc(s["ldd"], 16)
            sp.wait_ge(s["ldd"], 16)
            flat = scr["ld"].rearrange("b h -> (b h)")
            nc.sync.dma_start(L4[:], flat.rearrange("(l p) -> p l", p=P), allow_slow_non_contiguous=True).then_inc(s["back"], 16)
            nc.sync.dma_start(LD[:], flat[None, :].to_broadcast([P, B * HB])).then_inc(s["back"], 16)
            sp.wait_ge(s["back"], 32)
            for r in range(4):
                sp.wait_ge(s["parts"], 6)
                nc.sync.dma_start(scr["aug"][r].rearrange("(l b) h q -> (b h) l q", l=BL), part[:, r]).then_inc(s["r_out"], 16)
            sp.wait_ge(s["r_out"], 64)

        @block.vector
        def _(dve):
            nc.vector.memset(ec[:], -9 * LN2).then_inc(s["pre"], 1)
            nc.vector.tensor_scalar(hb[:], w["c_bd"][:], 0.5, None, ALU.mult).then_inc(s["pre"], 1)
            dve.wait_ge(s["back"], 32)
            rep = L4[:][:, :, None].to_broadcast([P, BL, P])
            for r in range(2):
                nc.vector.tensor_tensor(full[:, r], rep, w["c_row"][:, r:r + 1, :].to_broadcast([P, BL, P]), ALU.mult).then_inc(s["parts"], 1)
            for r in range(2):
                dve.wait_ge(s["parts"], r + 1)
                nc.vector.tensor_copy(part[:, 2 * r], full[:, r]).then_inc(s["parts"], 1)
            for r in range(2):
                dve.wait_ge(s["parts"], r + 3)
                nc.vector.tensor_tensor(part[:, 2 * r + 1], full[:, r], part[:, 2 * r], ALU.subtract).then_inc(s["parts"], 1)


def retention_attend(nc, k, tag, w, scr, VO, LD):
    with ExitStack() as ctx:
        s = sems(nc, ctx, tag, "init ka_in0 ka_in1 kb_in0 kb_in1 m_in0 m_in1 const masked a_done max_done mt_done neg_done b_done exp_done "
                 "dmul_done pv_done ev_done t_done rec_done on_done o_done vo_done dexp vs_done")
        ka_in, kb_in, m_in = (s["ka_in0"], s["ka_in1"]), (s["kb_in0"], s["kb_in1"]), (s["m_in0"], s["m_in1"])
        ps = lambda name, shape: ctx.enter_context(nc.psum_tensor(tag + name, shape, F32))
        sb = lambda name, shape, dt=F32: ctx.enter_context(nc.sbuf_tensor(tag + name, shape, dt))
        pa = ps("pa", [P, 2, 2, T])
        pb = ps("pb", [P, 2, 2 * T])
        pv = ps("pv", [P, 2, 2 * T])
        tb = ps("tb", [P, HG, HG, 32])
        misc = ps("misc", [P, 4, P])
        KA = sb("KA", [QROWS, 2, HG, T], F16)
        KB = sb("KB", [KROWS, 2, HG, T], F16)
        Q = sb("Q", [QROWS, 2, HG, T], F16)
        Qm = sb("Qm", [KROWS, 2, HB, T], F16)
        M = sb("M", [P, 2, 2 * HB])
        MT = sb("MT", [2 * HB, 2, P], F16)
        E = sb("E", [P, 8, 4, P])
        Dm = sb("Dm", [P, 2, HB, P])
        Vs = sb("Vs", [P, 2, 2, HB, 32])
        pvs = sb("pvs", [P, HG, T])
        rec = sb("rec", [P, HG, HG])
        O = sb("O", [P, 2, HB, HD])
        LEAD = 3
        block = ctx.enter_context(nc.Block())

        def load_ka(sp, i, u):
            b = i * 2 + u
            at_least(sp, s["a_done"], HB * (b - 1))
            at = bass.ds(b * T, T)
            nc.sync.dma_start(KA[:, u], scr["k"][:, :, at].rearrange("m (r g) t -> (m r) g t", g=HG)).then_inc(ka_in[u], 16)
            nc.sync.dma_start(Q[:, u], scr["q"][:, :, at].rearrange("m (r g) t -> (m r) g t", g=HG)).then_inc(ka_in[u], 16)

        def load_kb(sp, i, u):
            b = i * 2 + u
            at_least(sp, s["b_done"], HB * (b - 1))
            nc.sync.dma_start(KB[0:QROWS, u], scr["k"][:, :, bass.ds(b * T, T)].rearrange("m (r g) t -> (m r) g t", g=HG)).then_inc(kb_in[u], 16)
            nc.sync.dma_start(Qm[QROWS + 1:KROWS, u, :, 0:P], scr["aug"][:, bass.ds(b, 1)].rearrange("r b h q -> r (b h) q")).then_inc(kb_in[u], 16)

        @block.sync
        def _(sp):
            def put_max(i, u):
                b = i * 2 + u
                sp.wait_ge(s["neg_done"], b + 1)
                nc.sync.dma_start(Qm[QROWS:QROWS + 1, u].rearrange("o h (a q) -> o (h a) q", a=2), MT[:, u, :]).then_inc(m_in[u], 16)

            def iteration(i, u, last=False):
                if not last:
                    nxt = (i, 1) if u == 0 else (i + 1, 0)
                    if not (isinstance(i, int) and i == 0 and u == 0):
                        load_kb(sp, *nxt)
                    if not (isinstance(i, int) and i == B // 2 - 1):
                        load_ka(sp, i + 1, u)
                    put_max(*nxt)

            sp.wait_ge(s["init"], 4)
            for u in range(2):
                nc.sync.dma_start(KB[QROWS:KROWS, u].rearrange("r g t -> r (g t)"), w["c_kaug"]).then_inc(s["const"], 16)
            for u in range(2):
                load_ka(sp, 0, u)
                load_kb(sp, 0, u)
            put_max(0, 0)
            iteration(0, 0)
            iteration(0, 1)
            with sp.Fori(1, B // 2 - 1) as i:
                for u in range(2):
                    iteration(i, u)
            iteration(B // 2 - 1, 0)

        @block.tensor
        def _(pe):
            pe.wait_ge(s["const"], 32)

            def scores_q(i, u, h):
                b = i * 2 + u
                if h == 0:
                    pe.wait_ge(ka_in[u], 32 * (i + 1))
                if h % HG == 0:
                    pe.wait_ge(s["masked"], HG * b + h // HG + 1)
                at_least(pe, s["max_done"], HB * b + h - 1)
                for qt in range(2):
                    m = nc.tensor.matmul(pa[:, h % 2, qt, :], lhsT=Qm[0:QROWS, u, h, qt * P:(qt + 1) * P], rhs=KA[:, u, h // HG, :],
                                         start=True, stop=True, skip_group_check=True)
                m.then_inc(s["a_done"], 1)

            def turn_max(i, u):
                b = i * 2 + u
                pe.wait_ge(s["max_done"], HB * (b + 1))
                at_least(pe, s["neg_done"], b)
                at_least(pe, s["vo_done"], b - 1)
                nc.tensor.transpose(misc[0:2 * HB, 0, :], M[:, u, :], k.ident[:]).then_inc(s["mt_done"], 1)

            def scores_k(i, u, h):
                b = i * 2 + u
                if h == 0:
                    pe.wait_ge(kb_in[u], 32 * (i + 1))
                    pe.wait_ge(m_in[u], 16 * (i + 1))
                at_least(pe, s["exp_done"], HB * b + h - 1)
                for kt in range(2):
                    m = nc.tensor.matmul(pb[:, h % 2, kt * T:(kt + 1) * T], lhsT=KB[:, u, h // HG, kt * P:(kt + 1) * P],
                                         rhs=Qm[:, u, h, :], start=True, stop=True, skip_group_check=True)
                m.then_inc(s["b_done"], 1)

            def values(i, u, g):
                b = i * 2 + u
                if g == 0:
                    pe.wait_ge(s["vs_done"], b + 1)
                at_least(pe, s["ev_done"], HG * b + g - 1)
                pe.wait_ge(s["dmul_done"], HB * b + HG * (g + 1))
                for kt in range(2):
                    for hh in range(HG):
                        h = HG * g + hh
                        m = nc.tensor.matmul(pv[32 * hh:32 * (hh + 1), g % 2, 0:T], lhsT=Vs[:, u, kt, h, :],
                                             rhs=E[:, h % 8, 2 * kt:2 * kt + 2, :].rearrange("p a q -> p (a q)"),
                                             start=(kt == 0), stop=(kt == 1), skip_group_check=True)
                m.then_inc(s["pv_done"], 1)

            def turn_out(b, qt):
                pe.wait_ge(s["ev_done"], HG * (b + 1))
                at_least(pe, s["on_done"], 2 * b + qt)
                for g in range(HG):
                    m = nc.tensor.transpose(tb[:, g].rearrange("p a b -> p (a b)"), pvs[:, g, qt * P:(qt + 1) * P], k.ident[:])
                m.then_inc(s["t_done"], 1)

            def turn_back(b):
                at_least(pe, s["vo_done"], b)
                if not (isinstance(b, int) and b == B - 1):
                    pe.wait_ge(s["neg_done"], b + 2)
                for qt in range(2):
                    pe.wait_ge(s["on_done"], 2 * b + qt + 1)
                    m = nc.tensor.transpose(misc[:, 1 + qt, :], O[:, qt].rearrange("p h d -> p (h d)"), k.ident[:])
                m.then_inc(s["o_done"], 1)

            def iteration(i, u, first=False, last=False):
                b = i * 2 + u
                for t in range(HB + LEAD):
                    if t < HB and not last:
                        scores_q(*((i, 1) if u == 0 else (i + 1, 0)), t)
                    if t == 2 and not first:
                        values(*((i, 0) if u == 1 else (i - 1, 1)), HG - 1)
                    if t == 4 and not first:
                        turn_out(b - 1, 0)
                    if t == 8 and not first:
                        turn_out(b - 1, 1)
                    if t == 11 and not first:
                        turn_back(b - 1)
                    if t == HB + 1 and not last:
                        turn_max(*((i, 1) if u == 0 else (i + 1, 0)))
                    if 0 <= t - LEAD < HB:
                        scores_k(i, u, t - LEAD)
                    v = t - LEAD - 3
                    if v >= 3 and v % HG == 3:
                        values(i, u, v // HG)

            for h in range(HB):
                scores_q(0, 0, h)
            turn_max(0, 0)
            iteration(0, 0, first=True)
            iteration(0, 1)
            with pe.Fori(1, B // 2 - 1) as i:
                for u in range(2):
                    iteration(i, u)
            iteration(B // 2 - 1, 0)
            iteration(B // 2 - 1, 1, last=True)
            values(B // 2 - 1, 1, HG - 1)
            turn_out(B - 1, 0)
            turn_out(B - 1, 1)
            turn_back(B - 1)

        @block.vector
        def _(dve):
            nc.vector.memset(Vs[:], 0.0).then_inc(s["init"], 1)
            nc.vector.memset(Qm[96:KROWS], 0.0).then_inc(s["init"], 1)
            nc.vector.memset(KB[96:KROWS], 0.0).then_inc(s["init"], 1)
            dve.wait_ge(s["init"], 3)
            nc.vector.memset(Vs[:, :, :, :, HD:HD + 1], 1.0).then_inc(s["init"], 1)

            def mask(i, u, g):
                b = i * 2 + u
                if g == 0:
                    dve.wait_ge(ka_in[u], 32 * (i + 1))
                at_least(dve, s["b_done"], HB * (b - 2) + HG * (g + 1))
                for hh in range(HG):
                    m = nc.vector.tensor_scalar(Qm[0:QROWS, u, HG * g + hh, :], Q[:, u, g, :], w["c_mask"][0:QROWS, hh:hh + 1],
                                                None, ALU.mult)
                m.then_inc(s["masked"], 1)

            def maximum(i, u, h):
                b = i * 2 + u
                dve.wait_ge(s["a_done"], HB * b + h + 1)
                if h == 0:
                    at_least(dve, s["mt_done"], b - 1)
                nc.vector.tensor_reduce(out=M[:, u, 2 * h:2 * h + 2], in_=pa[:, h % 2], axis=AX.X, op=ALU.max).then_inc(s["max_done"], 1)

            def negate(i, u):
                b = i * 2 + u
                dve.wait_ge(s["mt_done"], b + 1)
                at_least(dve, m_in[u], 16 * i)
                nc.vector.tensor_scalar(MT[:, u, :], misc[0:2 * HB, 0, :], -1.0, None, ALU.mult).then_inc(s["neg_done"], 1)

            def normalise(b, qt):
                dve.wait_ge(s["t_done"], 2 * b + qt + 1)
                at_least(dve, s["on_done"], 2 * b + qt)
                nc.vector.reciprocal(rec[:], tb[:, :, :, HD]).then_inc(s["rec_done"], 1)
                dve.wait_ge(s["rec_done"], 2 * b + qt + 1)
                at_least(dve, s["o_done"], b)
                nc.vector.tensor_tensor(O[:, qt], tb[:, :, :, 0:HD].rearrange("p a b d -> p (a b) d"),
                                        rec[:].rearrange("p a b -> p (a b)")[:, :, None].to_broadcast([P, HB, HD]), ALU.mult).then_inc(s["on_done"], 1)

            def iteration(i, u, first=False, last=False, mask_next=True):
                b = i * 2 + u
                nxt = (i, 1) if u == 0 else (i + 1, 0)
                for t in range(HB + LEAD + 1):
                    if t < HB and not last:
                        maximum(*nxt, t)
                    if t in (5, 9) and not first:
                        normalise(b - 1, t // 9)
                    r = t - LEAD
                    if mask_next and r >= HG and r % HG == 0:
                        mask(i + 1, u, r // HG - 1)
                    if t == HB + 2 and not last:
                        negate(*nxt)

            dve.wait_ge(s["init"], 4)
            for u in range(2):
                for g in range(HG):
                    mask(0, u, g)
            for h in range(HB):
                maximum(0, 0, h)
            negate(0, 0)
            iteration(0, 0, first=True)
            iteration(0, 1)
            with dve.Fori(1, B // 2 - 1) as i:
                for u in range(2):
                    iteration(i, u)
            iteration(B // 2 - 1, 0, mask_next=False)
            iteration(B // 2 - 1, 1, last=True, mask_next=False)
            for qt in range(2):
                normalise(B - 1, qt)

        @block.scalar
        def _(act):
            def decay(b, u, h):
                if h == 0:
                    at_least(act, s["dmul_done"], HB * (b - 1))
                nc.scalar.activation(Dm[:, u, h, :], w["c_pos"][:], ACT.Exp, scale=LD[:, bass.ds(b * HB + h, 1)]).then_inc(s["dexp"], 1)

            def evac(b, g):
                act.wait_ge(s["pv_done"], HG * b + g + 1)
                if g == 0:
                    at_least(act, s["t_done"], 2 * b)
                nc.scalar.copy(pvs[:, g, :], pv[:, g % 2, 0:T]).then_inc(s["ev_done"], 1)

            def place(b):
                act.wait_ge(s["o_done"], b + 1)
                act.wait_ge(s["vs_done"], b + 1)
                nc.scalar.copy(VO[:, bass.ds(b * 2, 2), :], misc[:, 1:3, :]).then_inc(s["vo_done"], 1)

            def iteration(i, u, first=False, last=False):
                b = i * 2 + u
                if not first:
                    evac(b - 1, HG - 1)
                for h in range(HB):
                    act.wait_ge(s["b_done"], HB * b + h + 1)
                    at_least(act, s["pv_done"], HG * b + h // HG - 1) if h % HG == 0 else None
                    nc.scalar.activation(E[:, h % 8].rearrange("p a q -> p (a q)"), pb[:, h % 2, :], ACT.Exp).then_inc(s["exp_done"], 1)
                    if not last:
                        decay(b + 1, 1 - u, h)
                    if h == 9 and not first:
                        place(b - 1)
                    if h >= 7 and h % HG == 3:
                        evac(b, h // HG - 1)

            for h in range(HB):
                decay(0, 0, h)
            iteration(0, 0, first=True)
            iteration(0, 1)
            with act.Fori(1, B // 2 - 1) as i:
                for u in range(2):
                    iteration(i, u)
            iteration(B // 2 - 1, 0)
            iteration(B // 2 - 1, 1, last=True)
            evac(B - 1, HG - 1)
            place(B - 1)

        @block.gpsimd
        def _(pool):
            pool.wait_ge(s["init"], 4)

            def prepare(b, u):
                at_least(pool, s["pv_done"], HG * (b - 1))
                nc.gpsimd.tensor_copy(Vs[:, u, :, :, 0:HD], VO[:, bass.ds(b * 2, 2), :].rearrange("p a (h d) -> p a h d", d=HD))\
                    .then_inc(s["vs_done"], 1)

            def iteration(i, u, last=False):
                b = i * 2 + u
                for h in range(HB):
                    if h == HB // 2 and not last:
                        prepare(b + 1, 1 - u)
                    pool.wait_ge(s["dexp"], HB * b + h + 1)
                    pool.wait_ge(s["exp_done"], HB * b + h + 1)
                    diag = E[:, h % 8, 0:4:3, :]
                    nc.gpsimd.tensor_tensor(diag, diag, Dm[:, u, h:h + 1, :].to_broadcast([P, 2, P]), ALU.mult).then_inc(s["dmul_done"], 1)

            prepare(0, 0)
            iteration(0, 0)
            iteration(0, 1)
            with pool.Fori(1, B // 2 - 1) as i:
                for u in range(2):
                    iteration(i, u)
            iteration(B // 2 - 1, 0)
            iteration(B // 2 - 1, 1, last=True)


def retention_finish(nc, k, tag, w, scr, VO):
    with ExitStack() as ctx:
        s = sems(nc, ctx, tag, "st mv mm dm sqd var ve rst ab gin0 gin1 za_done zb_done z_done y_done bias_done res_done nh")
        gin = (s["gin0"], s["gin1"])
        ps = lambda name, shape: ctx.enter_context(nc.psum_tensor(tag + name, shape, F32))
        sb = lambda name, shape, dt=F32: ctx.enter_context(nc.sbuf_tensor(tag + name, shape, dt))
        mu = ps("mu", [P, B])
        vr = ps("vr", [P, B])
        y = ps("y", [P, 2, GW])
        st = sb("st", [P, B, 6])
        mv = sb("mv", [P, B, 2])
        dm = sb("dm", [P, B])
        sq = sb("sq", [P, B])
        ve = sb("ve", [P, B])
        rs = sb("rs", [P, B])
        nh = sb("nh", [P, B])
        a = sb("a", [P, B])
        sh = sb("sh", [P, B])
        gate = sb("gate", [P, 2, GW])
        z = sb("z", [P, 3, GW])
        block = ctx.enter_context(nc.Block())
        seq = lambda ap: ap.rearrange("p (b t) -> p b t", b=2)

        @block.sync
        def _(sp):
            def load(g, slot):
                at_least(sp, s["z_done"], g - 1)
                nc.sync.dma_start(gate[:, slot, :], scr["gate"][:, bass.ds(g * GW, GW)]).then_inc(gin[slot], 16)
            for u in range(2):
                load(u, u)
            with sp.Fori(1, NG // 2) as i:
                for u in range(2):
                    load(i * 2 + u, u)

        @block.tensor
        def _(pe):
            pe.wait_ge(s["mv"], B)
            nc.tensor.matmul(mu[:], lhsT=w["c_avg"][:], rhs=mv[:, :, 0], start=True, stop=True).then_inc(s["mm"], 1)
            pe.wait_ge(s["var"], 1)
            nc.tensor.matmul(vr[:], lhsT=w["c_avg"][:], rhs=sq[:], start=True, stop=True).then_inc(s["mm"], 1)

            def out(g, slot):
                pe.wait_ge(s["z_done"], g + 1)
                at_least(pe, s["res_done"], g - 1)
                for i in range(GT):
                    m = nc.tensor.matmul(y[:, slot, i * P:(i + 1) * P], lhsT=z[:, 2, i * P:(i + 1) * P], rhs=w["c_wo"][:],
                                         start=True, stop=True, skip_group_check=True)
                m.then_inc(s["y_done"], 1)
            out(0, 0)
            out(1, 1)
            with pe.Fori(1, NG // 2) as i:
                for u in range(2):
                    out(i * 2 + u, u)

        @block.vector
        def _(dve):
            for b in range(B):
                nc.vector.bn_stats(st[:, b, :], VO[:, 2 * b:2 * b + 2, :].rearrange("p a q -> p (a q)")).then_inc(s["st"], 1)
            for b in range(B):
                dve.wait_ge(s["st"], b + 1)
                nc.vector.bn_aggr(mv[:, b, :], st[:, b, :]).then_inc(s["mv"], 1)
            dve.wait_ge(s["mm"], 1)
            dve.wait_ge(s["mv"], B)
            nc.vector.tensor_tensor(dm[:], mv[:, :, 0], mu[:], ALU.subtract).then_inc(s["dm"], 1)
            dve.wait_ge(s["dm"], 1)
            nc.vector.tensor_tensor(sq[:], dm[:], dm[:], ALU.mult).then_inc(s["sqd"], 1)
            dve.wait_ge(s["sqd"], 1)
            nc.vector.tensor_tensor(sq[:], sq[:], mv[:, :, 1], ALU.add).then_inc(s["var"], 1)
            dve.wait_ge(s["mm"], 2)
            nc.vector.tensor_scalar(ve[:], vr[:], LN_EPS, None, ALU.add).then_inc(s["ve"], 1)
            dve.wait_ge(s["rst"], 1)
            nc.vector.tensor_scalar(a[:], rs[:], w["c_gamma"][:, 0:1], 0.5, ALU.mult, ALU.mult).then_inc(s["ab"], 1)
            nc.vector.tensor_scalar(sh[:], dm[:], 0.0, w["c_beta"][:, 0:1], ALU.mult, ALU.add).then_inc(s["ab"], 1)
            dve.wait_ge(s["ab"], 2)
            nc.vector.tensor_tensor(dm[:], mu[:], a[:], ALU.mult).then_inc(s["ab"], 1)
            dve.wait_ge(s["ab"], 3)
            nc.vector.scalar_tensor_tensor(out=sh[:], in0=sh[:], scalar=0.5, in1=dm[:], op0=ALU.mult, op1=ALU.subtract).then_inc(s["ab"], 1)
            dve.wait_ge(s["ab"], 4)

            def scale(g):
                at_least(dve, s["zb_done"], g)
                nc.vector.tensor_tensor(seq(z[:, 0, :]), VO[:, bass.ds(g * GT, GT), :].rearrange("p (b a) q -> p b (a q)", b=2),
                                        a[:, bass.ds(g * 2, 2)][:, :, None].to_broadcast([P, 2, T]), ALU.mult).then_inc(s["za_done"], 1)

            def apply(g, slot, i):
                dve.wait_ge(s["zb_done"], g + 1)
                dve.wait_ge(gin[slot], 16 * (i + 1))
                at_least(dve, s["y_done"], g)
                nc.vector.tensor_tensor(z[:, 2, :], z[:, 1, :], gate[:, slot, :], ALU.mult).then_inc(s["z_done"], 1)

            def residual(g, slot):
                dve.wait_ge(s["y_done"], g + 1)
                dve.wait_ge(s["bias_done"], g + 1)
                xg = k.X[:, bass.ds(g * GT, GT), :].rearrange("p a b -> p (a b)")
                nc.vector.tensor_tensor(xg, y[:, slot, :], xg, ALU.add).then_inc(s["res_done"], 1)
            scale(0)
            apply(0, 0, 0)
            scale(1)
            apply(1, 1, 0)
            residual(0, 0)
            with dve.Fori(1, NG // 2) as i:
                for u in range(2):
                    g = i * 2 + u
                    scale(g)
                    apply(g, u, i)
                    residual(g - 1, 1 - u)
            residual(NG - 1, 1)
            dve.wait_ge(s["res_done"], NG)

        @block.gpsimd
        def _(pool):
            nc.gpsimd.memset(nh[:], -0.5).then_inc(s["nh"], 1)
            pool.wait_ge(s["nh"], 1)
            pool.wait_ge(s["ve"], 1)
            nc.gpsimd.tensor_tensor(rs[:], ve[:], nh[:], ALU.pow).then_inc(s["rst"], 1)
            pool.wait_ge(s["ab"], 4)

            def one(g):
                xg = k.X[:, bass.ds(g * GT, GT), :]
                nc.gpsimd.tensor_tensor(xg, xg, w["c_bo"][:, None, :].to_broadcast([P, GT, D]), ALU.add).then_inc(s["bias_done"], 1)
                pool.wait_ge(s["za_done"], g + 1)
                at_least(pool, s["z_done"], g)
                nc.gpsimd.tensor_tensor(seq(z[:, 1, :]), seq(z[:, 0, :]), sh[:, bass.ds(g * 2, 2)][:, :, None].to_broadcast([P, 2, T]),
                                        ALU.add).then_inc(s["zb_done"], 1)
            one(0)
            with pool.Fori(1, NG) as g:
                one(g)


def retention_scratch(nc):
    d = lambda name, shape, dt=F32: nc.dram_tensor(name, shape, dt).ap()
    return {"q": d("q_d", [3, P, TOK], F16), "k": d("k_d", [3, P, TOK], F16), "gate": d("gate_d", [P, TOK]),
            "ld": d("ld_d", [B, HB]), "aug": d("aug_d", [4, B, HB, P], F16)}


def stage_wkv(nc, k, tag, w):
    import math
    eps = math.exp(-1 / 12)
    EPS = {"r": eps / 2.0, "k": eps + 0.3 * 1 / 11, "v": eps}
    LO, HI = math.exp(-20.0), math.exp(10.0)
    ERMAX = math.exp(60.0)
    NM = w["b_wk"].shape[1] // P
    with ExitStack() as ctx:
        s = sems(nc, ctx, tag, "ln_tick ln_rstd turned xT_ready mixed k_done kw_done v_done r_done y_done "
                 "eu_done e_done er_done act_tick y0_done head ber_done bf_done tail b_done a_done t_done bias_done res_done "
                 "pre_v pre_p pre_dma")
        ps = lambda name, shape: ctx.enter_context(nc.psum_tensor(tag + name, shape, F32))
        sb = lambda name, shape, dt=F32: ctx.enter_context(nc.sbuf_tensor(tag + name, shape, dt))
        turn = ps("turn", [P, GW])
        kp = ps("kp", [P, 2, GW])
        vp = ps("vp", [P, 2, GW])
        rp = ps("rp", [P, GW])
        y = ps("y", [P, 2, GW])
        xT = sb("xT", [P, 2, T + 1])
        part = sb("part", [P, 3, GW])
        mix = sb("mix", [P, 2, 3, GW])
        NS = 8
        NC = 4
        ee = sb("ee", [P, NS, 2, GW])
        ev = sb("ev", [P, 2, GW])
        euv = sb("euv", [P, NS, GW])
        ce = sb("ce", [P, NC, 2, T + 1])
        cev = sb("cev", [P, NC, 2, T + 1])
        lnb = sb("lnb", [P, GW])
        y0 = sb("y0", [P, NS, GW])
        rec = sb("rec", [P, GW])
        wkv = sb("wkv", [P, 2, GW])
        ones = sb("ones", [P, T])
        ub = sb("ub", [P, NM])
        nbr = sb("nbr", [P, NM])
        wos = sb("wos", [P, NM, D])
        nw = sb("nw", [1, NM * P])
        nwp = sb("nwp", [1, 3, NM * P], BF16)
        decay = sb("decay", [3, NM * P], BF16)
        left = sb("left", [3, 2, T], BF16)
        lefti = sb("lefti", [3, 2, T])
        block = ctx.enter_context(nc.Block())
        seq = lambda ap: ap.rearrange("p (b t) -> p b t", b=2)

        @block.sync
        def _(sp):
            sp.wait_ge(s["pre_v"], 9)
            sp.wait_ge(s["pre_p"], 3)
            for i in range(3):
                nc.sync.dma_start(decay[i:i + 1, :], nwp[0:1, i, :]).then_inc(s["pre_dma"], 16)
            sp.wait_ge(s["pre_dma"], 48)

        @block.vector
        def _(dve):
            nc.vector.memset(ones[:], 1.0).then_inc(s["pre_v"], 1)
            nc.vector.tensor_tensor(ub[:], w["b_u"][:], w["b_bk"][:], ALU.add).then_inc(s["pre_v"], 1)
            nc.vector.tensor_scalar(nbr[:], w["b_br"][:], -1.0, None, ALU.mult).then_inc(s["pre_v"], 1)
            nc.vector.tensor_scalar(wos[:], w["b_wo"][:], -1.0, None, ALU.mult).then_inc(s["pre_v"], 1)
            nc.vector.tensor_scalar(nw[:], w["b_td"][0:1, :], 0.0, -1.0, ALU.max, ALU.mult).then_inc(s["pre_v"], 1)
            dve.wait_ge(s["pre_v"], 5)
            nc.vector.tensor_copy(nwp[:, 0, :], nw[:]).then_inc(s["pre_v"], 1)
            dve.wait_ge(s["pre_v"], 6)
            nc.vector.tensor_tensor(nw[:], nw[:], nwp[:, 0, :], ALU.subtract).then_inc(s["pre_v"], 1)
            dve.wait_ge(s["pre_v"], 7)
            nc.vector.tensor_copy(nwp[:, 1, :], nw[:]).then_inc(s["pre_v"], 1)
            dve.wait_ge(s["pre_v"], 8)
            nc.vector.tensor_tensor(nwp[:, 2, :], nw[:], nwp[:, 1, :], ALU.subtract).then_inc(s["pre_v"], 1)
            dve.wait_ge(s["pre_v"], 9)
            dve.wait_ge(s["pre_p"], 3)

            def ln(g, slot, wait, between=None):
                def xn_free():
                    if between:
                        between()
                    if wait:
                        dve.wait_ge(s["turned"], g - 1)
                layernorm_dve(k, s, dve, g, slot, xn_free)

            def mixes(g, slot, wait):
                dve.wait_ge(s["xT_ready"], g + 1)
                if wait:
                    dve.wait_ge(s["v_done"], (g - 1) * NM)
                    dve.wait_ge(s["r_done"], (g - 1) * NM)
                for i, n in enumerate("rkv"):
                    nc.vector.scalar_tensor_tensor(out=seq(mix[:, slot, i, :]), in0=xT[:, :, 0:T], scalar=EPS[n],
                                                   in1=seq(part[:, i, :]), op0=ALU.mult, op1=ALU.add).then_inc(s["mixed"], 1)

            def head(n, m, later):
                q = m % NS
                dve.wait_ge(s["e_done"], n + 1)
                at_least(dve, s["a_done"], n - NC + 1)
                nc.vector.tensor_scalar(ee[:, q, :, :], ee[:, q, :, :], LO, HI, ALU.max, ALU.min).then_inc(s["head"], 1)
                dve.wait_ge(s["v_done"], n + 1)
                dve.wait_ge(s["head"], 7 * n + 1)
                nc.vector.scalar_tensor_tensor(out=ev[:, m % 2, :], in0=vp[:, m % 2, :], scalar=w["b_bv"][:, m:m + 1],
                                               in1=ee[:, q, 0, :], op0=ALU.add, op1=ALU.mult).then_inc(s["head"], 1)
                nc.vector.scalar_tensor_tensor(out=euv[:, q, :], in0=vp[:, m % 2, :], scalar=w["b_bv"][:, m:m + 1],
                                               in1=ee[:, q, 1, :], op0=ALU.add, op1=ALU.mult).then_inc(s["head"], 1)
                for b in range(2):
                    nc.vector.tensor_tensor_scan(ce[:, m % NC, b, 1:T + 1], ones[:], ee[:, q, 0, b * T:(b + 1) * T], 0.0,
                                                 ALU.mult, ALU.add).then_inc(s["head"], 1)
                dve.wait_ge(s["head"], 7 * n + 2)
                for b in range(2):
                    nc.vector.tensor_tensor_scan(cev[:, m % NC, b, 1:T + 1], ones[:], ev[:, m % 2, b * T:(b + 1) * T], 0.0,
                                                 ALU.mult, ALU.add).then_inc(s["head"], 1)

            def fold(n, m):
                q = m % NS
                dve.wait_ge(s["b_done"], n + 1)
                dve.wait_ge(s["er_done"], n + 1)
                nc.vector.scalar_tensor_tensor(out=y0[:, q, :], in0=y0[:, q, :], scalar=ERMAX, in1=ee[:, q, 1, :],
                                               op0=ALU.min, op1=ALU.mult).then_inc(s["ber_done"], 1)

            def tail(n, m):
                q = m % NS
                dve.wait_ge(s["t_done"], n + 1)
                nc.vector.scalar_tensor_tensor(out=rec[:], in0=ee[:, q, 1, :], scalar=2.0, in1=y0[:, q, :],
                                               op0=ALU.subtract, op1=ALU.mult).then_inc(s["tail"], 1)
                dve.wait_ge(s["a_done"], n + 1)
                dve.wait_ge(s["tail"], 2 * n + 1)
                at_least(dve, s["y_done"], n - 1)
                nc.vector.tensor_tensor(wkv[:, m % 2, :], euv[:, q, :], rec[:], ALU.mult).then_inc(s["tail"], 1)

            def residual(g, slot):
                dve.wait_ge(s["y_done"], (g + 1) * NM)
                dve.wait_ge(s["bias_done"], g + 1)
                xg = k.X[:, bass.ds(g * GT, GT), :].rearrange("p a b -> p (a b)")
                nc.vector.tensor_tensor(xg, y[:, slot, :], xg, ALU.add).then_inc(s["res_done"], 1)

            def group(g, u, first):
                for m in range(NM):
                    n = g * NM + m
                    if m == 4:
                        mixes(g + 1, 1 - u, not first)
                    if m == 6 and not first:
                        residual(g - 1, 1 - u)

                    def unit():
                        if not first or m >= 4:
                            at_least(dve, s["tail"], 2 * (n - 4))
                            tail(n - 4, (m - 4) % NM)
                        head(n, m, not first or m >= NS)
                        if not first or m >= 1:
                            fold(n - 1, (m - 1) % NM)
                    if m == 0:
                        ln(g + 1, 1 - u, not first, unit)
                    else:
                        unit()

            ln(0, 0, False)
            mixes(0, 0, False)
            group(0, 0, True)
            group(1, 1, False)
            with dve.Fori(1, NG // 2) as i:
                for u in range(2):
                    group(i * 2 + u, u, False)
            fold(NG * NM - 1, NM - 1)
            for j in (4, 3, 2, 1):
                dve.wait_ge(s["tail"], 2 * (NG * NM - j))
                tail(NG * NM - j, NM - j)
            residual(NG - 1, 1)
            dve.wait_ge(s["res_done"], NG)

        @block.gpsimd
        def _(pool):
            nc.gpsimd.memset(decay[:], 0.0).then_inc(s["pre_p"], 1)
            nc.gpsimd.memset(ce[:, :, :, 0:1], 0.0)
            nc.gpsimd.memset(xT[:, :, 0:1], 0.0)
            for i in range(3):
                nc.gpsimd.memset(seq(part[:, i, :])[:, :, T - 1:T], 0.0)
            nc.gpsimd.memset(cev[:, :, :, 0:1], 0.0).then_inc(s["pre_p"], 1)
            nc.gpsimd.iota(lefti[:], pattern=[[0, 2], [-1, T]], base=T - 1, channel_multiplier=0,
                           allow_small_or_imprecise_dtypes=True).then_inc(s["pre_p"], 1)
            pool.wait_ge(s["pre_p"], 3)
            nc.gpsimd.tensor_copy(left[:], lefti[:]).then_inc(s["pre_p"], 1)
            layernorm_pool(k, s, pool, 0)

            def sums(n, m):
                q = m % NS
                pool.wait_ge(s["head"], 7 * n + 7)
                nc.gpsimd.tensor_tensor(seq(ee[:, q, 1, :]), ce[:, m % NC, :, 0:T], seq(ee[:, q, 1, :]), ALU.add).then_inc(s["b_done"], 1)
                nc.gpsimd.tensor_tensor(seq(euv[:, q, :]), cev[:, m % NC, :, 0:T], seq(euv[:, q, :]), ALU.add).then_inc(s["a_done"], 1)

            def add_gate(n, m):
                q = m % NS
                pool.wait_ge(s["ber_done"], n + 1)
                nc.gpsimd.tensor_tensor(ee[:, q, 1, :], ee[:, q, 1, :], y0[:, q, :], ALU.add).then_inc(s["bf_done"], 1)

            def prod(n, m):
                q = m % NS
                pool.wait_ge(s["y0_done"], n + 1)
                nc.gpsimd.tensor_tensor(ee[:, q, 1, :], ee[:, q, 1, :], y0[:, q, :], ALU.mult).then_inc(s["t_done"], 1)

            def group(g, first):
                for m in range(NM):
                    n = g * NM + m
                    if m == 0:
                        layernorm_pool(k, s, pool, g + 1)
                        pool.wait_ge(s["ln_tick"], (g + 1) * LN_TICKS)
                        xg = k.X[:, bass.ds(g * GT, GT), :]
                        nc.gpsimd.tensor_tensor(xg, xg, w["b_bo"][:, None, :].to_broadcast([P, GT, D]),
                                                ALU.add).then_inc(s["bias_done"], 1)
                    if not first or m >= 3:
                        prod(n - 3, (m - 3) % NM)
                    sums(n, m)
                    if not first or m >= 1:
                        add_gate(n - 1, (m - 1) % NM)
            group(0, True)
            with pool.Fori(1, NG) as g:
                group(g, False)
            add_gate(NG * NM - 1, NM - 1)
            for j in (3, 2, 1):
                prod(NG * NM - j, NM - j)

        @block.tensor
        def _(pe):
            pe.wait_ge(s["pre_p"], 4)
            pe.wait_ge(s["pre_v"], 9)
            pe.wait_ge(s["pre_dma"], 48)

            def turn_in(g, slot, wait):
                pe.wait_ge(s["ln_tick"], (g + 1) * LN_TICKS)
                if wait:
                    pe.wait_ge(s["xT_ready"], g)
                for i in range(GT):
                    mm = nc.tensor.transpose(turn[:, i * P:(i + 1) * P], k.xn[:, slot, i, :], k.ident[:])
                mm.then_inc(s["turned"], 1)

            def key(n, m, slot):
                at_least(pe, s["e_done"], n - 1)
                nc.tensor.matmul(kp[:, m % 2, :], lhsT=w["b_wk"][:, m * P:(m + 1) * P], rhs=mix[:, slot, 1, :],
                                 start=True, stop=True, skip_group_check=True).then_inc(s["k_done"], 1)

            def gate(n, m, slot):
                at_least(pe, s["er_done"], n)
                nc.tensor.matmul(rp[:], lhsT=w["b_wr"][:, m * P:(m + 1) * P], rhs=mix[:, slot, 0, :],
                                 start=True, stop=True).then_inc(s["r_done"], 1)

            def value(n, m, slot):
                at_least(pe, s["head"], 7 * (n - 2) + 3)
                nc.tensor.matmul(vp[:, m % 2, :], lhsT=w["b_wv"][:, m * P:(m + 1) * P], rhs=mix[:, slot, 2, :],
                                 start=True, stop=True).then_inc(s["v_done"], 1)

            def add_decay(n, m):
                pe.wait_ge(s["eu_done"], n + 1)
                nc.tensor.matmul(kp[:, m % 2, :], lhsT=decay[:, m * P:(m + 1) * P], rhs=left[:].rearrange("p b t -> p (b t)"),
                                 start=False, stop=True, skip_group_check=True).then_inc(s["kw_done"], 1)

            def out(n, m, slot, free):
                pe.wait_ge(s["tail"], 2 * (n + 1))
                if m == 0:
                    at_least(pe, s["res_done"], free)
                for i in range(GT):
                    mm = nc.tensor.matmul(y[:, slot, i * P:(i + 1) * P], lhsT=wkv[:, m % 2, i * P:(i + 1) * P],
                                          rhs=wos[:, m, :], start=(m == 0 and i == 0), stop=(m == NM - 1),
                                          skip_group_check=True)
                mm.then_inc(s["y_done"], 1)

            def group(g, u, first):
                for m in range(NM):
                    n = g * NM + m
                    if m == 0:
                        pe.wait_ge(s["mixed"], 3 * (g + 1))
                    key(n, m, u)
                    if not first or m >= 1:
                        add_decay(n - 1, (m - 1) % NM)
                    gate(n, m, u)
                    value(n, m, u)
                    if not first or m >= 6:
                        out(n - 6, (m - 6) % NM, u if m >= 6 else 1 - u, g - 1)
                    if m == 2:
                        turn_in(g + 1, 1 - u, True)

            turn_in(0, 0, False)
            group(0, 0, True)
            group(1, 1, False)
            with pe.Fori(1, NG // 2) as i:
                for u in range(2):
                    group(i * 2 + u, u, False)
            N = NG * NM
            add_decay(N - 1, NM - 1)
            for j in (6, 5, 4, 3, 2, 1):
                out(N - j, NM - j, 1, None)

        @block.scalar
        def _(act):
            act.wait_ge(s["pre_v"], 3)
            act.wait_ge(s["pre_p"], 2)

            def evac(g, wait):
                act.wait_ge(s["turned"], g + 1)
                if wait:
                    act.wait_ge(s["mixed"], 3 * g)
                nc.scalar.copy(xT[:, :, 1:T + 1], seq(turn[:])).then_inc(s["act_tick"], 1)
                for i, n in enumerate("rkv"):
                    mm = nc.scalar.activation(seq(part[:, i, :])[:, :, 0:T - 1], seq(turn[:])[:, :, 1:T], ACT.Copy,
                                              scale=1.0 - EPS[n])
                mm.then_inc(s["xT_ready"], 1)

            def gate(n, m):
                act.wait_ge(s["r_done"], n + 1)
                nc.scalar.activation(y0[:, m % NS, :], rp[:], ACT.Exp, bias=nbr[:, m:m + 1], scale=-1.0).then_inc(s["er_done"], 1)

            def eu(n, m, later):
                q = m % NS
                act.wait_ge(s["k_done"], n + 1)
                if later:
                    act.wait_ge(s["tail"], 2 * (n - NS + 1))
                nc.scalar.activation(ee[:, q, 1, :], kp[:, m % 2, :], ACT.Exp, bias=ub[:, m:m + 1]).then_inc(s["eu_done"], 1)

            def e(n, m):
                q = m % NS
                act.wait_ge(s["kw_done"], n + 1)
                nc.scalar.activation(ee[:, q, 0, :], kp[:, m % 2, :], ACT.Exp, bias=w["b_bk"][:, m:m + 1]).then_inc(s["e_done"], 1)

            def recip(n, m, ticks, later):
                act.wait_ge(s["bf_done"], n + 1)
                if later:
                    act.wait_ge(s["y0_done"], n)
                nc.scalar.activation(lnb[:], ee[:, m % NS, 1, :], ACT.Ln).then_inc(s["act_tick"], 1)
                act.wait_ge(s["act_tick"], ticks)
                nc.scalar.activation(y0[:, m % NS, :], lnb[:], ACT.Exp, scale=-1.0).then_inc(s["y0_done"], 1)

            def group(g, u, first):
                for m in range(NM):
                    n = g * NM + m
                    if m == 3:
                        evac(g + 1, True)
                    if not first or m >= 1:
                        e(n - 1, (m - 1) % NM)
                    eu(n, m, not first or m >= NS)
                    gate(n, m)
                    if not first or m >= 3:
                        recip(n - 3, (m - 3) % NM, n - 2 + g + (2 if m >= 3 else 1), not first or m >= 4)

            nc.scalar.preload_act_table_set("natural_log_exp_and_others")
            evac(0, False)
            group(0, 0, True)
            group(1, 1, False)
            with act.Fori(1, NG // 2) as i:
                for u in range(2):
                    group(i * 2 + u, u, False)
            N = NG * NM
            e(N - 1, NM - 1)
            for j in (3, 2, 1):
                recip(N - j, NM - j, N - j + 1 + NG + 1, True)


NE = 8
CAP = 2 * T // NE + 1
ROUNDS = -(-CAP // 8)
NJH = 4
QB = 4
NQ = B // QB
SL = NE * CAP
NCH = 5
CH = SL // NCH
QW = QB * CAP
RB = P // NE


def stage_route(nc, k, tag, w, xn_d, val_d, idx_d):
    with ExitStack() as ctx:
        s = sems(nc, ctx, tag, "ln_tick ln_rstd xn_done turned xT_ready logits stored0 stored1 soft exp_done rows work top0 top1 out")
        ps = lambda name, shape: ctx.enter_context(nc.psum_tensor(tag + name, shape, F32))
        sb = lambda name, shape, dt=F32: ctx.enter_context(nc.sbuf_tensor(tag + name, shape, dt))
        turn = ps("turn", [P, 2, GW])
        lg = ps("lg", [P, TILES, NE])
        rows = ps("rows", [P, 2, T])
        xT = sb("xT", [P, 2, GW])
        mx = sb("mx", [P, TILES])
        dl = sb("dl", [P, TILES, NE])
        ex = sb("ex", [P, TILES, NE])
        sm = sb("sm", [P, TILES])
        rs = sb("rs", [P, TILES])
        sc = sb("sc", [P, 2, B, NE])
        work = sb("work", [P, 2, T])
        val = sb("val", [P, 2, ROUNDS * 8])
        idx = sb("idx", [P, 2, ROUNDS * 8], U32)
        idf = sb("idf", [P, 2, ROUNDS * 8])
        stored = (s["stored0"], s["stored1"])
        MOMENTS = GT + 7
        mean = sb("mean", [P, 2, GT])
        vareps = sb("vareps", [P, 2, GT])
        rstd = sb("rstd", [P, 2, GT])
        block = ctx.enter_context(nc.Block())

        @block.sync
        def _(sp):
            with sp.Fori(0, NG // 2) as i:
                for u in range(2):
                    g = i * 2 + u
                    sp.wait_ge(s["xn_done"], (g + 1) * GT)
                    nc.sync.dma_start(xn_d[bass.ds(g * GT, GT), :, :].rearrange("a p d -> p a d"),
                                      k.xn[:, u, :, :]).then_inc(stored[u], 16)
            for u in range(2):
                sp.wait_ge(stored[u], 16 * (NG // 2))
            for r, top in enumerate((s["top0"], s["top1"])):
                sp.wait_ge(top, 3 * ROUNDS)
                nc.sync.dma_start(val_d[r * P:(r + 1) * P, :], val[:, r, 0:CAP]).then_inc(s["out"], 16)
                nc.sync.dma_start(idx_d[r * P:(r + 1) * P, :], idf[:, r, 0:CAP]).then_inc(s["out"], 16)
            sp.wait_ge(s["out"], 64)

        @block.vector
        def _(dve):
            def moments(g, u):
                at_least(dve, s["ln_tick"], g * MOMENTS)
                at_least(dve, s["xn_done"], (g - 1) * GT)
                for i in range(GT):
                    nc.vector.bn_stats(k.stats[:, i, :], k.X[:, g * GT + i, :]).then_inc(s["ln_tick"], 1)
                dve.wait_ge(s["ln_tick"], g * MOMENTS + GT)
                mean_e, dev_e, mean_o, dev_o = (k.stats[:, :, j] for j in (1, 2, 4, 5))
                nc.vector.tensor_tensor(k.diff[:], mean_e, mean_o, ALU.subtract).then_inc(s["ln_tick"], 1)
                nc.vector.scalar_tensor_tensor(out=k.dev[:], in0=dev_e, scalar=D * LN_EPS, in1=dev_o, op0=ALU.add, op1=ALU.add)\
                    .then_inc(s["ln_tick"], 1)
                nc.vector.tensor_tensor(mean[:, u, :], mean_e, mean_o, ALU.add).then_inc(s["ln_tick"], 1)
                dve.wait_ge(s["ln_tick"], g * MOMENTS + GT + 1)
                nc.vector.scalar_tensor_tensor(out=k.diff[:], in0=k.diff[:], scalar=D / 4, in1=k.diff[:], op0=ALU.mult, op1=ALU.mult)\
                    .then_inc(s["ln_tick"], 1)
                dve.wait_ge(s["ln_tick"], g * MOMENTS + GT + 4)
                nc.vector.tensor_tensor(k.dev[:], k.dev[:], k.diff[:], ALU.add).then_inc(s["ln_tick"], 1)
                nc.vector.tensor_scalar(mean[:, u, :], mean[:, u, :], 0.5, None, ALU.mult).then_inc(s["ln_tick"], 1)
                dve.wait_ge(s["ln_tick"], g * MOMENTS + GT + 5)
                nc.vector.tensor_scalar(vareps[:, u, :], k.dev[:], 1.0 / D, None, ALU.mult).then_inc(s["ln_tick"], 1)

            def normalise(g, u, wait):
                if wait:
                    dve.wait_ge(s["turned"], g - 1)
                    dve.wait_ge(stored[u], (g - u) * 8)
                dve.wait_ge(s["ln_rstd"], g + 1)
                for i in range(GT):
                    nc.vector.tensor_scalar(k.xn[:, u, i, :], k.X[:, g * GT + i, :], mean[:, u, i:i + 1], rstd[:, u, i:i + 1],
                                            ALU.subtract, ALU.mult).then_inc(s["xn_done"], 1)

            moments(0, 0)
            for u in range(2):
                moments(u + 1, 1 - u)
                normalise(u, u, False)
            with dve.Fori(1, NG // 2) as i:
                for u in range(2):
                    g = i * 2 + u
                    moments(g + 1, 1 - u)
                    normalise(g, u, True)
            bc = lambda v: v[:, :, None].to_broadcast([P, TILES, NE])
            dve.wait_ge(s["logits"], NG)
            nc.vector.tensor_reduce(mx[:], lg[:], AX.X, ALU.max).then_inc(s["soft"], 1)
            dve.wait_ge(s["soft"], 1)
            nc.vector.tensor_tensor(dl[:], lg[:], bc(mx), ALU.subtract).then_inc(s["soft"], 1)
            dve.wait_ge(s["exp_done"], 1)
            nc.vector.tensor_reduce(sm[:], ex[:], AX.X, ALU.add).then_inc(s["soft"], 1)
            dve.wait_ge(s["soft"], 3)
            nc.vector.reciprocal(rs[:], sm[:]).then_inc(s["soft"], 1)
            dve.wait_ge(s["soft"], 4)
            nc.vector.tensor_tensor(sc[:].rearrange("p h b e -> p b h e"), ex[:].rearrange("p (b h) e -> p b h e", h=2),
                                    rs[:].rearrange("p (b h) -> p b h", h=2)[:, :, :, None].to_broadcast([P, B, 2, NE]),
                                    ALU.mult).then_inc(s["soft"], 1)
            dve.wait_ge(s["rows"], 1)
            nc.vector.tensor_copy(work[:], rows[:]).then_inc(s["work"], 1)
            dve.wait_ge(s["work"], 1)
            for n in range(ROUNDS):
                eight = slice(8 * n, 8 * n + 8)
                for r, top in enumerate((s["top0"], s["top1"])):
                    if n:
                        dve.wait_ge(top, 3 * n)
                    nc.vector.max(val[:, r, eight], work[:, r, :]).then_inc(top, 1)
                for r, top in enumerate((s["top0"], s["top1"])):
                    dve.wait_ge(top, 3 * n + 1)
                    nc.vector.max_index(idx[:, r, eight], val[:, r, eight], work[:, r, :]).then_inc(top, 1)
                for r, top in enumerate((s["top0"], s["top1"])):
                    if n < ROUNDS - 1:
                        dve.wait_ge(top, 3 * n + 2)
                        nc.vector.match_replace(work[:, r, :], val[:, r, eight], work[:, r, :], -1.0).then_inc(top, 1)
            for r, top in enumerate((s["top0"], s["top1"])):
                dve.wait_ge(top, 3 * ROUNDS - 1)
                nc.vector.tensor_copy(idf[:, r, :], idx[:, r, :]).then_inc(top, 1)

        @block.gpsimd
        def _(pool):
            with pool.Fori(0, NG // 2) as i:
                for u in range(2):
                    g = i * 2 + u
                    pool.wait_ge(s["ln_tick"], (g + 1) * MOMENTS)
                    nc.gpsimd.tensor_tensor(rstd[:, u, :], vareps[:, u, :], k.neg_half[:], ALU.pow).then_inc(s["ln_rstd"], 1)

        @block.tensor
        def _(pe):
            def turn_in(g, slot, wait):
                pe.wait_ge(s["xn_done"], (g + 1) * GT)
                if wait:
                    pe.wait_ge(s["xT_ready"], g - 1)
                for i in range(GT):
                    mm = nc.tensor.transpose(turn[:, slot, i * P:(i + 1) * P], k.xn[:, slot, i, :], k.ident[:])
                mm.then_inc(s["turned"], 1)

            def logits(g, slot):
                pe.wait_ge(s["xT_ready"], g + 1)
                for i in range(GT):
                    mm = nc.tensor.matmul(lg[:, g * GT + i, :], lhsT=xT[:, slot, i * P:(i + 1) * P], rhs=w["m_router"][:],
                                          start=True, stop=True)
                mm.then_inc(s["logits"], 1)
            turn_in(0, 0, False)
            turn_in(1, 1, False)
            with pe.Fori(0, NG // 2 - 1) as i:
                for u in range(2):
                    g = i * 2 + u
                    logits(g, u)
                    turn_in(g + 2, u, True)
            logits(NG - 2, 0)
            logits(NG - 1, 1)
            pe.wait_ge(s["soft"], 5)
            for r in range(2):
                for h in range(2):
                    mm = nc.tensor.transpose(rows[:, r, h * P:(h + 1) * P],
                                             sc[:, h, r * RB:(r + 1) * RB, :].rearrange("p b e -> p (b e)"), k.ident[:])
            mm.then_inc(s["rows"], 1)

        @block.scalar
        def _(act):
            def evac(g, slot, wait):
                act.wait_ge(s["turned"], g + 1)
                if wait:
                    act.wait_ge(s["logits"], g - 1)
                nc.scalar.copy(xT[:, slot, :], turn[:, slot, :]).then_inc(s["xT_ready"], 1)
            evac(0, 0, False)
            evac(1, 1, False)
            with act.Fori(1, NG // 2) as i:
                for u in range(2):
                    evac(i * 2 + u, u, True)
            act.wait_ge(s["soft"], 2)
            nc.scalar.activation(ex[:], dl[:], ACT.Exp).then_inc(s["exp_done"], 1)


def stage_experts(nc, k, tag, w, xn_d, val_d, idx_d):
    with ExitStack() as ctx:
        s = sems(nc, ctx, tag, "const slots cols_ps cols high low stage0 stage1 onehot misc misc_free up_done gelu_done "
                 "down_done y_done sel_done")
        ps = lambda name, shape: ctx.enter_context(nc.psum_tensor(tag + name, shape, F32))
        sb = lambda name, shape, dt=F32: ctx.enter_context(nc.sbuf_tensor(tag + name, shape, dt))
        misc = ps("misc", [P, 4, 512])
        hid = ps("hid", [P, 2, 512])
        yp = ps("yp", [P, 2, 512])
        tok = sb("tok", [P, 2])
        steps = sb("steps", [P, T])
        both = sb("both", [B, 2, SL])
        cols = sb("cols", [CH, 2, NCH, B])
        xs = sb("xs", [P, 2, 2 * QB, D])
        xh = sb("xh", [P, 2, 2 * QB, D], F16)
        xl = sb("xl", [P, 2, 2 * QB, D], F16)
        ir = sb("ir", [P, 2, QB, SL])
        oh = sb("oh", [P, 2, 2, SL], F16)
        xg = sb("xg", [P, 2, NE, QB, CAP])
        hT = sb("hT", [P, 2, NJH, QW])
        yT = sb("yT", [P, QB, NE, CAP])
        ys = sb("ys", [CH, 2, NCH, D])
        sel = sb("sel", [CH, QB, NCH, T])
        stage = (s["stage0"], s["stage1"])
        block = ctx.enter_context(nc.Block())
        UNITS = 8 + 3 * QB
        first_unit = lambda q: q * UNITS + 8
        tail_order = [("t", 0, 0), ("t", 0, 1), ("t", 1, 0), ("t", 1, 1), ("o", 0, 0), ("t", 2, 0), ("t", 2, 1),
                      ("o", 1, 0), ("t", 3, 0), ("t", 3, 1), ("o", 2, 0), ("o", 3, 0)]
        split = ((0, 3), (3, 5))

        @block.sync
        def _(sp):
            def load(q, slot, wait):
                if wait == 2:
                    sp.wait_ge(s["misc"], 8)
                if wait > 2:
                    sp.wait_ge(s["misc"], first_unit(q - 3) + 8)
                nc.sync.dma_start(xs[:, slot, :, :], xn_d[bass.ds(q * 2 * QB, 2 * QB), :, :].rearrange("a p d -> p a d"))\
                    .then_inc(stage[slot], 16)
                nc.sync.dma_start(ir[:, slot, :, :].rearrange("p b s -> p (b s)"),
                                  idx_d[bass.ds(q * QB * NE, QB * NE), :].rearrange("r c -> (r c)").partition_broadcast(P))\
                    .then_inc(stage[slot], 16)
            for q in range(4):
                load(q, q % 2, q)
                if q == 1:
                    for i, d in enumerate((val_d, idx_d)):
                        nc.sync.dma_start(both[:, i, :], d.rearrange("(b e) c -> b (e c)", e=NE)).then_inc(s["slots"], 16)
            with sp.Fori(2, NQ // 2) as i:
                for u in range(2):
                    load(i * 2 + u, u, 4)
            sp.wait_ge(s["slots"], 32)
            for u in range(2):
                sp.wait_ge(stage[u], 32 * (NQ // 2))

        @block.gpsimd
        def _(pool):
            nc.gpsimd.iota(tok[:], pattern=[[P, 2]], base=0, channel_multiplier=1,
                           allow_small_or_imprecise_dtypes=True).then_inc(s["const"], 1)
            nc.gpsimd.iota(steps[:], pattern=[[1, T]], base=0, channel_multiplier=0,
                           allow_small_or_imprecise_dtypes=True).then_inc(s["const"], 1)

            def low_part(q, slot):
                pool.wait_ge(s["high"], q + 1)
                nc.gpsimd.tensor_tensor(xl[:, slot], xs[:, slot], xh[:, slot], ALU.subtract).then_inc(s["low"], 1)
            low_part(0, 0)
            low_part(1, 1)
            with pool.Fori(1, NQ // 2) as i:
                for u in range(2):
                    low_part(i * 2 + u, u)

        @block.vector
        def _(dve):
            dve.wait_ge(s["const"], 2)

            def onehot(q, slot, b):
                if b == 0:
                    dve.wait_ge(stage[slot], 16 * (q - slot) + 32)
                for h in range(2):
                    nc.vector.tensor_scalar(oh[:, b % 2, h, :], ir[:, slot, b, :], tok[:, h:h + 1], None,
                                            ALU.is_equal).then_inc(s["onehot"], 1)

            def take(slot, unit, number):
                b, er = unit // 2, unit % 2
                dve.wait_ge(s["misc"], number + 1)
                n = NE // 2
                nc.vector.tensor_copy(xg[:, slot, er * n:(er + 1) * n, b, :],
                                      misc[:, unit % 4, 0:n * CAP]
                                      .rearrange("p (e c) -> p e c", e=n)).then_inc(s["misc_free"], 1)

            def y_out(q, e):
                dve.wait_ge(s["down_done"], q * NE + e + 1)
                nc.vector.tensor_scalar(yT[:, :, e, :], yp[:, e % 2, 0:QW].rearrange("p (b c) -> p b c", b=QB),
                                        w["m_b2"][:, e:e + 1], None, ALU.add).then_inc(s["y_done"], 1)

            def select(q, n):
                b, c = n // NCH, n % NCH
                nc.vector.tensor_scalar(sel[:, b, c, :], steps[0:CH, :], cols[:, 1, c, bass.ds(q * QB + b, 1)],
                                        cols[:, 0, c, bass.ds(q * QB + b, 1)], ALU.is_equal, ALU.mult).then_inc(s["sel_done"], 1)

            def tail(q, number):
                for i, (kind, b, part) in enumerate(tail_order):
                    bank = (8 + i) % 4
                    dve.wait_ge(s["misc"], number + i + 1)
                    if kind == "t":
                        c0, c1 = split[part]
                        nc.vector.tensor_copy(ys[:, b % 2, c0:c1, :].rearrange("p c d -> p (c d)"),
                                              misc[0:CH, bank, 0:(c1 - c0) * D]).then_inc(s["misc_free"], 1)
                    else:
                        xb = k.X[:, bass.ds((q * QB + b) * 2, 2), :].rearrange("p a d -> p (a d)")
                        nc.vector.tensor_tensor(xb, misc[:, bank, 0:2 * D], xb, ALU.add).then_inc(s["misc_free"], 1)

            def quad(q, u, first, last):
                number = first_unit(q)
                if not last:
                    onehot(q + 1, 1 - u, 0)
                for e in range(NE):
                    if not last and e % 2 == 0 and e // 2 + 1 < QB:
                        onehot(q + 1, 1 - u, e // 2 + 1)
                    if not last:
                        take(1 - u, e, number + e)
                    for m in range(QB * NCH * e // NE, QB * NCH * (e + 1) // NE):
                        select(q, m)
                    y_out(q, e)
                tail(q, number if last else number + 8)

            onehot(0, 0, 0)
            for unit in range(8):
                if unit % 2 == 0 and unit // 2 + 1 < QB:
                    onehot(0, 0, unit // 2 + 1)
                take(0, unit, unit)
            dve.wait_ge(s["cols_ps"], 1)
            nc.vector.tensor_copy(cols[:].rearrange("p i c b -> p (i c b)"), yp[0:CH, 0, 0:2 * NCH * B]).then_inc(s["cols"], 1)
            dve.wait_ge(s["cols"], 1)
            quad(0, 0, True, False)
            quad(1, 1, False, False)
            with dve.Fori(1, NQ // 2 - 1) as i:
                for u in range(2):
                    quad(i * 2 + u, u, False, False)
            quad(NQ - 2, 0, False, False)
            quad(NQ - 1, 1, False, True)
            dve.wait_ge(s["misc_free"], 8 + NQ * UNITS - 8)

        @block.tensor
        def _(pe):
            def gather(q, slot, unit, number, later):
                b, er = unit // 2, unit % 2
                n = NE // 2 * CAP
                if unit == 0:
                    pe.wait_ge(s["low"], q + 1)
                pe.wait_ge(s["onehot"], 2 * (QB * q + b + 1))
                if later:
                    pe.wait_ge(s["misc_free"], number - 3)
                for h in range(2):
                    for i, part in enumerate((xh, xl)):
                        mm = nc.tensor.matmul(misc[:, unit % 4, 0:n], lhsT=part[:, slot, 2 * b + h, :],
                                              rhs=oh[:, b % 2, h, er * n:(er + 1) * n], start=(h + i == 0), stop=(h + i == 2))
                mm.then_inc(s["misc"], 1)

            def up(q, slot, e, j, later):
                c = e * NJH + j
                if e == 0 and j == 0:
                    pe.wait_ge(s["misc_free"], first_unit(q - 1) + 8 if later else 8)
                if later or c >= 2:
                    pe.wait_ge(s["gelu_done"], q * NE * NJH + c - 1)
                nc.tensor.matmul(hid[:, c % 2, 0:QW], lhsT=w["m_w1"][:, e, j * P:(j + 1) * P],
                                 rhs=xg[:, slot, e, :, :].rearrange("p b c -> p (b c)"), start=True, stop=True)\
                    .then_inc(s["up_done"], 1)

            def down(q, e, j, later):
                pe.wait_ge(s["gelu_done"], q * NE * NJH + e * NJH + j + 1)
                if j == 0 and (later or e >= 2):
                    pe.wait_ge(s["y_done"], q * NE + e - 1)
                mm = nc.tensor.matmul(yp[:, e % 2, 0:QW], lhsT=w["m_w2"][:, e, j, :], rhs=hT[:, e % 2, j, :],
                                      start=(j == 0), stop=(j == NJH - 1))
                if j == NJH - 1:
                    mm.then_inc(s["down_done"], 1)

            def quad(q, u, first, last):
                number = first_unit(q)
                for j in range(NJH):
                    up(q, u, 0, j, not first)
                for e in range(NE):
                    if not last:
                        gather(q + 1, 1 - u, e, number + e, True)
                    for j in range(NJH):
                        if e + 1 < NE:
                            up(q, u, e + 1, j, True)
                        down(q, e, j, not first)
                pe.wait_ge(s["y_done"], (q + 1) * NE)
                number = number if last else number + 8
                for i, (kind, b, part) in enumerate(tail_order):
                    bank = (8 + i) % 4
                    pe.wait_ge(s["misc_free"], number + i - 3)
                    if kind == "t":
                        c0, c1 = split[part]
                        for c in range(c0, c1):
                            mm = nc.tensor.transpose(misc[0:CH, bank, (c - c0) * D:(c - c0 + 1) * D],
                                                     yT[:, b, :, :].rearrange("p e c -> p (e c)")[:, c * CH:(c + 1) * CH], k.ident[:])
                    else:
                        at = max(n for n, (kk, bb, _) in enumerate(tail_order) if kk == "t" and bb == b)
                        pe.wait_ge(s["misc_free"], number + at + 1)
                        pe.wait_ge(s["sel_done"], (q * QB + b + 1) * NCH)
                        for h in range(2):
                            for c in range(NCH):
                                mm = nc.tensor.matmul(misc[:, bank, h * D:(h + 1) * D], lhsT=sel[:, b, c, h * P:(h + 1) * P],
                                                      rhs=ys[:, b % 2, c, :], start=(c == 0), stop=(c == NCH - 1))
                    mm.then_inc(s["misc"], 1)

            for unit in range(8):
                gather(0, 0, unit, unit, unit >= 4)
            pe.wait_ge(s["slots"], 32)
            for i in range(2):
                for c in range(NCH):
                    at = (i * NCH + c) * B
                    mm = nc.tensor.transpose(yp[0:CH, 0, at:at + B], both[:, i, c * CH:(c + 1) * CH], k.ident[0:B, 0:B])
            mm.then_inc(s["cols_ps"], 1)
            pe.wait_ge(s["cols"], 1)
            quad(0, 0, True, False)
            quad(1, 1, False, False)
            with pe.Fori(1, NQ // 2 - 1) as i:
                for u in range(2):
                    quad(i * 2 + u, u, False, False)
            quad(NQ - 2, 0, False, False)
            quad(NQ - 1, 1, False, True)

        @block.scalar
        def _(act):
            def high_part(q, slot):
                act.wait_ge(stage[slot], 16 * (q - slot) + 32)
                nc.scalar.copy(xh[:, slot], xs[:, slot]).then_inc(s["high"], 1)

            def quad(q, u, first, last):
                for e in range(NE):
                    if e == 1 and not last:
                        high_part(q + 2, u)
                    for j in range(NJH):
                        c = e * NJH + j
                        act.wait_ge(s["up_done"], q * NE * NJH + c + 1)
                        if j == 0 and (not first or e >= 2):
                            act.wait_ge(s["down_done"], q * NE + e - 1)
                        nc.scalar.activation(hT[:, e % 2, j, :], hid[:, c % 2, 0:QW], ACT.Gelu,
                                             bias=w["m_b1"][:, c:c + 1]).then_inc(s["gelu_done"], 1)
            high_part(0, 0)
            high_part(1, 1)
            quad(0, 0, True, False)
            quad(1, 1, False, False)
            with act.Fori(1, NQ // 2 - 1) as i:
                for u in range(2):
                    quad(i * 2 + u, u, False, False)
            quad(NQ - 2, 0, False, True)
            quad(NQ - 1, 1, False, True)


def stage_moe(nc, k, tag, w, xn_d, val_d, idx_d):
    stage_route(nc, k, tag + "r_", w, xn_d, val_d, idx_d)
    stage_experts(nc, k, tag + "x_", w, xn_d, val_d, idx_d)


def stage_rnn(nc, k, tag, w):
    CK = GW // B
    with ExitStack() as outer:
        osb = lambda name, shape, dt=F32: outer.enter_context(nc.sbuf_tensor(tag + name, shape, dt))
        bx = osb("bx", [P, T, B])
        H = osb("H", [P, B, T])

        with ExitStack() as ctx:
            s = sems(nc, ctx, tag + "p_", "ln_tick ln_rstd diag turned xT_ready bx_done bx_out dx_done res_done")
            ps = lambda name, shape: ctx.enter_context(nc.psum_tensor(tag + name, shape, F32))
            turn = ps("turn", [P, 2, GW])
            bxp = ps("bxp", [P, 2, GW])
            dx = ps("dx", [P, 2, GW])
            xT = ctx.enter_context(nc.sbuf_tensor(tag + "xT", [P, 2, GW], F32))
            diag = ctx.enter_context(nc.sbuf_tensor(tag + "diag", [P, P], F32))
            block = ctx.enter_context(nc.Block())

            @block.vector
            def _(dve):
                nc.vector.tensor_scalar(diag[:], k.ident[:], w["r_d"][:, 0:1], None, ALU.mult).then_inc(s["diag"], 1)

                def ln(g, slot, wait, between=None):
                    def xn_free():
                        if between:
                            between()
                        if wait:
                            dve.wait_ge(s["turned"], g - 1)
                    layernorm_dve(k, s, dve, g, slot, xn_free)

                def residual(g, slot):
                    dve.wait_ge(s["dx_done"], g + 1)
                    xg = k.X[:, bass.ds(g * GT, GT), :].rearrange("p a b -> p (a b)")
                    nc.vector.tensor_tensor(xg, dx[:, slot, :], xg, ALU.add).then_inc(s["res_done"], 1)
                ln(0, 0, False)
                ln(1, 1, False)
                for u in range(2):
                    ln(u + 2, u, True, lambda: residual(u, u))
                with dve.Fori(1, NG // 2) as i:
                    for u in range(2):
                        g = i * 2 + u
                        ln(g + 2, u, True, lambda: residual(g, u))
                dve.wait_ge(s["res_done"], NG)

            @block.gpsimd
            def _(pool):
                with pool.Fori(0, NG + 2) as g:
                    layernorm_pool(k, s, pool, g)

            @block.tensor
            def _(pe):
                pe.wait_ge(s["diag"], 1)

                def turn_in(g, slot, wait):
                    pe.wait_ge(s["ln_tick"], (g + 1) * LN_TICKS)
                    if wait:
                        pe.wait_ge(s["xT_ready"], g - 1)
                    for i in range(GT):
                        mm = nc.tensor.transpose(turn[:, slot, i * P:(i + 1) * P], k.xn[:, slot, i, :], k.ident[:])
                    mm.then_inc(s["turned"], 1)

                def products(g, slot, wait):
                    pe.wait_ge(s["xT_ready"], g + 1)
                    if wait:
                        pe.wait_ge(s["bx_out"], g - 1)
                    nc.tensor.matmul(bxp[:, slot, :], lhsT=w["r_b"][:], rhs=xT[:, slot, :], start=True, stop=True)\
                        .then_inc(s["bx_done"], 1)
                    if wait:
                        pe.wait_ge(s["res_done"], g - 1)
                    for i in range(GT):
                        mm = nc.tensor.matmul(dx[:, slot, i * P:(i + 1) * P], lhsT=xT[:, slot, i * P:(i + 1) * P],
                                              rhs=diag[:], start=True, stop=True)
                    mm.then_inc(s["dx_done"], 1)
                turn_in(0, 0, False)
                products(0, 0, False)
                turn_in(1, 1, False)
                products(1, 1, False)
                turn_in(2, 0, True)
                with pe.Fori(1, NG // 2) as i:
                    for u in range(2):
                        g = i * 2 + u
                        products(g, u, True)
                        turn_in(g + 1, 1 - u, True)

            @block.scalar
            def _(act):
                def evac(g, slot, wait):
                    act.wait_ge(s["turned"], g + 1)
                    if wait:
                        act.wait_ge(s["dx_done"], g - 1)
                    nc.scalar.copy(xT[:, slot, :], turn[:, slot, :]).then_inc(s["xT_ready"], 1)

                def bx_out(g, slot):
                    act.wait_ge(s["bx_done"], g + 1)
                    nc.scalar.copy(bx[:, :, bass.ds(g * 2, 2)].rearrange("p t b -> p b t"),
                                   bxp[:, slot, :].rearrange("p (b t) -> p b t", b=2)).then_inc(s["bx_out"], 1)
                evac(0, 0, False)
                bx_out(0, 0)
                evac(1, 1, False)
                bx_out(1, 1)
                evac(2, 0, True)
                with act.Fori(1, NG // 2) as i:
                    for u in range(2):
                        g = i * 2 + u
                        bx_out(g, u)
                        evac(g + 1, 1 - u, True)
                act.wait_ge(s["bx_out"], NG)

        with ExitStack() as ctx:
            s = sems(nc, ctx, tag + "s_", "h_done p_done kept seeded")
            rec = ctx.enter_context(nc.psum_tensor(tag + "rec", [P, 2, GW], F32))
            ring = ctx.enter_context(nc.sbuf_tensor(tag + "ring", [P, 2, CK, B], F32))
            block = ctx.enter_context(nc.Block())
            SEEDS = 4
            SW = GW // SEEDS

            @block.gpsimd
            def _(pool):
                nc.gpsimd.memset(ring[:, 1, CK - 1, :], 0.0).then_inc(s["h_done"], 1)

                def keep(c, slot):
                    pool.wait_ge(s["h_done"], c * CK + CK + 1)
                    nc.gpsimd.tensor_copy(H[:, :, bass.ds(c * CK, CK)].rearrange("p b t -> p t b"),
                                          ring[:, slot, :, :]).then_inc(s["kept"], 1)
                with pool.Fori(0, T // CK // 2) as i:
                    for u in range(2):
                        keep(i * 2 + u, u)
                pool.wait_ge(s["kept"], T // CK)

            @block.tensor
            def _(pe):
                def seed(c, slot, piece):
                    mm = nc.tensor.matmul(rec[:, slot, piece * SW:(piece + 1) * SW], lhsT=k.ident[:],
                                          rhs=bx[:, bass.ds(c * CK + piece * (CK // SEEDS), CK // SEEDS), :].rearrange("p t b -> p (t b)"),
                                          start=(piece == 0), stop=False, skip_group_check=True)
                    if piece == SEEDS - 1:
                        mm.then_inc(s["seeded"], 1)

                def chunk(c, slot, last):
                    for t in range(CK):
                        pe.wait_ge(s["h_done"], c * CK + t + 1)
                        prev = ring[:, slot, t - 1, :] if t else ring[:, 1 - slot, CK - 1, :]
                        nc.tensor.matmul(rec[:, slot, t * B:(t + 1) * B], lhsT=w["r_a"][:], rhs=prev,
                                         start=False, stop=True, skip_group_check=True).then_inc(s["p_done"], 1)
                        if not last and t % (CK // SEEDS) == 0:
                            seed(c + 1, 1 - slot, t // (CK // SEEDS))
                for piece in range(SEEDS):
                    seed(0, 0, piece)
                NC = T // CK
                with pe.Fori(0, NC // 2 - 1) as i:
                    for u in range(2):
                        chunk(i * 2 + u, u, False)
                chunk(NC - 2, 0, False)
                chunk(NC - 1, 1, True)

            @block.scalar
            def _(act):
                def chunk(c, slot, wait):
                    if wait:
                        act.wait_ge(s["kept"], c - 1)
                    for t in range(CK):
                        act.wait_ge(s["p_done"], c * CK + t + 1)
                        nc.scalar.activation(ring[:, slot, t, :], rec[:, slot, t * B:(t + 1) * B], ACT.Tanh).then_inc(s["h_done"], 1)
                chunk(0, 0, False)
                chunk(1, 1, False)
                with act.Fori(1, T // CK // 2) as i:
                    for u in range(2):
                        chunk(i * 2 + u, u, True)

        with ExitStack() as ctx:
            s = sems(nc, ctx, tag + "c_", "h_ready y_done res_done")
            y = ctx.enter_context(nc.psum_tensor(tag + "y", [P, 2, GW], F32))
            hs = ctx.enter_context(nc.sbuf_tensor(tag + "hs", [P, 2, GW], F32))
            block = ctx.enter_context(nc.Block())

            @block.scalar
            def _(act):
                def stage(g, slot, wait):
                    if wait:
                        act.wait_ge(s["y_done"], g - 1)
                    nc.scalar.copy(hs[:, slot, :], H[:, bass.ds(g * 2, 2), :].rearrange("p b t -> p (b t)")).then_inc(s["h_ready"], 1)
                stage(0, 0, False)
                stage(1, 1, False)
                with act.Fori(1, NG // 2) as i:
                    for u in range(2):
                        stage(i * 2 + u, u, True)

            @block.tensor
            def _(pe):
                def product(g, slot, wait):
                    pe.wait_ge(s["h_ready"], g + 1)
                    if wait:
                        pe.wait_ge(s["res_done"], g - 1)
                    for i in range(GT):
                        mm = nc.tensor.matmul(y[:, slot, i * P:(i + 1) * P], lhsT=hs[:, slot, i * P:(i + 1) * P],
                                              rhs=w["r_c"][:], start=True, stop=True)
                    mm.then_inc(s["y_done"], 1)
                product(0, 0, False)
                product(1, 1, False)
                with pe.Fori(1, NG // 2) as i:
                    for u in range(2):
                        product(i * 2 + u, u, True)

            @block.vector
            def _(dve):
                with dve.Fori(0, NG // 2) as i:
                    for u in range(2):
                        g = i * 2 + u
                        dve.wait_ge(s["y_done"], g + 1)
                        xg = k.X[:, bass.ds(g * GT, GT), :].rearrange("p a b -> p (a b)")
                        nc.vector.tensor_tensor(xg, y[:, u, :], xg, ALU.add).then_inc(s["res_done"], 1)
                dve.wait_ge(s["res_done"], NG)


def lay_out(a):
    c = np.ascontiguousarray
    col = lambda v: c(v.reshape(-1, P).T)
    rows = lambda w: c(w.reshape(-1, P, w.shape[-1]).transpose(1, 0, 2))
    o = {"x": a["L0_attn_a_x"]}
    o["f_w1"] = a["L1_ffn_w1"]
    o["f_b1"] = col(a["L1_ffn_b1"])
    o["f_w2"] = rows(a["L1_ffn_w2"])
    o["f_b2"] = c(np.broadcast_to(a["L1_ffn_b2"], (P, D)))
    for n, src in (("wr", "Wr"), ("wk", "Wk"), ("wv", "Wv")):
        o["b_" + n] = c(a["L1_attn_b_" + src].T)
    o["b_wo"] = rows(c(a["L1_attn_b_Wo"].T))
    for n in ("br", "bk", "bv"):
        o["b_" + n] = col(a["L1_attn_b_" + n])
    o["b_u"] = col(a["L1_attn_b_U"])
    o["b_td"] = a["L1_attn_b_time_decay"].reshape(1, -1)
    o["b_bo"] = c(np.broadcast_to(a["L1_attn_b_bo"], (P, D)))
    o["m_router"] = c(a["L0_ffn_router_w"].T)
    o["m_w1"] = c(a["L0_ffn_w1"].transpose(1, 0, 2))
    o["m_b1"] = col(a["L0_ffn_b1"].reshape(-1))
    o["m_w2"] = c(a["L0_ffn_w2"].reshape(NE, NJH, P, D).transpose(2, 0, 1, 3))
    o["m_b2"] = c(a["L0_ffn_b2"].T)
    o["r_a"] = c(a["L1_attn_a_A"].T)
    o["r_b"] = c(a["L1_attn_a_B_w"].T)
    o["r_c"] = c(a["L1_attn_a_C_w"].T)
    o["r_d"] = col(a["L1_attn_a_D"])
    o["a_mux"] = col(a["L0_attn_a_mu_x"])
    o["a_wx1"] = a["L0_attn_a_W_x1"]
    LR = a["L0_attn_a_W_x2"].shape[2]
    wx2 = np.zeros((P, 5, D), np.float32)
    for i in range(5):
        at = LR * min(i, 3)
        wx2[at:at + LR, i, :] = a["L0_attn_a_W_x2"][:, i, :].T
    o["a_wx2"] = wx2
    o["a_xb"] = c(a["L0_attn_a_x_bias"].T)
    o["a_ww1"] = a["L0_attn_a_W_w1"]
    o["a_ww2"] = a["L0_attn_a_W_w2"]
    o["a_bw2"] = c(np.tile(a["L0_attn_a_b_w2"], 2).reshape(P, 1))
    o["a_wr"] = a["L0_attn_a_W_r"]
    o["a_wk"] = a["L0_attn_a_W_k"]
    o["a_wv"] = c(np.repeat(a["L0_attn_a_W_v"].reshape(D, HA, VD).transpose(0, 2, 1), KD, axis=2))
    o["a_wg"] = a["L0_attn_a_W_g"]
    o["a_u"] = c(np.tile(a["L0_attn_a_u"].reshape(-1), 2).reshape(P, 1))
    o["a_gnw"] = col(a["L0_attn_a_gn_w"])
    o["a_gnb"] = col(a["L0_attn_a_gn_b"])
    o["a_wo"] = a["L0_attn_a_W_o"]
    sel = np.zeros((2, HA, KD, 2, VD, HA, VD), np.float32)
    for b in range(2):
        for h in range(HA):
            for v in range(VD):
                sel[b, h, :, b, v, h, :] = -1.0 / VD
                sel[b, h, :, b, v, h, v] += 1.0
    o["a_sel"] = sel.reshape(P, 2, VD, P)
    o["a_bo"] = np.kron(np.eye(HA), np.full((VD, VD), 1.0 / VD)).astype(np.float32)
    p = np.arange(P)
    hh, dd, g = p // (HD * HG), (p // HG) % HD, p % HG
    feat = (HG * g + hh) * HD + dd
    swap = (HG * g + hh) * HD + (dd ^ 1)
    q, kk, bq, bk = (a["L0_attn_b_" + n] for n in ("wq", "wk", "bq", "bk"))
    o["c_wqk"] = c(np.stack([q[feat].T, q[swap].T, kk[feat].T, kk[swap].T], axis=1))
    o["c_bqk"] = c(np.stack([bq[feat], bq[swap], bk[feat], bk[swap]], axis=1))
    inv = 1.0 / 10000.0 ** (np.arange(0, HD, 2) / HD)
    ang = np.arange(T)[None, :] * inv[dd % (HD // 2)][:, None]
    cos, sin = np.cos(ang), np.sin(ang) * np.where(dd % 2 == 0, -1.0, 1.0)[:, None]
    o["c_tab"] = np.stack([cos, sin, cos / HD ** 0.5, sin / HD ** 0.5], axis=1).astype(np.float32)
    for n in ("wv", "wg", "wo", "wd"):
        o["c_" + n] = c(a["L0_attn_b_" + n].T)
    for n in ("bv", "bo"):
        o["c_" + n] = c(np.broadcast_to(a["L0_attn_b_" + n], (P, D)))
    for n in ("bg", "gamma", "beta"):
        o["c_" + n] = col(a["L0_attn_b_" + n])
    o["c_bd"] = c(a["L0_attn_b_bd"].reshape(HB, 1))
    o["c_avg"] = np.kron(np.eye(HB), np.full((HD, HD), 1.0 / HD)).astype(np.float32)
    o["c_mask"] = (((p // HD) % HG)[:, None] == np.arange(HG)[None, :]).astype(np.float32)
    o["c_pos"] = np.maximum(p[:, None] - p[None, :], 0).astype(np.float32)
    o["c_row"] = c(np.broadcast_to(np.stack([np.full(P, 256.0), -p]), (P, 2, P)).astype(np.float32))
    late = (np.arange(T) >= P).astype(np.float32)
    kaug = np.stack([np.ones(T), late * np.arange(T) / 256, late * np.arange(T) / 256, late, late])
    o["c_kaug"] = np.tile(kaug, (1, HG)).astype(np.float16)
    return o


def stage_weights(nc, k, ctx, tag, args, prefix):
    tiles, loads = {}, []
    for name, ap in args.items():
        if not name.startswith(prefix):
            continue
        if name == "c_kaug":
            tiles[name] = ap
            continue
        t = ctx.enter_context(nc.sbuf_tensor(tag + name, list(ap.shape), F32))
        tiles[name] = t
        loads.append((t[:], ap))
    return tiles, loads


def start_loads(nc, s, name, loads):
    with nc.Block() as block:
        @block.sync
        def _(sp):
            for dst, src in loads:
                nc.sync.dma_start(dst, src).then_inc(s[name], 16)


def wait_loads(nc, s, name, loads):
    with nc.Block() as block:
        @block.sync
        def _(sp):
            sp.wait_ge(s[name], 16 * len(loads))


def hybrid_program(nc, args, out):
    with ExitStack() as top:
        k = open_core(nc, top)
        wf, loads_f = stage_weights(nc, k, top, "w", args, "f_")
        xn_d = nc.dram_tensor("xn_d", [TILES, P, D], F32).ap()
        val_d = nc.dram_tensor("val_d", [B * NE, CAP], F32).ap()
        idx_d = nc.dram_tensor("idx_d", [B * NE, CAP], F32).ap()
        scr = retention_scratch(nc)

        arrived = sems(nc, top, "in_", "m c r b")
        wr, loads_r = stage_weights(nc, k, top, "w", args, "r_")

        with ExitStack() as moe:
            wm, loads_m = stage_weights(nc, k, moe, "w", args, "m_")
            with ExitStack() as ctx:
                wa, loads_a = stage_weights(nc, k, ctx, "w", args, "a_")
                stage_load(nc, k, args["x"], loads_a)
                start_loads(nc, arrived, "m", loads_m)
                stage_rwkv(nc, k, "a_", wa)
            with ExitStack() as ctx:
                wc, loads_c = stage_weights(nc, k, ctx, "w", args, "c_")
                wait_loads(nc, arrived, "m", loads_m)
                start_loads(nc, arrived, "c", loads_c)
                stage_moe(nc, k, "m0_", wm, xn_d, val_d, idx_d)
                wait_loads(nc, arrived, "c", loads_c)
                start_loads(nc, arrived, "r", loads_r + loads_f)
                stage_retention(nc, k, "c_", wc, scr)
            stage_moe(nc, k, "m1_", wm, xn_d, val_d, idx_d)
        with ExitStack() as ctx:
            wait_loads(nc, arrived, "r", loads_r + loads_f)
            stage_rnn(nc, k, "r_", wr)
            wb, loads_b = stage_weights(nc, k, ctx, "w", args, "b_")
            start_loads(nc, arrived, "b", loads_b)
            stage_ffn(nc, k, "f0_", wf["f_w1"], wf["f_b1"], wf["f_w2"], wf["f_b2"])
            wait_loads(nc, arrived, "b", loads_b)
            stage_wkv(nc, k, "b_", wb)
        stage_ffn(nc, k, "f1_", wf["f_w1"], wf["f_b1"], wf["f_w2"], wf["f_b2"])
        stage_store(nc, k, out)


def kernel(**inputs):
    import concourse.bacc as _bacc
    from concourse import mybir as _mybir
    from concourse.bass_utils import run_bass_kernel_spmd as _run

    nc = _bacc.Bacc("TRN2", target_bir_lowering=False, num_devices=1)
    arrays, args = {}, {}
    for name, a in lay_out({n: np.asarray(v) for n, v in inputs.items()}).items():
        a = np.ascontiguousarray(a)
        arrays["in_" + name] = a
        args[name] = nc.dram_tensor("in_" + name, a.shape, _mybir.dt.from_np(a.dtype), kind="ExternalInput").ap()
    out = nc.dram_tensor("out_x", (B, T, D), F32, kind="ExternalOutput").ap()
    hybrid_program(nc, args, out)
    r = _run(nc, [arrays], core_ids=[0])
    return r.results[0]["out_x"]
```
